# Optimizing a Trainium2 kernel written in Bass

```python
import numpy as np
import jax
import jax.numpy as jnp

def _softmax(x, axis=-1):
    return jax.nn.softmax(x, axis=axis)

def _gelu(x):
    return jax.nn.gelu(x, approximate=True)

def _silu(x):
    return jax.nn.silu(x)

def _sigmoid(x):
    return jax.nn.sigmoid(x)

def _layernorm(x, axis=-1, eps=1e-05):
    m = jnp.mean(x, axis=axis, keepdims=True)
    v = jnp.var(x, axis=axis, keepdims=True)
    return (x - m) / jnp.sqrt(v + eps)

def _scatter_add(tgt, idx, src, axis=0):
    return tgt.at[idx].add(src)

def _segment_sum(src, seg, n):
    return jax.ops.segment_sum(src, seg, n)
kernel_name = 'mk_seq_preln_d2_jaxref_r8_6cc790'

def setup_inputs(seed: int=0):
    np.random.seed(seed)
    _w = jnp.asarray

    def _L0_attn_setup():
        import jax, jax.numpy as jnp
        import numpy as np
        HIDDEN, HEADS, HDIM = (128, 8, 64)
        B, S = (4, 1024)
        LN_EPS = 1e-06
        key = jax.random.key(seed)
        ks = jax.random.split(key, 12)
        inner = HEADS * HDIM
        sd = HIDDEN ** (-0.5)
        return {'x': jax.random.normal(ks[0], (B, S, HIDDEN), jnp.float32), 'Wq': jax.random.normal(ks[1], (HIDDEN, inner), jnp.float32) * sd, 'bq': jnp.zeros((inner,), jnp.float32), 'Wk': jax.random.normal(ks[2], (HIDDEN, inner), jnp.float32) * sd, 'bk': jnp.zeros((inner,), jnp.float32), 'Wv': jax.random.normal(ks[3], (HIDDEN, inner), jnp.float32) * sd, 'bv': jnp.zeros((inner,), jnp.float32), 'Wo': jax.random.normal(ks[4], (inner, HIDDEN), jnp.float32) * inner ** (-0.5), 'bo': jnp.zeros((HIDDEN,), jnp.float32), 'alpha': jnp.ones((HEADS, HDIM), jnp.float32), 'aug_param': jax.random.normal(ks[5], (1, HEADS, HDIM), jnp.float32), 'ln_scale': jnp.ones((HIDDEN,), jnp.float32), 'ln_bias': jnp.zeros((HIDDEN,), jnp.float32)}
    _L0_attn_in = _L0_attn_setup()

    def _L0_ffn_setup():
        import jax, jax.numpy as jnp
        import numpy as np
        TOP_K = 2
        key = jax.random.key(seed)
        ks = jax.random.split(key, 6)
        B, S, H, F, E = (4, 256, 128, 512, 8)
        x = jax.random.normal(ks[0], (B, S, H), dtype=jnp.float32)
        gate_w = jax.random.normal(ks[1], (E, H), dtype=jnp.float32) * 0.02
        W1 = jax.random.normal(ks[2], (E, H, F), dtype=jnp.float32) * (1.0 / np.sqrt(H))
        b1 = jnp.zeros((E, F), dtype=jnp.float32)
        W2 = jax.random.normal(ks[3], (E, F, H), dtype=jnp.float32) * (1.0 / np.sqrt(F))
        b2 = jnp.zeros((E, H), dtype=jnp.float32)
        sW1 = jax.random.normal(ks[4], (H, F), dtype=jnp.float32) * (1.0 / np.sqrt(H))
        sb1 = jnp.zeros((F,), dtype=jnp.float32)
        sW2 = jax.random.normal(ks[5], (F, H), dtype=jnp.float32) * (1.0 / np.sqrt(F))
        sb2 = jnp.zeros((H,), dtype=jnp.float32)
        return {'x': x, 'gate_w': gate_w, 'W1': W1, 'b1': b1, 'W2': W2, 'b2': b2, 'sW1': sW1, 'sb1': sb1, 'sW2': sW2, 'sb2': sb2}
    _L0_ffn_in = _L0_ffn_setup()

    def _L1_attn_setup():
        import jax, jax.numpy as jnp
        import numpy as np
        H = 128
        NH = 16
        HD = H // NH
        BETA = 1.0
        STEPS = 2
        EPS_NORM = 1e-12
        EPS_LN = 1e-05

        def _l2norm(x):
            n = jnp.linalg.norm(x, axis=-1, keepdims=True)
            return x / jnp.maximum(n, EPS_NORM)
        key = jax.random.key(seed)
        ks = jax.random.split(key, 10)
        s = 1.0 / np.sqrt(H)
        return {'hidden_states': jax.random.normal(ks[0], (2, 256, H), jnp.float32), 'Wq': jax.random.normal(ks[1], (H, H), jnp.float32) * s, 'bq': jnp.zeros((H,), jnp.float32), 'Wk': jax.random.normal(ks[2], (H, H), jnp.float32) * s, 'bk': jnp.zeros((H,), jnp.float32), 'Wv': jax.random.normal(ks[3], (H, H), jnp.float32) * s, 'bv': jnp.zeros((H,), jnp.float32), 'Wo': jax.random.normal(ks[4], (H, H), jnp.float32) * s, 'bo': jnp.zeros((H,), jnp.float32), 'ln_w': jnp.ones((H,), jnp.float32), 'ln_b': jnp.zeros((H,), jnp.float32)}
    _L1_attn_in = _L1_attn_setup()

    def _L1_ffn_setup():
        import jax, jax.numpy as jnp
        from jax import lax
        import numpy as np
        D_MODEL = 128
        HIDDEN = 64
        N_EXPERTS = 32
        TOP_K = 2
        B, S = (1, 512)

        def _moe_group(x2, router_w, wg, wu, wd, top_k):
            T = x2.shape[0]
            n_experts = router_w.shape[1]
            logits = x2 @ router_w
            scores = jax.nn.softmax(logits, axis=-1)
            expert_weights, expert_indices = lax.top_k(scores, top_k)
            flat_e = expert_indices.reshape(-1)
            flat_w = expert_weights.reshape(-1)
            flat_t = jnp.repeat(jnp.arange(T), top_k)
            order = jnp.argsort(flat_e)
            tok = flat_t[order]
            xs = x2[tok]
            group_sizes = jnp.bincount(flat_e, length=n_experts).astype(jnp.int32)
            gate = lax.ragged_dot(xs, wg, group_sizes)
            up = lax.ragged_dot(xs, wu, group_sizes)
            ys = lax.ragged_dot(jax.nn.silu(gate) * up, wd, group_sizes)
            ys = ys * flat_w[order][:, None]
            return jnp.zeros_like(x2).at[tok].add(ys)
        key = jax.random.key(seed)
        ks = jax.random.split(key, 9)
        w = lambda k, shape: jax.random.normal(k, shape, dtype=jnp.float32) * 0.02
        return {'x': jax.random.normal(ks[0], (B, S, D_MODEL), dtype=jnp.float32), 'router_w0': w(ks[1], (D_MODEL, N_EXPERTS)), 'wg0': w(ks[2], (N_EXPERTS, D_MODEL, HIDDEN)), 'wu0': w(ks[3], (N_EXPERTS, D_MODEL, HIDDEN)), 'wd0': w(ks[4], (N_EXPERTS, HIDDEN, D_MODEL)), 'router_w1': w(ks[5], (D_MODEL, N_EXPERTS)), 'wg1': w(ks[6], (N_EXPERTS, D_MODEL, HIDDEN)), 'wu1': w(ks[7], (N_EXPERTS, D_MODEL, HIDDEN)), 'wd1': w(ks[8], (N_EXPERTS, HIDDEN, D_MODEL))}
    _L1_ffn_in = _L1_ffn_setup()
    _d = {'L0_attn_x': _L0_attn_in['x'], 'L0_attn_Wq': _L0_attn_in['Wq'], 'L0_attn_bq': _L0_attn_in['bq'], 'L0_attn_Wk': _L0_attn_in['Wk'], 'L0_attn_bk': _L0_attn_in['bk'], 'L0_attn_Wv': _L0_attn_in['Wv'], 'L0_attn_bv': _L0_attn_in['bv'], 'L0_attn_Wo': _L0_attn_in['Wo'], 'L0_attn_bo': _L0_attn_in['bo'], 'L0_attn_alpha': _L0_attn_in['alpha'], 'L0_attn_aug_param': _L0_attn_in['aug_param'], 'L0_attn_ln_scale': _L0_attn_in['ln_scale'], 'L0_attn_ln_bias': _L0_attn_in['ln_bias'], 'L0_ffn_gate_w': _L0_ffn_in['gate_w'], 'L0_ffn_W1': _L0_ffn_in['W1'], 'L0_ffn_b1': _L0_ffn_in['b1'], 'L0_ffn_W2': _L0_ffn_in['W2'], 'L0_ffn_b2': _L0_ffn_in['b2'], 'L0_ffn_sW1': _L0_ffn_in['sW1'], 'L0_ffn_sb1': _L0_ffn_in['sb1'], 'L0_ffn_sW2': _L0_ffn_in['sW2'], 'L0_ffn_sb2': _L0_ffn_in['sb2'], 'L1_attn_Wq': _L1_attn_in['Wq'], 'L1_attn_bq': _L1_attn_in['bq'], 'L1_attn_Wk': _L1_attn_in['Wk'], 'L1_attn_bk': _L1_attn_in['bk'], 'L1_attn_Wv': _L1_attn_in['Wv'], 'L1_attn_bv': _L1_attn_in['bv'], 'L1_attn_Wo': _L1_attn_in['Wo'], 'L1_attn_bo': _L1_attn_in['bo'], 'L1_attn_ln_w': _L1_attn_in['ln_w'], 'L1_attn_ln_b': _L1_attn_in['ln_b'], 'L1_ffn_router_w0': _L1_ffn_in['router_w0'], 'L1_ffn_wg0': _L1_ffn_in['wg0'], 'L1_ffn_wu0': _L1_ffn_in['wu0'], 'L1_ffn_wd0': _L1_ffn_in['wd0'], 'L1_ffn_router_w1': _L1_ffn_in['router_w1'], 'L1_ffn_wg1': _L1_ffn_in['wg1'], 'L1_ffn_wu1': _L1_ffn_in['wu1'], 'L1_ffn_wd1': _L1_ffn_in['wd1']}
    _x0 = _d['L0_attn_x']
    _d['L0_attn_x'] = jax.random.normal(jax.random.fold_in(jax.random.key(seed), 1), (16, 256, 128), dtype=_x0.dtype)
    del _x0
    return _d

def reference(L0_attn_x, L0_attn_Wq, L0_attn_bq, L0_attn_Wk, L0_attn_bk, L0_attn_Wv, L0_attn_bv, L0_attn_Wo, L0_attn_bo, L0_attn_alpha, L0_attn_aug_param, L0_attn_ln_scale, L0_attn_ln_bias, L0_ffn_gate_w, L0_ffn_W1, L0_ffn_b1, L0_ffn_W2, L0_ffn_b2, L0_ffn_sW1, L0_ffn_sb1, L0_ffn_sW2, L0_ffn_sb2, L1_attn_Wq, L1_attn_bq, L1_attn_Wk, L1_attn_bk, L1_attn_Wv, L1_attn_bv, L1_attn_Wo, L1_attn_bo, L1_attn_ln_w, L1_attn_ln_b, L1_ffn_router_w0, L1_ffn_wg0, L1_ffn_wu0, L1_ffn_wd0, L1_ffn_router_w1, L1_ffn_wg1, L1_ffn_wu1, L1_ffn_wd1):

    def _L0_attn_ref(x, Wq, bq, Wk, bk, Wv, bv, Wo, bo, alpha, aug_param, ln_scale, ln_bias):
        import jax, jax.numpy as jnp
        import numpy as np
        HIDDEN, HEADS, HDIM = (128, 8, 64)
        B, S = (4, 1024)
        LN_EPS = 1e-06
        b, s, _ = x.shape
        h, d = alpha.shape
        scale = d ** (-0.5)
        q = (x @ Wq + bq).reshape(b, s, h, d)
        k = (x @ Wk + bk).reshape(b, s, h, d)
        v = (x @ Wv + bv).reshape(b, s, h, d)
        decay = jax.nn.sigmoid(alpha)

        def step(state, qkv):
            q_t, k_t, v_t = qkv
            attn = jax.nn.softmax(jnp.einsum('bhd,bhd->bh', q_t, k_t) * scale, axis=-1)
            new_state = decay * state + (1.0 - decay) * attn[..., None] * v_t
            return (new_state, new_state)
        qs = jnp.moveaxis(q, 1, 0)
        ks_ = jnp.moveaxis(k, 1, 0)
        vs = jnp.moveaxis(v, 1, 0)
        init = jnp.zeros((b, h, d), x.dtype)
        _, states = jax.lax.scan(step, init, (qs, ks_, vs))
        states = jnp.moveaxis(states, 0, 1)
        aug = jax.nn.sigmoid(q * aug_param)
        out = (q * states + aug).reshape(b, s, h * d)
        out = out @ Wo + bo
        mean = jnp.mean(out, axis=-1, keepdims=True)
        var = jnp.var(out, axis=-1, keepdims=True)
        return (out - mean) * jax.lax.rsqrt(var + LN_EPS) * ln_scale + ln_bias

    def _L0_ffn_ref(x, gate_w, W1, b1, W2, b2, sW1, sb1, sW2, sb2):
        import jax, jax.numpy as jnp
        import numpy as np
        TOP_K = 2
        B, S, H = x.shape
        E = gate_w.shape[0]
        x_flat = x.reshape(-1, H)
        logits = x_flat @ gate_w.T
        probs = jax.nn.softmax(logits.astype(jnp.float32), axis=-1)
        top_w, sel = jax.lax.top_k(probs, TOP_K)
        top_w = top_w / jnp.sum(top_w, axis=-1, keepdims=True)
        combine = jnp.sum(jax.nn.one_hot(sel, E, dtype=top_w.dtype) * top_w[..., None], axis=1)
        combine = combine.astype(x.dtype)
        h = jax.nn.gelu(jnp.einsum('th,ehf->tef', x_flat, W1) + b1[None], approximate=False)
        y = jnp.einsum('tef,efh->teh', h, W2) + b2[None]
        out = jnp.einsum('teh,te->th', y, combine)
        sh = jax.nn.gelu(x_flat @ sW1 + sb1, approximate=False)
        out = out + sh @ sW2 + sb2
        return out.reshape(B, S, H)

    def _L1_attn_ref(hidden_states, Wq, bq, Wk, bk, Wv, bv, Wo, bo, ln_w, ln_b):
        import jax, jax.numpy as jnp
        import numpy as np
        H = 128
        NH = 16
        HD = H // NH
        BETA = 1.0
        STEPS = 2
        EPS_NORM = 1e-12
        EPS_LN = 1e-05

        def _l2norm(x):
            n = jnp.linalg.norm(x, axis=-1, keepdims=True)
            return x / jnp.maximum(n, EPS_NORM)
        B, S, _ = hidden_states.shape
        residual = hidden_states
        mu = jnp.mean(hidden_states, axis=-1, keepdims=True)
        var = jnp.mean(jnp.square(hidden_states - mu), axis=-1, keepdims=True)
        x = (hidden_states - mu) * jax.lax.rsqrt(var + EPS_LN) * ln_w + ln_b
        q = (x @ Wq + bq).reshape(B, S, NH, HD)
        k = (x @ Wk + bk).reshape(B, S, NH, HD)
        v = (x @ Wv + bv).reshape(B, S, NH, HD)
        q = _l2norm(q)
        k = _l2norm(k)
        state = q
        for _ in range(STEPS):
            sim = jnp.einsum('bqhd,bkhd->bqhk', state, k)
            att = jax.nn.softmax(BETA * sim, axis=-1)
            state = jnp.einsum('bqhk,bkhd->bqhd', att, v)
        o = state.reshape(B, S, H) @ Wo + bo
        return residual + o

    def _L1_ffn_ref(x, router_w0, wg0, wu0, wd0, router_w1, wg1, wu1, wd1):
        import jax, jax.numpy as jnp
        from jax import lax
        import numpy as np
        D_MODEL = 128
        HIDDEN = 64
        N_EXPERTS = 32
        TOP_K = 2
        B, S = (1, 512)

        def _moe_group(x2, router_w, wg, wu, wd, top_k):
            T = x2.shape[0]
            n_experts = router_w.shape[1]
            logits = x2 @ router_w
            scores = jax.nn.softmax(logits, axis=-1)
            expert_weights, expert_indices = lax.top_k(scores, top_k)
            flat_e = expert_indices.reshape(-1)
            flat_w = expert_weights.reshape(-1)
            flat_t = jnp.repeat(jnp.arange(T), top_k)
            order = jnp.argsort(flat_e)
            tok = flat_t[order]
            xs = x2[tok]
            group_sizes = jnp.bincount(flat_e, length=n_experts).astype(jnp.int32)
            gate = lax.ragged_dot(xs, wg, group_sizes)
            up = lax.ragged_dot(xs, wu, group_sizes)
            ys = lax.ragged_dot(jax.nn.silu(gate) * up, wd, group_sizes)
            ys = ys * flat_w[order][:, None]
            return jnp.zeros_like(x2).at[tok].add(ys)
        b, s, d = x.shape
        x2 = x.reshape(-1, d)
        out0 = _moe_group(x2, router_w0, wg0, wu0, wd0, TOP_K)
        out1 = _moe_group(x2, router_w1, wg1, wu1, wd1, TOP_K)
        out = (out0 * TOP_K + out1 * TOP_K) / (TOP_K + TOP_K)
        return out.reshape(b, s, d)
    x = L0_attn_x
    x = x + _L0_attn_ref(_layernorm(x, axis=-1), L0_attn_Wq, L0_attn_bq, L0_attn_Wk, L0_attn_bk, L0_attn_Wv, L0_attn_bv, L0_attn_Wo, L0_attn_bo, L0_attn_alpha, L0_attn_aug_param, L0_attn_ln_scale, L0_attn_ln_bias)
    x = x + _L0_ffn_ref(_layernorm(x, axis=-1), L0_ffn_gate_w, L0_ffn_W1, L0_ffn_b1, L0_ffn_W2, L0_ffn_b2, L0_ffn_sW1, L0_ffn_sb1, L0_ffn_sW2, L0_ffn_sb2)
    x = x + _L1_attn_ref(_layernorm(x, axis=-1), L1_attn_Wq, L1_attn_bq, L1_attn_Wk, L1_attn_bk, L1_attn_Wv, L1_attn_bv, L1_attn_Wo, L1_attn_bo, L1_attn_ln_w, L1_attn_ln_b)
    x = x + _L1_ffn_ref(_layernorm(x, axis=-1), L1_ffn_router_w0, L1_ffn_wg0, L1_ffn_wu0, L1_ffn_wd0, L1_ffn_router_w1, L1_ffn_wg1, L1_ffn_wu1, L1_ffn_wd1)
    return x

_drawn_inputs = setup_inputs


def setup_inputs(seed=0):
    import zlib

    import numpy as np

    out = dict(_drawn_inputs(seed))
    spreads = {'L0_attn_bq': (0.0, 0.1),
     'L0_attn_bk': (0.0, 0.323),
     'L0_attn_bv': (0.0, 0.1),
     'L0_attn_bo': (0.0, 0.1),
     'L0_attn_alpha': (1.0, 0.2),
     'L0_attn_ln_scale': (1.0, 0.2),
     'L0_attn_ln_bias': (0.0, 0.1),
     'L0_ffn_b1': (0.0, 0.269),
     'L0_ffn_b2': (0.0, 0.1),
     'L0_ffn_sb1': (0.0, 0.1),
     'L0_ffn_sb2': (0.0, 0.1),
     'L1_attn_bq': (0.0, 0.8),
     'L1_attn_bk': (0.0, 0.8),
     'L1_attn_bv': (0.0, 0.1),
     'L1_attn_bo': (0.0, 0.1),
     'L1_attn_ln_w': (1.0, 0.2),
     'L1_attn_ln_b': (0.0, 0.1)}
    factors = {'L1_attn_Wq': 8.0,
     'L1_ffn_router_w0': 8.0,
     'L1_ffn_wg0': 8.0,
     'L1_ffn_wu0': 8.0,
     'L1_ffn_wd0': 8.0,
     'L1_ffn_router_w1': 8.0,
     'L1_ffn_wg1': 8.0,
     'L1_ffn_wu1': 8.0,
     'L1_ffn_wd1': 8.0}
    for name, (base, spread) in spreads.items():
        noise = np.random.default_rng([zlib.crc32(name.encode()), seed]).standard_normal(out[name].shape)
        drawn = base * np.exp(spread * noise) if base else spread * noise
        out[name] = jnp.asarray(drawn.astype(out[name].dtype))
    for name, factor in factors.items():
        out[name] = (out[name] * factor).astype(out[name].dtype)
    return out
```

```python
from contextlib import ExitStack

import concourse.bass as bass
from concourse import mybir

F32 = mybir.dt.float32
BF16 = mybir.dt.bfloat16
I32 = mybir.dt.int32
U32 = mybir.dt.uint32
ALU = mybir.AluOpType
ACT = mybir.ActivationFunctionType
AX = mybir.AxisListType

P = 128
TOK = 4096
SEQ = 256
SUP = 512
LN_EPS = 1e-5
LN0_EPS = 1e-6


class Chain:

    def __init__(self, eng, sem, passed=None):
        self.eng, self.sem, self.base, self.n, self.passed = eng, sem, 0, 0, passed

    def start(self, base):
        self.base, self.n = base, 0

    def own_wait(self):
        self.eng.sem_inc(self.passed, 1)

    def step(self, ins, own_wait=False):
        self.n += 1
        ins.then_inc(self.sem, 1)
        self.eng.wait_ge(self.sem, self.base + self.n)
        if own_wait:
            self.own_wait()


class Scope:

    def __init__(self, nc, tag):
        self.nc, self.tag, self.ctx, self.sems = nc, tag, ExitStack(), []

    def __enter__(self):
        return self

    def __exit__(self, *e):
        with self.nc.Block() as block:
            @block.sync
            def _(sp):
                for s in self.sems[0::3]:
                    sp.sem_clear(s)

            @block.scalar
            def _(act):
                for s in self.sems[1::3]:
                    act.sem_clear(s)

            @block.tensor
            def _(pe):
                for s in self.sems[2::3]:
                    pe.sem_clear(s)
        return self.ctx.__exit__(*e)

    def sb(self, name, shape, dt=F32):
        return self.ctx.enter_context(self.nc.sbuf_tensor(f"{self.tag}_{name}", shape, dt))

    def ps(self, name, shape, dt=F32):
        return self.ctx.enter_context(self.nc.psum_tensor(f"{self.tag}_{name}", shape, dt))

    def sem(self, name):
        s = self.ctx.enter_context(self.nc.semaphore(f"{self.tag}_{name}"))
        self.sems.append(s)
        return s



def recurrent_mixer(nc, T, x_in, x_out):
    NS = TOK // SUP
    NT = SUP // P
    NC = 4
    with Scope(nc, "a") as S:
        sb, ps, sem = S.sb, S.ps, S.sem
        wq, wk, wv = sb("wq", [P, 512]), sb("wk", [P, 512]), sb("wv", [P, 512])
        wo, wo_h = sb("wo", [P, NC, P]), sb("wo_h", [P, NC, P])
        cols = sb("cols", [P, 5, NC])
        rows = sb("rows", [1, P])
        lns, lnb = sb("lns", [P, P]), sb("lnb", [P, P])
        ident, headsel = sb("ident", [P, P]), sb("headsel", [P, 32])
        ident_bf = sb("ident_bf", [P, P], BF16)
        sel3 = sb("sel3", [32, NC, P], BF16)
        halves, one_row = sb("halves", [P, P]), sb("one_row", [1, P])
        mhalf = sb("mhalf", [P, 1])
        decay, omd = sb("decay", [P, NC]), sb("omd", [P, NC])
        th_a, bvs = sb("th_a", [P, NC]), sb("bvs", [P, NC])
        augh, augb = sb("augh", [P, NC]), sb("augb", [P, NC])
        bo_b = sb("bo_b", [P, P])

        x = [sb(f"x{u}", [P, NT, P]) for u in range(2)]
        xres = [sb(f"xres{u}", [P, NT, P]) for u in range(2)]
        xn, xnT = sb("xn", [P, NT, P]), sb("xnT", [P, SUP])
        bst, mv = sb("bst", [P, NT, 6]), sb("mv", [P, NT, 2])
        veps, rstd = sb("veps", [P, NT]), sb("rstd", [P, NT])
        qT = [sb(f"qT{u}", [P, NC, SUP]) for u in range(2)]
        th = [sb(f"th{u}", [P, NC, SUP]) for u in range(2)]
        vT = [sb(f"vT{u}", [P, NC, SUP]) for u in range(2)]
        qk = sb("qk", [P, NC, SUP])
        st, g = sb("st", [P, NC, SUP]), sb("g", [P, NC, SUP])
        sc = sb("sc", [P, SUP])
        mx, e8, sm, r8 = sb("mx", [P, NT]), sb("e8", [P, NT, 8]), sb("sm", [P, NT]), sb("r8", [P, NT])
        res = sb("res", [P, NT, 8])
        a3 = sb("a3", [P, NT, 32], BF16)
        a3T = sb("a3T", [32, SUP], BF16)
        o = sb("o", [P, NT, P])
        obst, omv = sb("obst", [P, NT, 6]), sb("omv", [P, NT, 2])
        oveps, orstd = sb("oveps", [P, NT]), sb("orstd", [P, NT])
        y = [sb(f"y{u}", [P, NT, P]) for u in range(2)]

        pT = ps("pT", [P, SUP])
        pP = [ps(f"pP{n}", [P, SUP]) for n in range(4)]
        pS = ps("pS", [P, SUP])
        pA = ps("pA", [P, SUP])
        pA3 = ps("pA3", [P, 2 * SUP], BF16)

        consts = sem("consts")
        x_loaded = [sem(f"x_loaded{u}") for u in range(2)]
        stored = [sem(f"stored{u}") for u in range(2)]
        memsets, coef_act, coef_dve = sem("memsets"), sem("coef_act"), sem("coef_dve")
        bo_done = sem("bo_done")
        dve_passed, pool_passed = sem("dve_passed"), sem("pool_passed")
        set_c, in_c, out_c, dve_c, pool_c = (sem(x) for x in ("set_c", "in_c", "out_c", "dve_c", "pool_c"))
        veps_ready, rstd_ready, xn_ready = sem("veps_ready"), sem("rstd_ready"), sem("xn_ready")
        xT_done, xnT_ready = sem("xT_done"), sem("xnT_ready")
        proj_done = sem("proj_done")
        q_ready, tanh_ready, v_ready = sem("q_ready"), sem("tanh_ready"), sem("v_ready")
        qk_ready = sem("qk_ready")
        sc_done, sc_copied, scT_done = sem("sc_done"), sem("sc_copied"), sem("scT_done")
        e_shifted, e_done, a3_ready = sem("e_shifted"), sem("e_done"), sem("a3_ready")
        a3T_done, a3T_copied, bc_done = sem("a3T_done"), sem("a3T_copied"), sem("bc_done")
        u_ready, st_ready, g_ready = sem("u_ready"), sem("st_ready"), sem("g_ready")
        wo_done, o_copied = sem("wo_done"), sem("o_copied")
        oveps_ready, orstd_ready = sem("oveps_ready"), sem("orstd_ready")
        xres_ready, y_ready = sem("xres_ready"), sem("y_ready")

        xv = x_in.rearrange("(s t p) d -> s p t d", t=NT, p=P)
        ov = x_out.rearrange("(s t p) d -> s p t d", t=NT, p=P)
        NCONST = 12

        def each_step(eng, step):
            step(0, 0, first=True)
            step(0, 1)
            step(0, 2)
            with eng.Fori(0, (NS - 4) // 2) as i:
                step(i, 3)
                step(i, 4)
            step((NS - 4) // 2, 3, last=True)

        with nc.Block() as block:
            @block.sync
            def _(sp):
                sp.dma_start(x[0][:], xv[0]).then_inc(x_loaded[0], 16)
                for dst, src in ((ident, T["ident"]), (ident_bf, T["ident_bf"].bitcast(BF16)), (wq, T["L0_attn_Wq"]), (wk, T["L0_attn_Wk"]), (wv, T["L0_attn_Wv"]),
                                 (cols, T["a_cols"]), (headsel, T["headsel"]), (sel3, T["sel3"].bitcast(BF16)),
                                 (wo, T["L0_attn_Wo"].rearrange("(c p) n -> p c n", p=P)),
                                 (rows, T["L0_attn_bo"].rearrange("(a n) -> a n", a=1)),
                                 (lns, T["L0_attn_ln_scale"].partition_broadcast(P)),
                                 (lnb, T["L0_attn_ln_bias"].partition_broadcast(P))):
                    sp.dma_start(dst[:], src).then_inc(consts, 16)

                def step(i, r, first=False, last=False):
                    s, u = 2 * i + r, r % 2
                    if not last:
                        if not first:
                            sp.wait_ge(xres_ready, s)
                        sp.dma_start(x[1 - u][:], xv[s + 1]).then_inc(x_loaded[1 - u], 16)
                    if not first:
                        store(s - 1, 1 - u)

                def store(s, u):
                    sp.wait_ge(y_ready, s + 1)
                    sp.dma_start(ov[s], y[u][:]).then_inc(stored[u], 16)

                each_step(sp, step)
                store(NS - 1, 1)
                for u in range(2):
                    sp.wait_ge(stored[u], 16 * NS // 2)

            @block.vector
            def _(dve):
                ch_set, ch, ch_in, ch_out = (Chain(dve, x, dve_passed) for x in (set_c, dve_c, in_c, out_c))
                dve.memset(halves[:], 0.5)
                dve.memset(one_row[:], 1.0)
                dve.memset(mhalf[:], -0.5)
                dve.memset(a3[:], 0.0).then_inc(memsets, 1)
                dve.wait_ge(coef_act, 1)
                dve.tensor_scalar(decay[:], th_a[:], 0.5, 0.5, ALU.mult, ALU.add)
                ch_set.step(dve.tensor_scalar(omd[:], th_a[:], -1.0, 1.0, ALU.mult, ALU.add))
                dve.tensor_tensor(bvs[:], omd[:], cols[:, 2, :], ALU.mult)
                ch_set.step(dve.tensor_scalar(augh[:], cols[:, 4, :], 0.5, None, ALU.mult))
                dve.tensor_tensor(augb[:], augh[:], cols[:, 0, :], ALU.mult).then_inc(coef_dve, 1)
                dve.tensor_scalar(wo_h[:], wo[:], 0.5, None, ALU.mult)
                dve.wait_ge(bo_done, 1)
                dve.tensor_copy(bo_b[:], pS[:, 0:P]).then_inc(coef_dve, 1)
                dve.wait_ge(coef_dve, 2)

                def layernorm_in(i, r, first=False):
                    s, u = 2 * i + r, r % 2
                    ch_in.start(2 * s)
                    dve.wait_ge(x_loaded[u], 16 * (i + r // 2) + 16)
                    for t in range(NT):
                        last = dve.bn_stats(bst[:, t, :], x[u][:, t, :])
                    ch_in.step(last, own_wait=True)
                    for t in range(NT):
                        last = dve.bn_aggr(mv[:, t, :], bst[:, t, :])
                    ch_in.step(last)
                    dve.tensor_scalar(veps[:], mv[:, :, 1], LN_EPS, None, ALU.add).then_inc(veps_ready, 1)
                    dve.wait_ge(rstd_ready, s + 1)
                    if not first:
                        dve.wait_ge(xT_done, s)
                    for t in range(NT):
                        last = dve.tensor_scalar(xn[:, t, :], x[u][:, t, :], mv[:, t, 0:1], rstd[:, t:t + 1],
                                                 ALU.subtract, ALU.mult)
                    last.then_inc(xn_ready, 1)

                def layernorm_out(i, r):
                    s, u = 2 * i + r, r % 2
                    ch_out.start(4 * s)
                    dve.wait_ge(wo_done, s + 1)
                    dve.tensor_tensor(o[:], pS[:].rearrange("p (t n) -> p t n", t=NT),
                                      bo_b[:].unsqueeze(1).to_broadcast([P, NT, P]), ALU.add).then_inc(o_copied, 1)
                    dve.wait_ge(o_copied, s + 1)
                    for t in range(NT):
                        last = dve.bn_stats(obst[:, t, :], o[:, t, :])
                    ch_out.step(last, own_wait=True)
                    for t in range(NT):
                        last = dve.bn_aggr(omv[:, t, :], obst[:, t, :])
                    ch_out.step(last)
                    dve.tensor_scalar(oveps[:], omv[:, :, 1], LN0_EPS, None, ALU.add).then_inc(oveps_ready, 1)
                    dve.wait_ge(orstd_ready, s + 1)
                    for t in range(NT):
                        last = dve.tensor_scalar(o[:, t, :], o[:, t, :], omv[:, t, 0:1], orstd[:, t:t + 1],
                                                 ALU.subtract, ALU.mult)
                    ch_out.step(last)
                    ch_out.step(dve.tensor_tensor(o[:], o[:], lns[:].unsqueeze(1).to_broadcast([P, NT, P]), ALU.mult))
                    dve.wait_ge(xres_ready, s + 1)
                    if r >= 2:
                        dve.wait_ge(stored[u], 16 * (i + r // 2))
                    dve.tensor_tensor(y[u][:], o[:], xres[u][:], ALU.add).then_inc(y_ready, 1)

                def step(i, r, first=False, last=False):
                    s, u = 2 * i + r, r % 2
                    if not last:
                        layernorm_in(i, r + 1)
                    for c in range(NC):
                        dve.wait_ge(proj_done, 12 * s + 3 * c + 2)
                        dve.wait_ge(q_ready, NC * s + c + 1)
                        if c == 0 and not first:
                            dve.wait_ge(sc_done, s)
                        dve.scalar_tensor_tensor(qk[:, c, :], pP[(3 * c + 1) % 4][:], cols[:, 1, c:c + 1], qT[u][:, c, :],
                                                 ALU.add, ALU.mult).then_inc(qk_ready, 1)
                    if not first:
                        layernorm_out(i, r - 1)
                    ch.start(8 * s)
                    dve.wait_ge(scT_done, s + 1)
                    scv = pA[:].rearrange("p (t c r) -> p t c r", t=NT, c=NC)[:, :, :, 0:2]
                    e4 = e8[:].rearrange("p t (c r) -> p t c r", r=2)
                    ch.step(dve.tensor_reduce(mx[:], scv, AX.XY, ALU.max))
                    dve.tensor_tensor(e4, scv, mx[:].unsqueeze(2).unsqueeze(3).to_broadcast([P, NT, NC, 2]),
                                      ALU.subtract).then_inc(e_shifted, 1)
                    dve.wait_ge(e_done, s + 1)
                    ch.step(dve.tensor_reduce(sm[:], e8[:], AX.X, ALU.add))
                    ch.step(dve.reciprocal(r8[:], sm[:]))
                    ch.step(dve.tensor_tensor(res[:], e8[:], r8[:].unsqueeze(2).to_broadcast([P, NT, 8]), ALU.mult))
                    if not first:
                        dve.wait_ge(a3T_done, s)
                    split3(dve, ch, res[:], [a3[:, :, 8 * k:8 * k + 8] for k in range(3)], a3_ready)
                    for c in range(NC):
                        dve.wait_ge(bc_done, NC * s + c + 1)
                        dve.wait_ge(v_ready, NC * s + c + 1)
                        dve.tensor_tensor(vT[u][:, c, :], pP[c][:], vT[u][:, c, :], ALU.mult).then_inc(u_ready, 1)
                    for c in range(NC):
                        dve.wait_ge(u_ready, NC * s + c + 1)
                        if not first:
                            dve.wait_ge(g_ready, NC * (s - 1) + c + 1)
                        for b in range(2):
                            w = slice(b * SEQ, (b + 1) * SEQ)
                            last_i = dve.tensor_tensor_scan(st[:, c, w], decay[:, c:c + 1].to_broadcast([P, SEQ]),
                                                            vT[u][:, c, w], 0.0, ALU.mult, ALU.add)
                        last_i.then_inc(st_ready, 1)

                layernorm_in(0, 0, first=True)
                each_step(dve, step)
                layernorm_out(0, NS - 1)

            @block.scalar
            def _(act):
                act.wait_ge(consts, 16 * NCONST)
                act.activation(th_a[:], cols[:, 3, :], ACT.Tanh, scale=0.5).then_inc(coef_act, 1)
                act.wait_ge(coef_dve, 1)

                def copy_xnT(s, first=False):
                    act.wait_ge(xT_done, s + 1)
                    act.activation(xnT[:], pT[:], ACT.Copy).then_inc(xnT_ready, 1)

                def step(i, r, first=False, last=False):
                    s, u = 2 * i + r, r % 2
                    for c in range(NC):
                        act.wait_ge(proj_done, 12 * s + 3 * c + 1)
                        q_ps = pP[(3 * c) % 4]
                        if c == 0 and r >= 2:
                            act.wait_ge(g_ready, NC * (s - 1))
                        act.activation(qT[u][:, c, :], q_ps[:], ACT.Identity, bias=cols[:, 0, c:c + 1]).then_inc(q_ready, 1)
                        act.activation(th[u][:, c, :], q_ps[:], ACT.Tanh, scale=augh[:, c:c + 1],
                                       bias=augb[:, c:c + 1]).then_inc(tanh_ready, 1)
                        act.wait_ge(proj_done, 12 * s + 3 * c + 3)
                        act.activation(vT[u][:, c, :], pP[(3 * c + 2) % 4][:], ACT.Identity, scale=omd[:, c:c + 1],
                                       bias=bvs[:, c:c + 1]).then_inc(v_ready, 1)
                    act.wait_ge(sc_done, s + 1)
                    act.activation(sc[:], pS[:], ACT.Copy).then_inc(sc_copied, 1)
                    if not last:
                        copy_xnT(s + 1)
                    act.wait_ge(e_shifted, s + 1)
                    act.activation(e8[:], e8[:], ACT.Exp, scale=0.125).then_inc(e_done, 1)
                    act.wait_ge(a3T_done, s + 1)
                    act.activation(a3T[:], pA3[0:32, 0:SUP], ACT.Copy).then_inc(a3T_copied, 1)

                copy_xnT(0)
                each_step(act, step)

            @block.tensor
            def _(pe):
                pe.wait_ge(consts, 16 * NCONST)
                pe.wait_ge(memsets, 1)
                for c in range(NC):
                    pe.matmul(pS[:, 0:P], halves[:], wo[:, c, :], start=(c == 0), stop=False)
                pe.matmul(pS[:, 0:P], one_row[:], rows[:], start=False, stop=True).then_inc(bo_done, 1)

                def transpose_x(s, first=False):
                    pe.wait_ge(xn_ready, s + 1)
                    if not first:
                        pe.wait_ge(xnT_ready, s)
                    for t in range(NT):
                        last = pe.transpose(pT[:, t * P:(t + 1) * P], xn[:, t, :], ident[:])
                    last.then_inc(xT_done, 1)

                def out_proj(s):
                    pe.wait_ge(g_ready, NC * s + NC)
                    for t in range(NT):
                        for c in range(NC):
                            last = pe.matmul(pS[:, t * P:(t + 1) * P], g[:, c, t * P:(t + 1) * P], wo_h[:, c, :],
                                             start=(c == 0), stop=(c == NC - 1))
                    last.then_inc(wo_done, 1)

                def step(i, r, first=False, last=False):
                    s, u = 2 * i + r, r % 2
                    pe.wait_ge(xnT_ready, s + 1)
                    for c in range(NC):
                        for j, w in enumerate((wq, wk, wv)):
                            n = 3 * c + j
                            m = n - 4
                            if m >= 0:
                                pe.wait_ge((tanh_ready, qk_ready, v_ready)[m % 3], NC * s + m // 3 + 1)
                            elif not first:
                                pe.wait_ge(u_ready, NC * (s - 1) + n + 1)
                            pe.matmul(pP[n % 4][:], w[:, c * P:(c + 1) * P], xnT[:], start=True, stop=True).then_inc(proj_done, 1)
                    if not last:
                        transpose_x(s + 1)
                    if first:
                        pe.wait_ge(coef_dve, 2)
                    if r >= 2:
                        pe.wait_ge(o_copied, s - 1)
                    for c in range(NC):
                        pe.wait_ge(qk_ready, NC * s + c + 1)
                        last_i = pe.matmul(pS[32 * c:32 * c + 32, :], headsel[:], qk[:, c, :], start=True, stop=True)
                    last_i.then_inc(sc_done, 1)
                    pe.wait_ge(sc_copied, s + 1)
                    if not first:
                        pe.wait_ge(e_shifted, s)
                    for t in range(NT):
                        last_i = pe.transpose(pA[:, t * P:(t + 1) * P], sc[:, t * P:(t + 1) * P], ident[:])
                    last_i.then_inc(scT_done, 1)
                    if not first:
                        out_proj(s - 1)
                    pe.wait_ge(a3_ready, s + 1)
                    if not first:
                        pe.wait_ge(a3T_copied, s)
                    for t in range(NT):
                        last_i = pe.transpose(pA3[0:32, t * P:(t + 1) * P], a3[:, t, :], ident_bf[:])
                    last_i.then_inc(a3T_done, 1)
                    pe.wait_ge(a3T_copied, s + 1)
                    for c in range(NC):
                        m = 12 + c - 4
                        pe.wait_ge((tanh_ready, qk_ready, v_ready)[m % 3], NC * s + m // 3 + 1)
                        pe.matmul(pP[c][:], sel3[:, c, :], a3T[:], start=True, stop=True).then_inc(bc_done, 1)

                transpose_x(0, first=True)
                each_step(pe, step)
                pe.wait_ge(sc_copied, NS)
                out_proj(NS - 1)

            @block.gpsimd
            def _(pool):
                ch = Chain(pool, pool_c, pool_passed)
                pool.wait_ge(memsets, 1)

                def rsqrt_in(s):
                    pool.wait_ge(veps_ready, s + 1)
                    pool.tensor_tensor(rstd[:], veps[:], mhalf[:].to_broadcast([P, NT]), ALU.pow).then_inc(rstd_ready, 1)

                def rsqrt_out(s):
                    pool.wait_ge(oveps_ready, s + 1)
                    pool.tensor_tensor(orstd[:], oveps[:], mhalf[:].to_broadcast([P, NT]), ALU.pow).then_inc(orstd_ready, 1)

                def residual(i, r):
                    s, u = 2 * i + r, r % 2
                    pool.wait_ge(x_loaded[u], 16 * (i + r // 2) + 16)
                    if r >= 2:
                        pool.wait_ge(y_ready, s - 1)
                    pool.tensor_tensor(xres[u][:], x[u][:], lnb[:].unsqueeze(1).to_broadcast([P, NT, P]),
                                       ALU.add).then_inc(xres_ready, 1)

                def gate(s, u, first=False):
                    for c in range(NC):
                        pool.wait_ge(st_ready, NC * s + c + 1)
                        ch.start(NC * s)
                        ch.n = c
                        pool.wait_ge(tanh_ready, NC * s + c + 1)
                        ch.step(pool.tensor_tensor(qT[u][:, c, :], qT[u][:, c, :], st[:, c, :], ALU.mult))
                        if not first:
                            pool.wait_ge(wo_done, s)
                        pool.tensor_tensor(g[:, c, :], th[u][:, c, :], qT[u][:, c, :], ALU.add).then_inc(g_ready, 1)

                def step(i, r, first=False, last=False):
                    s, u = 2 * i + r, r % 2
                    if not last:
                        rsqrt_in(s + 1)
                    residual(i, r)
                    if not first:
                        rsqrt_out(s - 1)
                    gate(s, u, first)

                pool.wait_ge(consts, 16 * NCONST)
                rsqrt_in(0)
                each_step(pool, step)
                rsqrt_out(NS - 1)


def split3(dve, ch, res, parts, ready):
    ch.step(dve.tensor_copy(parts[0], res))
    ch.step(dve.tensor_tensor(res, res, parts[0], ALU.subtract))
    ch.step(dve.tensor_copy(parts[1], res))
    ch.step(dve.tensor_tensor(res, res, parts[1], ALU.subtract))
    dve.tensor_copy(parts[2], res).then_inc(ready, 1)



NT = SUP // P
NS = TOK // SUP
TOPK = 2
QUAD = 4


def span(eng, lo, hi, fn, least=2):
    q = lo
    while q < hi and (q < least or q % 2):
        fn(q, q % 2, q // 2)
        q += 1
    pairs = (hi - q) // 2
    if pairs > 1:
        with eng.Fori(0, pairs) as i:
            fn(2 * i + q, 0, i + q // 2)
            fn(2 * i + q + 1, 1, i + q // 2)
        q += 2 * pairs
    for q in range(q, hi):
        fn(q, q % 2, q // 2)


def from_step(q, n):
    return not isinstance(q, int) or q >= n


def expert_mixture(nc, T, x_in, x_out, layer):
    G, E = (1, 8) if layer == 0 else (2, 32)
    GE = G * E
    NBLK = -(-(TOPK * TOK + E * (P - 1)) // P // QUAD) * QUAD
    NQG = NBLK // QUAD
    NQ = G * NQG
    TE = NS * NT * E
    new = lambda name, rows: nc.dram_tensor(f"{name}_layer{layer}", [rows, P], F32, kind="Internal").ap()
    xg, yg = ([new(f"{name}{g}", NBLK * P) for g in range(G)] for name in ("rows", "results"))
    xn_d = new("normed", TOK)
    base_d = new("base", TOK) if layer == 0 else x_in
    with Scope(nc, "bd"[layer]) as S:
        sb, ps, sem = S.sb, S.ps, S.sem
        ident = sb("ident", [P, P])
        mhalf = sb("mhalf", [P, 1])
        bank = [ps(f"bank{n}", [P, 512]) for n in range(8)]

        best = sb("best", [P, G, NS, TOPK, NT])
        pick = sb("pick", [P, G, NS, TOPK, NT])
        wgt = sb("wgt", [P, G, NS, TOPK, NT])
        dest = sb("dest", [P, G, NS, TOPK, NT], U32)
        total = sb("total", [P, NS, G, NT])
        owner = sb("owner", [1, G * NBLK], I32)

        router = sb("router", [P, GE])
        if layer == 0:
            w1, w2 = sb("w1", [P, E * 512]), sb("w2", [P, E * 4 * P])
            b1, b2 = sb("b1", [P, E * 4]), sb("b2", [P, E * P])
            sw1, sw2 = sb("sw1", [P, 512]), sb("sw2", [P, 4, P])
            sb1, sb2 = sb("sb1", [P, 4]), sb("sb2", [P, P])
            loads = [(router, T["m_gate"]), (w1, T["L0_ffn_W1"].rearrange("e p f -> p e f")),
                     (w2, T["m_w2"]), (b1, T["m_b1"]),
                     (b2, T["L0_ffn_b2"].rearrange("e h -> (e h)").partition_broadcast(P)),
                     (sw1, T["L0_ffn_sW1"]), (sw2, T["L0_ffn_sW2"].rearrange("(c p) h -> p c h", p=P)),
                     (sb1, T["m_sb1"]), (sb2, T["L0_ffn_sb2"].partition_broadcast(P))]
        else:
            wgu, wd = sb("wgu", [P, GE * P]), sb("wd", [64, GE * P])
            loads = [(router, T["m_router"]), (wgu, T["m_wgu"]), (wd, T["m_wd"])]

        consts, cleared = sem("consts"), sem("cleared")
        memset = sem("memset")
        dve_passed, pool_passed = sem("dve_passed"), sem("pool_passed")
        x_loaded = [sem(f"x_loaded{u}") for u in range(2)]
        normed_stored = [sem(f"normed_stored{u}") for u in range(2)]
        base_stored = [sem(f"base_stored{u}") for u in range(2)]

        with Scope(nc, "bd"[layer] + "r") as R:
            zero = R.sb("zero", [P, 4, P])
            x = [R.sb(f"x{u}", [P, NT, P]) for u in range(2)]
            xn = [R.sb(f"xn{u}", [P, NT, P]) for u in range(2)]
            base = [R.sb(f"base{u}", [P, NT, P]) for u in range(2)]
            bst, mv = R.sb("bst", [P, NT, 6]), R.sb("mv", [P, NT, 2])
            veps, rstd = R.sb("veps", [P, NT]), R.sb("rstd", [P, NT])
            xnT = [R.sb(f"xnT{u}", [P, SUP]) for u in range(2)]
            lg, ex = R.sb("lg", [P, NT, G, E]), R.sb("ex", [P, NT, G, E])
            m8, i8 = R.sb("m8", [P, G, NT, 8]), R.sb("i8", [P, G, NT, 8], U32)
            sm = R.sb("sm", [P, G, NT])
            hT = [R.sb(f"hT{c}", [P, SUP]) for c in range(4)]
            pT, pL, pO, pH = bank[0], bank[1], bank[2], bank[3:7]
            ln_c, top_c = R.sem("ln_c"), R.sem("top_c")
            veps_ready, rstd_ready, xn_ready = R.sem("veps_ready"), R.sem("rstd_ready"), R.sem("xn_ready")
            xT_done, xnT_ready, lg_done = R.sem("xT_done"), R.sem("xnT_ready"), R.sem("lg_done")
            lg_shifted, ex_ready = R.sem("lg_shifted"), R.sem("ex_ready")
            h_done, h_ready, sh_done, base_ready = R.sem("h_done"), R.sem("h_ready"), R.sem("sh_done"), R.sem("base_ready")
            xv = x_in.rearrange("(s t p) d -> s p t d", t=NT, p=P)
            nv = xn_d.rearrange("(s t p) d -> s p t d", t=NT, p=P)
            bv = base_d.rearrange("(s t p) d -> s p t d", t=NT, p=P)

            with nc.Block() as block:
                @block.sync
                def _(sp):
                    sp.dma_start(x[0][:], xv[0]).then_inc(x_loaded[0], 16)
                    for dst, src in [(ident, T["ident"])] + loads:
                        sp.dma_start(dst[:], src).then_inc(consts, 16)

                    def step(s, u, h):
                        if not isinstance(s, int) or s + 1 < NS:
                            if from_step(s, 1):
                                sp.wait_ge(base_ready if layer == 0 else xn_ready, s)
                            sp.dma_start(x[1 - u][:], xv[s + 1]).then_inc(x_loaded[1 - u], 16)
                        sp.wait_ge(xn_ready, s + 1)
                        sp.dma_start(nv[s], xn[u][:]).then_inc(normed_stored[u], 16)
                        if layer == 0 and from_step(s, 1):
                            store_base(s - 1, 1 - u)

                    def store_base(s, u):
                        sp.wait_ge(base_ready, s + 1)
                        sp.dma_start(bv[s], base[u][:]).then_inc(base_stored[u], 16)

                    span(sp, 0, NS - 1, step)
                    step(NS - 1, (NS - 1) % 2, (NS - 1) // 2)
                    if layer == 0:
                        store_base(NS - 1, (NS - 1) % 2)
                        for u in range(2):
                            sp.wait_ge(base_stored[u], 16 * NS // 2)
                    for u in range(2):
                        sp.wait_ge(normed_stored[u], 16 * NS // 2)

                @block.scalar
                def _(act):
                    act.wait_ge(memset, 1)
                    for g in range(G):
                        gv = xg[g].rearrange("(n b p) d -> n p b d", b=4, p=P)
                        for n in range(NQG):
                            act.dma_start(gv[n], zero[:]).then_inc(cleared, 16)
                    act.wait_ge(consts, 16 * (len(loads) + 1))

                    def step(s, u, h):
                        act.wait_ge(xT_done, s + 1)
                        act.copy(xnT[u][:], pT[:]).then_inc(xnT_ready, 1)
                        if layer == 1:
                            act.wait_ge(lg_shifted, s + 1)
                            act.activation(ex[:], lg[:], ACT.Exp).then_inc(ex_ready, 1)
                        if layer == 0:
                            for c in range(4):
                                act.wait_ge(h_done, 4 * s + c + 1)
                                act.activation(hT[c][:], pH[c][:], ACT.Gelu, bias=sb1[:, c:c + 1]).then_inc(h_ready, 1)

                    span(act, 0, NS, step)
                    act.wait_ge(cleared, 16 * G * NQG)

                @block.tensor
                def _(pe):
                    pe.wait_ge(consts, 16 * (len(loads) + 1))

                    def step(s, u, h):
                        pe.wait_ge(xn_ready, s + 1)
                        for t in range(NT):
                            last = pe.transpose(pT[:, t * P:(t + 1) * P], xn[u][:, t, :], ident[:])
                        last.then_inc(xT_done, 1)
                        pe.wait_ge(xnT_ready, s + 1)
                        if from_step(s, 1):
                            pe.wait_ge(lg_shifted, s)
                        for t in range(NT):
                            last = pe.matmul(pL[:, t * GE:(t + 1) * GE], xnT[u][:, t * P:(t + 1) * P], router[:],
                                             start=True, stop=True)
                        last.then_inc(lg_done, 1)
                        if layer == 0:
                            for c in range(4):
                                pe.matmul(pH[c][:], sw1[:, c * P:(c + 1) * P], xnT[u][:], start=True,
                                          stop=True).then_inc(h_done, 1)
                            pe.wait_ge(h_ready, 4 * s + 4)
                            if from_step(s, 1):
                                pe.wait_ge(base_ready, s)
                            for t in range(NT):
                                for c in range(4):
                                    last = pe.matmul(pO[:, t * P:(t + 1) * P], hT[c][:, t * P:(t + 1) * P], sw2[:, c, :],
                                                     start=(c == 0), stop=(c == 3))
                            last.then_inc(sh_done, 1)

                    span(pe, 0, NS, step)

                @block.vector
                def _(dve):
                    ln, top = Chain(dve, ln_c, dve_passed), Chain(dve, top_c, dve_passed)
                    dve.memset(mhalf[:], -0.5)
                    dve.memset(zero[:], 0.0).then_inc(memset, 1)
                    dve.wait_ge(consts, 16 * (len(loads) + 1))

                    def layernorm(s, u, h):
                        ln.start(2 * s)
                        dve.wait_ge(x_loaded[u], 16 * h + 16)
                        for t in range(NT):
                            last = dve.bn_stats(bst[:, t, :], x[u][:, t, :])
                        ln.step(last, own_wait=True)
                        for t in range(NT):
                            last = dve.bn_aggr(mv[:, t, :], bst[:, t, :])
                        ln.step(last)
                        dve.tensor_scalar(veps[:], mv[:, :, 1], LN_EPS, None, ALU.add).then_inc(veps_ready, 1)
                        dve.wait_ge(rstd_ready, s + 1)
                        if from_step(s, 2):
                            dve.wait_ge(normed_stored[u], 16 * h)
                            dve.wait_ge(xT_done, s - 1)
                        for t in range(NT):
                            last = dve.tensor_scalar(xn[u][:, t, :], x[u][:, t, :], mv[:, t, 0:1], rstd[:, t:t + 1],
                                                     ALU.subtract, ALU.mult)
                        last.then_inc(xn_ready, 1)

                    def choose(s, u, h):
                        nsteps = 3 if layer == 0 else 4
                        top.start(nsteps * s)
                        dve.wait_ge(lg_done, s + 1)
                        if layer == 1 and from_step(s, 1):
                            dve.wait_ge(ex_ready, s)
                        top.step(dve.tensor_copy(lg[:].rearrange("p t g e -> p (t g e)"), pL[:, 0:NT * GE]), own_wait=True)
                        for g in range(G):
                            for t in range(NT):
                                last = dve.max(m8[:, g, t, :], lg[:, t, g, :])
                        top.step(last, own_wait=True)
                        for g in range(G):
                            for t in range(NT):
                                last = dve.max_index(i8[:, g, t, :], m8[:, g, t, :], lg[:, t, g, :])
                        top.step(last)
                        for g in range(G):
                            dve.tensor_copy(pick[:, g].rearrange("p s k t -> p (s k) t")[:, bass.ds(2 * s, 2), :],
                                            i8[:, g, :, 0:2].rearrange("p t k -> p k t"))
                            last = dve.tensor_copy(best[:, g].rearrange("p s k t -> p (s k) t")[:, bass.ds(2 * s, 2), :],
                                                   m8[:, g, :, 0:2].rearrange("p t k -> p k t"))
                        if layer == 0:
                            last.then_inc(lg_shifted, 1)
                        else:
                            for g in range(G):
                                last = dve.tensor_tensor(lg[:, :, g, :], lg[:, :, g, :],
                                                         m8[:, g, :, 0:1].to_broadcast([P, NT, E]), ALU.subtract)
                            last.then_inc(lg_shifted, 1)
                            dve.wait_ge(ex_ready, s + 1)
                            top.step(dve.tensor_reduce(sm[:].rearrange("p g t -> p t g"), ex[:], AX.X, ALU.add))
                            dve.tensor_copy(total[:].rearrange("p s g t -> p s (g t)")[:, bass.ds(s, 1), :],
                                            sm[:].rearrange("p g t -> p (g t)").unsqueeze(1))

                    def add_base(s, u, h):
                        dve.wait_ge(sh_done, s + 1)
                        if from_step(s, 2):
                            dve.wait_ge(base_stored[u], 16 * h)
                        top.start(3 * s + 2)
                        dve.tensor_tensor(base[u][:], pO[:].rearrange("p (t n) -> p t n", t=NT), x[u][:],
                                          ALU.add).then_inc(sum_ready, 1)
                        dve.wait_ge(sum_ready, s + 1)
                        dve.tensor_tensor(base[u][:], base[u][:], sb2[:].unsqueeze(1).to_broadcast([P, NT, P]),
                                          ALU.add).then_inc(base_ready, 1)

                    sum_ready = R.sem("sum_ready")
                    layernorm(0, 0, 0)

                    def step(s, u, h):
                        if not isinstance(s, int) or s + 1 < NS:
                            layernorm(s + 1, 1 - u, h + u)
                        choose(s, u, h)
                        if layer == 0:
                            add_base(s, u, h)

                    span(dve, 0, NS - 1, step)
                    step(NS - 1, (NS - 1) % 2, (NS - 1) // 2)

                @block.gpsimd
                def _(pool):
                    pool.wait_ge(memset, 1)

                    def step(s, u, h):
                        pool.wait_ge(veps_ready, s + 1)
                        pool.tensor_tensor(rstd[:], veps[:], mhalf[:].to_broadcast([P, NT]), ALU.pow).then_inc(rstd_ready, 1)

                    span(pool, 0, NS, step)

        with Scope(nc, "bd"[layer] + "s") as R:
            iota = R.sb("iota", [P, P])
            before, ones = R.sb("before", [P, P], BF16), R.sb("ones", [P, P], BF16)
            NTL = NS * NT
            oh = [R.sb(f"oh{k}", [P, NS, NT, E]) for k in range(TOPK)]
            both = R.sb("both", [P, NTL * E], BF16)
            tot, run = R.sb("tot", [P, E, NTL]), R.sb("run", [P, E, NTL])
            keep = R.sb("keep", [P, E, NTL])
            one_e = R.sb("one_e", [P, E])
            nbi, nb = R.sb("nbi", [P, E], I32), R.sb("nb", [P, E])
            end, start = R.sb("end", [P, E]), R.sb("start", [P, E])
            pos = R.sb("pos", [P, NS, NT, E])
            place = R.sb("place", [P, NS, TOPK, NT])
            cmp, own = R.sb("cmp", [1, NBLK, E]), R.sb("own", [1, NBLK])
            dif, den = R.sb("dif", [P, G, NS, TOPK, NT]), R.sb("den", [P, G, NS, NT])
            tables, route_c = R.sem("tables"), R.sem("route_c")
            both_ready, ranks_done, w_sub, w_exp = R.sem("both_ready"), R.sem("ranks_done"), R.sem("w_sub"), R.sem("w_exp")
            NB = -(-TE // 512)
            W = TE // NB
            rank_b, tot_b = bank[0:NB], bank[2:2 + NB]

            with nc.Block() as block:
                @block.sync
                def _(sp):
                    sp.dma_start(iota[:], T["m_iota"].partition_broadcast(P)).then_inc(tables, 16)
                    sp.dma_start(before[:], T["m_before"].bitcast(BF16)).then_inc(tables, 16)

                @block.scalar
                def _(act):
                    act.wait_ge(w_sub, 1)
                    act.activation(dif[:], dif[:], ACT.Exp).then_inc(w_exp, 1)

                @block.tensor
                def _(pe):
                    pe.wait_ge(tables, 32)
                    for g in range(G):
                        pe.wait_ge(both_ready, g + 1)
                        for n in range(NB):
                            pe.matmul(rank_b[n][:, 0:W], before[:], both[:, n * W:(n + 1) * W], start=True, stop=True)
                            last = pe.matmul(tot_b[n][:, 0:W], ones[:], both[:, n * W:(n + 1) * W], start=True, stop=True)
                        last.then_inc(ranks_done, 1)

                @block.vector
                def _(dve):
                    ch = Chain(dve, route_c)
                    dve.memset(ones[:], 1.0)
                    dve.memset(one_e[:], 1.0)
                    ch.step(dve.memset(keep[:], 1.0))
                    ch.step(dve.memset(keep[:, :, 0:1], 0.0))
                    dve.tensor_tensor(dif[:].rearrange("p g s k t -> p (g s) k t"),
                                      best[:].rearrange("p g s k t -> p (g s) k t"),
                                      best[:].rearrange("p g s k t -> p (g s) k t")[:, :, 0:1, :].to_broadcast(
                                          [P, G * NS, TOPK, NT]), ALU.subtract).then_inc(w_sub, 1)
                    dve.wait_ge(w_exp, 1)
                    if layer == 0:
                        ch.step(dve.tensor_tensor(den[:], dif[:, :, :, 0, :], dif[:, :, :, 1, :], ALU.add))
                    else:
                        ch.step(dve.tensor_scalar(den[:], total[:].rearrange("p s g t -> p g s t"), 2.0, None, ALU.mult))
                    ch.step(dve.reciprocal(den[:], den[:]))
                    for k in range(TOPK):
                        last = dve.tensor_tensor(wgt[:, :, :, k, :], dif[:, :, :, k, :], den[:], ALU.mult)
                    ch.step(last)
                    dve.wait_ge(tables, 32)
                    for g in range(G):
                        for k in range(TOPK):
                            last = dve.tensor_tensor(oh[k][:].rearrange("p s t e -> p s t e"),
                                                     iota[:, 0:E].unsqueeze(1).unsqueeze(1).to_broadcast([P, NS, NT, E]),
                                                     pick[:, g, :, k, :].unsqueeze(3).to_broadcast([P, NS, NT, E]), ALU.is_equal)
                        ch.step(last)
                        dve.tensor_tensor(both[:], oh[0][:].rearrange("p s t e -> p (s t e)"),
                                          oh[1][:].rearrange("p s t e -> p (s t e)"), ALU.add).then_inc(both_ready, 1)
                        dve.wait_ge(ranks_done, g + 1)
                        ntb = NTL // NB
                        for n in range(NB):
                            last = dve.tensor_copy(tot[:, :, n * ntb:(n + 1) * ntb],
                                                   tot_b[n][:, 0:W].rearrange("p (t e) -> p e t", e=E))
                        ch.step(last)
                        ch.step(dve.tensor_tensor_scan(run[:].rearrange("p e t -> p (e t)"), keep[:].rearrange("p e t -> p (e t)"),
                                                       tot[:].rearrange("p e t -> p (e t)"), 0.0, ALU.mult, ALU.add))
                        ch.step(dve.tensor_scalar(nbi[:], run[:, :, NTL - 1], float(P - 1), None, ALU.add))
                        ch.step(dve.tensor_scalar(nbi[:], nbi[:], 7, None, ALU.logical_shift_right))
                        ch.step(dve.tensor_copy(nb[:], nbi[:]))
                        ch.step(dve.tensor_tensor_scan(end[:], one_e[:], nb[:], 0.0, ALU.mult, ALU.add))
                        ch.step(dve.tensor_tensor(start[:], end[:], nb[:], ALU.subtract))
                        ch.step(dve.scalar_tensor_tensor(run[:], start[:].unsqueeze(2).to_broadcast([P, E, NTL]), float(P),
                                                         run[:], ALU.mult, ALU.add))
                        ch.step(dve.tensor_tensor(run[:], run[:], tot[:], ALU.subtract))
                        posf = pos[:].rearrange("p s t e -> p (s t) e")
                        for n in range(NB):
                            last = dve.tensor_tensor(posf[:, n * ntb:(n + 1) * ntb, :],
                                                     rank_b[n][:, 0:W].rearrange("p (t e) -> p t e", e=E),
                                                     run[:, :, n * ntb:(n + 1) * ntb].rearrange("p e t -> p t e"), ALU.add)
                        ch.step(last)
                        for k in range(TOPK):
                            last = dve.tensor_tensor(oh[k][:], oh[k][:], pos[:], ALU.mult)
                        ch.step(last)
                        for k in range(TOPK):
                            last = dve.tensor_reduce(place[:, :, k, :], oh[k][:], AX.X, ALU.add)
                        ch.step(last)
                        ch.step(dve.tensor_copy(dest[:, g], place[:]))
                        ch.step(dve.tensor_tensor(cmp[:], end[0:1, :].unsqueeze(1).to_broadcast([1, NBLK, E]),
                                                  iota[0:1, 0:NBLK].unsqueeze(2).to_broadcast([1, NBLK, E]), ALU.is_le))
                        ch.step(dve.tensor_reduce(own[:], cmp[:], AX.X, ALU.add))
                        ch.step(dve.tensor_scalar(own[:], own[:], float(E - 1), float(g * E), ALU.min, ALU.add))
                        ch.step(dve.tensor_copy(owner[0:1, g * NBLK:(g + 1) * NBLK], own[:]))

        with Scope(nc, "bd"[layer] + "e") as R:
            xs = [R.sb(f"xs{u}", [P, NT, P]) for u in range(2)]
            ids = [R.sb(f"ids{u}", [P, TOPK * NT], U32) for u in range(2)]
            got = [R.sb(f"got{u}", [P, TOPK, NT, P]) for u in range(2)]
            bs = [R.sb(f"bs{u}", [P, NT, P]) for u in range(2)]
            xq = [R.sb(f"xq{u}", [P, QUAD, P]) for u in range(2)]
            xqT = [R.sb(f"xqT{u}", [P, QUAD * P]) for u in range(2)]
            yq = [R.sb(f"yq{u}", [P, QUAD, P]) for u in range(2)]
            pX, pY = bank[0:2], bank[2:4]
            if layer == 0:
                wx = [R.sb(f"wx{n}", [P, 512]) for n in range(2)]
                bx = [R.sb(f"bx{n}", [P, 4]) for n in range(2)]
                hx = [R.sb(f"hx{n}", [P, 4, P]) for n in range(2)]
                pHx = bank[4:6]
            else:
                wx = [R.sb(f"wx{u}", [P, QUAD, P]) for u in range(2)]
                gs = [R.sb(f"gs{u}", [64, QUAD * P]) for u in range(2)]
                hx = [R.sb(f"hx{u}", [64, QUAD * P]) for u in range(2)]
                pG, pU = bank[4:6], bank[6:8]

            two = lambda name: [R.sem(f"{name}{u}") for u in range(2)]
            xs_loaded, bs_loaded, gathered, final_stored = two("xs_loaded"), two("bs_loaded"), two("gathered"), two("final_stored")
            scattered = [two(f"scattered{g}_") for g in range(G)]
            ids_ready, sum_c = R.sem("ids_ready"), R.sem("sum_c")
            xq_loaded, results_stored = two("xq_loaded"), two("results_stored")
            xqT_done, xqT_ready, w_ready, h_done, g_ready, h_ready, y_done, y_ready = (
                R.sem(n) for n in ("xqT_done", "xqT_ready", "w_ready", "hx_done", "g_ready", "hx_ready", "y_done", "y_ready"))
            nv = xn_d.rearrange("(s t p) d -> s p t d", t=NT, p=P)
            inv = base_d.rearrange("(s t p) d -> s p t d", t=NT, p=P)
            outv = x_out.rearrange("(s t p) d -> s p t d", t=NT, p=P)

            def each_quad(eng, fn, lo=0):
                span(eng, lo, NQ, fn)

            with nc.Block() as block:
                @block.gpsimd
                def _(pool):
                    add = Chain(pool, sum_c, pool_passed)

                    def take_ids(g, s, u):
                        pool.tensor_copy(ids[u][:], dest[:, g].rearrange("p s k t -> p s (k t)")[:, bass.ds(s, 1), :]
                                         .rearrange("p a n -> p (a n)")).then_inc(ids_ready, 1)

                    def scatter(g):
                        def load(s, u, h):
                            if from_step(s, 2):
                                pool.wait_ge(scattered[g][u], 16 * 8 * h)
                                add.own_wait()
                            elif g:
                                pool.wait_ge(scattered[g - 1][u], 16 * 8 * NS // 2)
                            pool.dma_start(xs[u][:], nv[s]).then_inc(xs_loaded[u], 16)

                        def step(s, u, h):
                            if not isinstance(s, int) or s + 1 < NS:
                                load(s + 1, 1 - u, h + u)
                            pool.wait_ge(xs_loaded[u], 16 * (NS // 2 * g + 1) + 16 * h)
                            add.own_wait()
                            take_ids(g, s, u)
                            pool.wait_ge(cleared, 16 * G * NQG)
                            pool.wait_ge(ids_ready, NS * g + 1 + s)
                            add.own_wait()
                            for k in range(TOPK):
                                for t in range(NT):
                                    n = k * NT + t
                                    pool.indirect_dma_start(xg[g], bass.IndirectOffsetOnAxis(ap=ids[u][:, n:n + 1], axis=0),
                                                            xs[u][:, t, :], None).then_inc(scattered[g][u], 16)

                        load(0, 0, 0)
                        span(pool, 0, NS - 1, step)
                        step(NS - 1, (NS - 1) % 2, (NS - 1) // 2)

                    def gather(g):
                        quads = NQG * (g + 1)
                        for u in range(2):
                            pool.wait_ge(results_stored[u], 16 * ((quads + 1 - u) // 2))
                        if g:
                            for u in range(2):
                                pool.wait_ge(final_stored[u], 16 * NS // 2)
                        src = inv if g == 0 else outv

                        def fetch(s, u, h):
                            if from_step(s, 2):
                                pool.wait_ge(final_stored[u], 16 * (NS // 2 * g) + 16 * h)
                                add.own_wait()
                            take_ids(g, s, u)
                            pool.dma_start(bs[u][:], src[s]).then_inc(bs_loaded[u], 16)
                            pool.wait_ge(ids_ready, NS * (G + g) + 1 + s)
                            add.own_wait()
                            for k in range(TOPK):
                                for t in range(NT):
                                    n = k * NT + t
                                    pool.indirect_dma_start(got[u][:, k, t, :], None, yg[g],
                                                            bass.IndirectOffsetOnAxis(ap=ids[u][:, n:n + 1], axis=0)
                                                            ).then_inc(gathered[u], 16)

                        def step(s, u, h):
                            if not isinstance(s, int) or s + 1 < NS:
                                fetch(s + 1, 1 - u, h + u)
                            pool.wait_ge(gathered[u], 16 * 8 * (NS // 2 * g + 1) + 16 * 8 * h)
                            add.start(3 * NS * g + 3 * s)
                            add.step(pool.tensor_tensor(got[u][:].rearrange("p k t d -> p (k t) d"),
                                                        got[u][:].rearrange("p k t d -> p (k t) d"),
                                                        wgt[:, g].rearrange("p s k t -> p (s k t)")[:, bass.ds(8 * s, 8)]
                                                        .unsqueeze(2).to_broadcast([P, 8, P]), ALU.mult))
                            pool.wait_ge(bs_loaded[u], 16 * (NS // 2 * g + 1) + 16 * h)
                            add.step(pool.tensor_tensor(bs[u][:], bs[u][:], got[u][:, 0], ALU.add))
                            add.step(pool.tensor_tensor(bs[u][:], bs[u][:], got[u][:, 1], ALU.add), own_wait=True)
                            pool.dma_start(outv[s], bs[u][:]).then_inc(final_stored[u], 16)

                        fetch(0, 0, 0)
                        span(pool, 0, NS - 1, step)
                        step(NS - 1, (NS - 1) % 2, (NS - 1) // 2)

                    for g in range(G):
                        scatter(g)
                    for g in range(G):
                        gather(g)
                    for u in range(2):
                        pool.wait_ge(final_stored[u], 16 * G * NS // 2)

                @block.sync
                def _(sp):
                    rows = [t.rearrange("(n b p) d -> n p b d", b=QUAD, p=P) for t in xg]
                    results = [t.rearrange("(n b p) d -> n p b d", b=QUAD, p=P) for t in yg]

                    def load(g, q, u):
                        if from_step(q, 2):
                            sp.wait_ge(xqT_done, q - 1)
                        sp.dma_start(xq[u][:], rows[g][q - g * NQG]).then_inc(xq_loaded[u], 16)

                    def store(g, q, u):
                        sp.wait_ge(y_ready, q + 1)
                        sp.dma_start(results[g][q - g * NQG], yq[u][:]).then_inc(results_stored[u], 16)

                    for g in range(G):
                        first = g * NQG
                        for u in range(2):
                            sp.wait_ge(scattered[g][u], 16 * 8 * NS // 2)
                        load(g, first, first % 2)
                        if g:
                            store(g - 1, first - 2, (first - 2) % 2)
                        load(g, first + 1, (first + 1) % 2)
                        if g:
                            store(g - 1, first - 1, (first - 1) % 2)

                        def step(q, u, h):
                            load(g, q + 1, 1 - u)
                            store(g, q - 1, 1 - u)

                        span(sp, first + 1, first + NQG - 1, step)
                    store(G - 1, NQ - 2, (NQ - 2) % 2)
                    store(G - 1, NQ - 1, (NQ - 1) % 2)
                    for u in range(2):
                        sp.wait_ge(results_stored[u], 16 * ((NQ + 1 - u) // 2))

                def owner_of(eng, n):
                    at = owner[0:1, n:n + 1] if isinstance(n, int) else owner[0:1, bass.ds(n, 1)]
                    return eng.value_load(at, min_val=0, max_val=GE - 1)

                @block.scalar
                def _(act):
                    def turn(q, u, h):
                        act.wait_ge(xqT_done, q + 1)
                        act.copy(xqT[u][:], pX[u][:]).then_inc(xqT_ready, 1)

                    def step0(q, u, h):
                        turn(q, u, h)
                        for j in range(QUAD):
                            act.wait_ge(h_done, QUAD * q + j + 1)
                            for c in range(4):
                                last = act.activation(hx[j % 2][:, c, :], pHx[j % 2][:, c * P:(c + 1) * P], ACT.Gelu,
                                                      bias=bx[j % 2][:, c:c + 1])
                            last.then_inc(h_ready, 1)

                    def step1(q, u, h):
                        turn(q, u, h)
                        act.wait_ge(h_done, q + 1)
                        act.activation(gs[u][:], pG[u][0:64, :], ACT.Silu).then_inc(g_ready, 1)

                    each_quad(act, step0 if layer == 0 else step1)

                @block.vector
                def _(dve):
                    def weights0(q, j):
                        e = owner_of(dve, QUAD * q + j)
                        if from_step(q, 1) or j >= 2:
                            dve.wait_ge(h_done, QUAD * q + j - 1)
                        dve.tensor_copy(wx[j % 2][:], w1[:, bass.ds(e * 512, 512)])
                        if from_step(q, 1) or j >= 2:
                            dve.wait_ge(h_ready, QUAD * q + j - 1)
                        dve.tensor_copy(bx[j % 2][:], b1[:, bass.ds(e * 4, 4)]).then_inc(w_ready, 1)

                    def results0(q, u, h):
                        es = [owner_of(dve, QUAD * q + j) for j in range(QUAD)]
                        if from_step(q, 2):
                            dve.wait_ge(results_stored[u], 16 * h)
                        dve.wait_ge(y_done, q + 1)
                        for j in range(QUAD):
                            last = dve.tensor_tensor(yq[u][:, j, :], pY[u][:, j * P:(j + 1) * P],
                                                     b2[:, bass.ds(es[j] * P, P)], ALU.add)
                        last.then_inc(y_ready, 1)

                    def step0(q, u, h):
                        for j in range(QUAD):
                            weights0(q, j)
                            if j == 1 and from_step(q, 1):
                                results0(q - 1, 1 - u, h - 1 + u)

                    def weights1(q, u):
                        es = [owner_of(dve, QUAD * q + j) for j in range(QUAD)]
                        if from_step(q, 2):
                            dve.wait_ge(h_done, q - 1)
                        for j in range(QUAD):
                            last = dve.tensor_copy(wx[u][:, j, :], wgu[:, bass.ds(es[j] * P, P)])
                        last.then_inc(w_ready, 1)

                    def results1(q, u, h):
                        if from_step(q, 2):
                            dve.wait_ge(results_stored[u], 16 * h)
                        dve.wait_ge(y_done, q + 1)
                        dve.tensor_copy(yq[u][:].rearrange("p b d -> p (b d)"), pY[u][:]).then_inc(y_ready, 1)

                    def step1(q, u, h):
                        if not isinstance(q, int) or q + 1 < NQ:
                            weights1(q + 1, 1 - u)
                        dve.wait_ge(g_ready, q + 1)
                        if from_step(q, 2):
                            dve.wait_ge(y_done, q - 1)
                        dve.tensor_tensor(hx[u][:], gs[u][:], pU[u][0:64, :], ALU.mult).then_inc(h_ready, 1)
                        if from_step(q, 1):
                            results1(q - 1, 1 - u, h - 1 + u)

                    if layer == 0:
                        each_quad(dve, step0)
                        results0(NQ - 1, (NQ - 1) % 2, (NQ - 1) // 2)
                    else:
                        weights1(0, 0)
                        span(dve, 0, NQ - 1, step1)
                        step1(NQ - 1, (NQ - 1) % 2, (NQ - 1) // 2)
                        results1(NQ - 1, (NQ - 1) % 2, (NQ - 1) // 2)

                @block.tensor
                def _(pe):
                    def turn(q, u, h):
                        pe.wait_ge(xq_loaded[u], 16 * h + 16)
                        if from_step(q, 2):
                            pe.wait_ge(xqT_ready, q - 1)
                        for j in range(QUAD):
                            last = pe.transpose(pX[u][:, j * P:(j + 1) * P], xq[u][:, j, :], ident[:])
                        last.then_inc(xqT_done, 1)

                    def hidden0(q, u, j):
                        pe.wait_ge(w_ready, QUAD * q + j + 1)
                        if j == 0:
                            pe.wait_ge(xqT_ready, q + 1)
                        if from_step(q, 1) or j >= 2:
                            pe.wait_ge(h_ready, QUAD * q + j - 1)
                        for c in range(4):
                            last = pe.matmul(pHx[j % 2][:, c * P:(c + 1) * P], wx[j % 2][:, c * P:(c + 1) * P],
                                             xqT[u][:, j * P:(j + 1) * P], start=True, stop=True)
                        last.then_inc(h_done, 1)

                    def out0(q, u, j):
                        e = owner_of(pe, QUAD * q + j)
                        pe.wait_ge(h_ready, QUAD * q + j + 1)
                        if j == 0 and from_step(q, 2):
                            pe.wait_ge(y_ready, q - 1)
                        for c in range(4):
                            last = pe.matmul(pY[u][:, j * P:(j + 1) * P], hx[j % 2][:, c, :],
                                             w2[:, bass.ds(e * 512 + c * P, P)], start=(c == 0), stop=(c == 3))
                        if j == QUAD - 1:
                            last.then_inc(y_done, 1)

                    def step0(q, u, h):
                        turn(q, u, h)
                        for j in range(QUAD):
                            hidden0(q, u, j)
                            if j:
                                out0(q, u, j - 1)
                            elif from_step(q, 1):
                                out0(q - 1, 1 - u, QUAD - 1)

                    def hidden1(q, u):
                        pe.wait_ge(w_ready, q + 1)
                        pe.wait_ge(xqT_ready, q + 1)
                        if from_step(q, 2):
                            pe.wait_ge(h_ready, q - 1)
                        for j in range(QUAD):
                            cols = slice(j * P, (j + 1) * P)
                            pe.matmul(pG[u][0:64, cols], wx[u][:, j, 0:64], xqT[u][:, cols], start=True, stop=True)
                            last = pe.matmul(pU[u][0:64, cols], wx[u][:, j, 64:128], xqT[u][:, cols], start=True, stop=True)
                        last.then_inc(h_done, 1)

                    def out1(q, u):
                        es = [owner_of(pe, QUAD * q + j) for j in range(QUAD)]
                        pe.wait_ge(h_ready, q + 1)
                        if from_step(q, 2):
                            pe.wait_ge(y_ready, q - 1)
                        for j in range(QUAD):
                            cols = slice(j * P, (j + 1) * P)
                            last = pe.matmul(pY[u][:, cols], hx[u][:, cols], wd[:, bass.ds(es[j] * P, P)], start=True, stop=True)
                        last.then_inc(y_done, 1)

                    def step1(q, u, h):
                        turn(q, u, h)
                        hidden1(q, u)
                        if from_step(q, 1):
                            out1(q - 1, 1 - u)

                    if layer == 0:
                        each_quad(pe, step0)
                        out0(NQ - 1, (NQ - 1) % 2, QUAD - 1)
                    else:
                        each_quad(pe, step1)
                        out1(NQ - 1, (NQ - 1) % 2)



def hopfield_mixer(nc, T, x_in, x_out):
    NB = TOK // SEQ
    NT = SEQ // P
    NH, HD, NP, NG = 16, 8, 8, 4
    RING = 3
    with Scope(nc, "c") as S:
        sb, ps, sem = S.sb, S.ps, S.sem
        wqkv, wo = sb("wqkv", [P, 3 * P]), sb("wo", [P, P])
        bqkv, bo = sb("bqkv", [P, 3 * P]), sb("bo", [P, P])
        lnw, lnb = sb("lnw", [P, P]), sb("lnb", [P, P])
        ident, ident_bf = sb("ident", [P, P]), sb("ident_bf", [P, P], BF16)
        mhalf = sb("mhalf", [P, 1])

        x = [sb(f"x{u}", [P, NT, P]) for u in range(RING)]
        xres = [sb(f"xres{u}", [P, NT, P]) for u in range(RING)]
        y = [sb(f"y{u}", [P, NT, P]) for u in range(RING)]
        r, z = sb("r", [P, NT, P]), sb("z", [P, NT, P])
        st1, mv1, ve1, rs1 = sb("st1", [P, NT, 6]), sb("mv1", [P, NT, 2]), sb("ve1", [P, NT]), sb("rs1", [P, NT])
        st2, mv2, ve2, rs2 = sb("st2", [P, NT, 6]), sb("mv2", [P, NT, 2]), sb("ve2", [P, NT]), sb("rs2", [P, NT])
        zT = sb("zT", [P, SEQ])
        qk = sb("qk", [P, NT, 2 * NH, HD])
        sq, ss = sb("sq", [P, NT, 2 * NH, HD]), sb("ss", [P, NT * 2 * NH])
        rn, na, nb_ = sb("rn", [P, NT * 2 * NH]), sb("na", [P, NT * 2 * NH]), sb("nb", [P, NT * 2 * NH])
        parts = sb("parts", [P, NT, 2 * NH, 3, HD], BF16)
        q6, k6 = sb("q6", [P, NT, NH, 64], BF16), sb("k6", [P, NT, NH, 64], BF16)
        qT = sb("qT", [P, NP, SEQ], BF16)
        kT = [sb(f"kT{u}", [P, NP, SEQ], BF16) for u in range(RING)]
        v1 = [sb(f"v1{u}", [P, NT, NH, 32]) for u in range(RING)]
        e = [sb(f"e{n}", [P, 2, NT, SEQ]) for n in range(4)]
        ot0, ot1 = sb("ot0", [P, NG, SEQ]), sb("ot1", [P, NG, SEQ])
        otb = sb("otb", [P, NG, SEQ], BF16)
        rec, s0, mx = sb("rec", [P, NT, NH]), sb("s0", [P, NT, NH, HD]), sb("mx", [P, NT, NH])
        sparts = sb("sparts", [P, NT, NH, 3, HD], BF16)
        s6 = sb("s6", [P, NT, NH, 64], BF16)
        sT = sb("sT", [P, NP, SEQ], BF16)
        rec1, s1 = sb("rec1", [P, NT, NH]), sb("s1", [P, NT, NH, HD])
        s1T = sb("s1T", [P, SEQ])

        px = [ps(f"px{n}", [P, 2, NT * SEQ]) for n in range(2)]
        po = [ps(f"po{n}", [P, 512]) for n in range(2)]
        pm = [ps(f"pm{n}", [P, 512]) for n in range(2)]

        consts, memsets, memsets_pool = sem("consts"), sem("memsets"), sem("memsets_pool")
        x_loaded = [sem(f"x_loaded{u}") for u in range(RING)]
        stored = [sem(f"stored{u}") for u in range(RING)]
        ln_c, norm_c, mid_c, out_c = (sem(n) for n in ("ln_c", "norm_c", "mid_c", "out_c"))
        split_c, ssplit_c, zln_c, res_c = (sem(n) for n in ("split_c", "ssplit_c", "zln_c", "res_c"))
        ve1_ready, rs1_ready, r_ready = sem("ve1_ready"), sem("rs1_ready"), sem("r_ready")
        ve2_ready, rs2_ready, z_ready, xres_ready = sem("ve2_ready"), sem("rs2_ready"), sem("z_ready"), sem("xres_ready")
        zT_done, zT_ready, qkv_done, qkv_ready = sem("zT_done"), sem("zT_ready"), sem("qkv_done"), sem("qkv_ready")
        qk_normed, q6_ready, k6_ready = sem("qk_normed"), sem("q6_ready"), sem("k6_ready")
        k6T_done, kT_ready, q6T_done, qT_ready = sem("k6T_done"), sem("kT_ready"), sem("q6T_done"), sem("qT_ready")
        sim_done, exp_done, pv_done, ot_copied = sem("sim_done"), sem("exp_done"), sem("pv_done"), sem("ot_copied")
        otT_done, s0_ready, otb_ready = sem("otT_done"), sem("s0_ready"), sem("otb_ready")
        mxs_done, mx_ready = sem("mxs_done"), sem("mx_ready")
        s6_ready, aug_ready, s6T_done, sT_ready = sem("s6_ready"), sem("aug_ready"), sem("s6T_done"), sem("sT_ready")
        ot1T_done, s1_ready, s1T_done, s1T_ready = sem("ot1T_done"), sem("s1_ready"), sem("s1T_done"), sem("s1T_ready")
        dve_passed, pool_passed = sem("dve_passed"), sem("pool_passed")
        wo_done, y_ready = sem("wo_done"), sem("y_ready")

        xv = x_in.rearrange("(b t p) d -> b p t d", t=NT, p=P)
        yv = x_out.rearrange("(b t p) d -> b p t d", t=NT, p=P)
        NCONST = 10

        class Pass:

            def __init__(self, i, k):
                self.i, self.k, self.b = i, k, 3 * i + k
                b = self.b if isinstance(i, int) else RING + 1
                self.first_step = 0 <= b < NB
                self.second_step = 1 <= b <= NB
                self.prepare = b + 1 < NB
                self.between = 1 <= b <= NB
                self.finish = b >= 2
                self.n = b
                self.loop0 = 2 * self.b - 1 if b >= 1 else 0
                self.loop1 = 2 * self.b if b < NB else 2 * self.b - 1
                self.pend0 = None if b < 2 else (2 * self.b - 2, k - 2)
                self.pend1 = (self.loop0, k) if self.first_step else None

            def ring(self, d=0):
                return (self.k + d) % RING

            def turn(self, d=0):
                return self.i + (self.k + d) // RING

        def each_pass(eng, run):
            run(Pass(0, -1))
            for k in range(RING + 1):
                run(Pass(0, k))
            with eng.Fori(0, (NB - 4) // RING - 1) as i:
                for k in range(RING):
                    run(Pass(i, RING + 1 + k))
            for k in range(RING + 1, RING + 5):
                run(Pass((NB - 4) // RING - 1, k))

        with nc.Block() as block:
            @block.sync
            def _(sp):
                for dst, src in ((ident, T["ident"]), (ident_bf, T["ident_bf"].bitcast(BF16)),
                                 (lnw, T["L1_attn_ln_w"].partition_broadcast(P)),
                                 (lnb, T["L1_attn_ln_b"].partition_broadcast(P)),
                                 (bo, T["L1_attn_bo"].partition_broadcast(P)), (wo, T["L1_attn_Wo"])):
                    sp.dma_start(dst[:], src).then_inc(consts, 16)
                for n, name in enumerate("qkv"):
                    sp.dma_start(wqkv[:, n * P:(n + 1) * P], T[f"L1_attn_W{name}"]).then_inc(consts, 16)
                sp.dma_start(bqkv[:], T["c_bqkv"].partition_broadcast(P)).then_inc(consts, 16)

                def load(p, d):
                    if p.n + d >= RING:
                        sp.wait_ge(xres_ready, p.b + d - RING + 1)
                    sp.dma_start(x[p.ring(d)][:], xv[p.b + d]).then_inc(x_loaded[p.ring(d)], 16)

                def run(p):
                    if p.n == -1:
                        load(p, 1)
                    if p.n + 2 < NB:
                        load(p, 2)
                    if p.finish:
                        sp.wait_ge(y_ready, p.b - 1)
                        sp.dma_start(yv[p.b - 2], y[p.ring(-2)][:]).then_inc(stored[p.ring(-2)], 16)

                each_pass(sp, run)
                sp.wait_ge(y_ready, NB)
                sp.dma_start(yv[NB - 1], y[(NB - 1) % RING][:]).then_inc(stored[(NB - 1) % RING], 16)
                for u in range(RING):
                    sp.wait_ge(stored[u], 16 * len(range(u, NB, RING)))

            @block.vector
            def _(dve):
                ln, norm, mid, fin = (Chain(dve, s, dve_passed) for s in (ln_c, norm_c, mid_c, out_c))
                for t in (q6, k6, s6):
                    dve.memset(t[:].rearrange("p t h c -> p (t h c)").bitcast(U32), 0)
                for u in range(RING):
                    dve.memset(v1[u][:], 0.0)
                dve.memset(mhalf[:], -0.5).then_inc(memsets, 1)
                dve.wait_ge(memsets, 1)
                dve.memset(k6[:, :, :, 48:51], 1.0)
                for u in range(RING):
                    dve.memset(v1[u][:, :, :, HD:HD + 1], 1.0)
                dve.memset(na[:], 0.0).then_inc(memsets, 1)
                dve.wait_ge(consts, 16 * NCONST)
                dve.wait_ge(memsets, 2)

                def layernorms(p):
                    ln.start(4 * (p.b + 1))
                    xb = x[p.ring(1)]
                    dve.wait_ge(x_loaded[p.ring(1)], 16 * p.turn(1) + 16)
                    for t in range(NT):
                        last = dve.bn_stats(st1[:, t, :], xb[:, t, :])
                    ln.step(last, own_wait=True)
                    for t in range(NT):
                        last = dve.bn_aggr(mv1[:, t, :], st1[:, t, :])
                    ln.step(last)
                    dve.tensor_scalar(ve1[:], mv1[:, :, 1], LN_EPS, None, ALU.add).then_inc(ve1_ready, 1)
                    dve.wait_ge(rs1_ready, p.b + 2)
                    if p.n >= 0:
                        dve.wait_ge(xres_ready, p.b + 1)
                    for t in range(NT):
                        last = dve.tensor_scalar(r[:, t, :], xb[:, t, :], mv1[:, t, 0:1], rs1[:, t:t + 1],
                                                 ALU.subtract, ALU.mult)
                    last.then_inc(r_ready, 1)
                    dve.wait_ge(r_ready, p.b + 2)
                    for t in range(NT):
                        last = dve.bn_stats(st2[:, t, :], r[:, t, :])
                    ln.step(last, own_wait=True)
                    for t in range(NT):
                        last = dve.bn_aggr(mv2[:, t, :], st2[:, t, :])
                    ln.step(last)
                    dve.tensor_scalar(ve2[:], mv2[:, :, 1], LN_EPS, None, ALU.add).then_inc(ve2_ready, 1)

                def qkv_bias(p):
                    for t in range(NT):
                        dve.wait_ge(qkv_done, NT * (p.b + 1) + t + 1)
                        dve.tensor_tensor(qk[:, t, :, :].rearrange("p h d -> p (h d)"), pm[t][:, 0:2 * P], bqkv[:, 0:2 * P],
                                          ALU.add)
                        dve.tensor_tensor(v1[p.ring(1)][:, t, :, 0:HD],
                                          pm[t][:, 2 * P:3 * P].rearrange("p (h d) -> p h d", h=NH),
                                          bqkv[:, 2 * P:3 * P].rearrange("p (h d) -> p h d", h=NH),
                                          ALU.add).then_inc(qkv_ready, 1)

                def l2_norms(p):
                    norm.start(14 * (p.b + 1))
                    dve.wait_ge(qkv_ready, NT * (p.b + 2))
                    norm.step(dve.tensor_tensor(sq[:], qk[:], qk[:], ALU.mult))
                    norm.step(dve.tensor_reduce(ss[:], sq[:].rearrange("p t h d -> p (t h) d"), AX.X, ALU.add))
                    norm.step(dve.tensor_scalar(ss[:], ss[:], 1e-24, None, ALU.max))
                    norm.step(dve.tensor_scalar(na[:].bitcast(I32), ss[:].bitcast(I32), 1, None, ALU.logical_shift_right))
                    norm.step(dve.tensor_scalar(rn[:].bitcast(I32), na[:].bitcast(I32), -1.0, float(0x5F3759DF),
                                                ALU.mult, ALU.add))
                    for _ in range(3):
                        norm.step(dve.scalar_tensor_tensor(na[:], rn[:], -0.5, rn[:], ALU.mult, ALU.mult))
                        norm.step(dve.tensor_tensor(nb_[:], na[:], ss[:], ALU.mult))
                        norm.step(dve.scalar_tensor_tensor(rn[:], nb_[:], 1.5, rn[:], ALU.add, ALU.mult))
                    if p.n >= 0:
                        dve.wait_ge(q6_ready, p.b + 1)
                    dve.tensor_tensor(qk[:], qk[:], rn[:].rearrange("p (t h) -> p t h", t=NT).unsqueeze(3)
                                      .to_broadcast([P, NT, 2 * NH, HD]), ALU.mult).then_inc(qk_normed, 1)

                def normalise(chain, t, recip, s):
                    v = pm[t][:].rearrange("p (g j2 j1 c) -> p g j1 j2 c", g=NG, j2=2, j1=2)
                    rv = recip[:, t, :].rearrange("p (g j1 j2) -> p g j1 j2", g=NG, j1=2)
                    chain.step(dve.reciprocal(rv, v[:, :, :, :, HD]))
                    sv = s[:, t, :, :].rearrange("p (g j1 j2) d -> p g j1 j2 d", g=NG, j1=2)
                    for j1 in range(2):
                        last = dve.tensor_tensor(sv[:, :, j1], v[:, :, j1, :, 0:HD],
                                                 rv[:, :, j1, :].unsqueeze(3).to_broadcast([P, NG, 2, HD]), ALU.mult)
                    return last

                def state(p):
                    mid.start(7 * p.b)
                    for t in range(NT):
                        dve.wait_ge(otT_done, NT * p.b + t + 1)
                        if p.n >= 1 and t == 0:
                            dve.wait_ge(s6_ready, p.b)
                        normalise(mid, t, rec, s0).then_inc(s0_ready, 1)

                def maxima(p, d, units):
                    for n in units:
                        head = (n // 4) * 4 + 2 * (n % 4 % 2) + n % 4 // 2
                        dve.wait_ge(mxs_done, 16 * (p.b + d) + n + 1)
                        dve.tensor_reduce(mx[:, :, head], pm[n % 2][:].rearrange("p (t k) -> p t k", t=NT), AX.X,
                                          ALU.max).then_inc(mx_ready, 1)

                def shifts(p):
                    mid.start(7 * (p.b - 1) + 2)
                    dve.wait_ge(mx_ready, 16 * p.b)
                    mid.step(dve.scalar_tensor_tensor(mx[:], mx[:], -1.0, rec[:], ALU.mult, ALU.mult))
                    split3(dve, mid, mx[:], [s6[:, :, :, 48 + n] for n in range(3)], aug_ready)

                def s6T_copy(p):
                    for t in range(NT):
                        dve.wait_ge(s6T_done, NT * (p.b - 1) + t + 1)
                        dve.tensor_copy(sT[:, :, t * P:(t + 1) * P],
                                        pm[t][:].bitcast(BF16).rearrange("p (h q) -> p h q", h=NP)).then_inc(sT_ready, 1)

                def final_state(p):
                    fin.start(2 * (p.b - 2))
                    for t in range(NT):
                        dve.wait_ge(ot1T_done, NT * (p.b - 2) + t + 1)
                        normalise(fin, t, rec1, s1).then_inc(s1_ready, 1)

                def output(p):
                    u = p.ring(-2)
                    dve.wait_ge(wo_done, p.b - 1)
                    dve.wait_ge(xres_ready, p.b - 1)
                    if p.n - 2 >= RING:
                        dve.wait_ge(stored[u], 16 * p.turn(-2))
                    dve.tensor_tensor(y[u][:], pm[1][:, 0:NT * P].rearrange("p (t n) -> p t n", t=NT), xres[u][:],
                                      ALU.add).then_inc(y_ready, 1)

                def kT_copy(p):
                    for t in range(NT):
                        dve.wait_ge(k6T_done, NT * (p.b + 1) + t + 1)
                        dve.tensor_copy(kT[p.ring(1)][:, :, t * P:(t + 1) * P],
                                        pm[t][:].bitcast(BF16).rearrange("p (h q) -> p h q", h=NP)).then_inc(kT_ready, 1)

                def run(p):
                    if p.prepare:
                        layernorms(p)
                    if p.between:
                        maxima(p, -1, range(8, 16))
                        shifts(p)
                    if p.finish:
                        final_state(p)
                    if p.between:
                        s6T_copy(p)
                    if p.finish:
                        output(p)
                    if p.prepare:
                        qkv_bias(p)
                        l2_norms(p)
                    if p.first_step:
                        state(p)
                        maxima(p, 0, range(8))
                    if p.prepare:
                        kT_copy(p)

                each_pass(dve, run)
                p = Pass((NB + 1) // RING, (NB + 1) % RING)
                final_state(p)
                output(p)

            @block.scalar
            def _(act):
                def exp(loop, hp):
                    n = 8 * loop + hp
                    act.wait_ge(sim_done, n + 1)
                    if hp >= 4 or not isinstance(loop, int) or loop >= 1:
                        act.wait_ge(pv_done, 4 * loop + hp // 2 - 1)
                    act.activation(e[hp % 4][:].rearrange("p a t q -> p (a t q)"), px[hp % 2][:].rearrange("p a q -> p (a q)"),
                                   ACT.Exp).then_inc(exp_done, 1)

                def copy_ot(loop, g, step):
                    act.wait_ge(pv_done, 4 * loop + g + 1)
                    act.activation((ot0, ot1)[step][:, g, :], po[g % 2][:, 0:SEQ], ACT.Copy).then_inc(ot_copied, 1)

                def half(loop, step, exists, pend, pend_step, side):
                    for hp in range(NP):
                        if exists:
                            exp(loop, hp)
                        if hp == 0 and pend:
                            copy_ot(pend[0], 3, pend_step)
                        if hp % 2 == 0 and hp and exists:
                            if hp == 2 and step == 0:
                                side("ot0")
                            copy_ot(loop, hp // 2 - 1, step)
                        side(hp)

                def run(p):
                    def side0(at):
                        if at == "ot0" and not (isinstance(p.b, int) and p.b < 1):
                            act.wait_ge(otT_done, NT * p.b)
                            act.wait_ge(otb_ready, p.b)
                        if at == 7 and p.finish:
                            act.wait_ge(s1T_done, p.b - 1)
                            act.activation(s1T[:], pm[0][:, 0:SEQ], ACT.Copy).then_inc(s1T_ready, 1)

                    def side1(at):
                        if at == "ot0":
                            return
                        if at == 0 and p.prepare:
                            act.wait_ge(zT_done, p.b + 2)
                            act.activation(zT[:], pm[0][:, 0:SEQ], ACT.Copy).then_inc(zT_ready, 1)
                        if at == 7 and p.prepare:
                            for t in range(NT):
                                act.wait_ge(q6T_done, NT * (p.b + 1) + t + 1)
                                act.activation(qT[:, :, t * P:(t + 1) * P],
                                               pm[t][:].bitcast(BF16).rearrange("p (h q) -> p h q", h=NP),
                                               ACT.Copy).then_inc(qT_ready, 1)

                    if p.n >= 0:
                        half(p.loop0, 0, p.first_step, p.pend0, 1, side0)
                    half(p.loop1, 1, p.second_step, p.pend1, 0, side1)

                each_pass(act, run)
                copy_ot(2 * NB - 1, 3, 1)
                act.wait_ge(s1T_done, NB)
                act.activation(s1T[:], pm[0][:, 0:SEQ], ACT.Copy).then_inc(s1T_ready, 1)

            @block.tensor
            def _(pe):
                pe.wait_ge(consts, 16 * NCONST)
                pe.wait_ge(memsets, 2)

                def sims(loop, hp, qside, kside):
                    n = 8 * loop + hp
                    if hp >= 2 or not isinstance(loop, int) or loop >= 1:
                        pe.wait_ge(exp_done, n - 1)
                    for a in range(2):
                        rows = slice(64 * a, 64 * a + 64)
                        for t in range(NT):
                            last = pe.matmul(px[hp % 2][:, a, t * SEQ:(t + 1) * SEQ], kside[rows, hp, t * P:(t + 1) * P],
                                             qside[rows, hp, :], start=True, stop=True)
                    last.then_inc(sim_done, 1)

                def values(loop, g, v):
                    pe.wait_ge(exp_done, 8 * loop + 2 * g + 2)
                    if g >= 2 or not isinstance(loop, int) or loop >= 1:
                        pe.wait_ge(ot_copied, 4 * loop + g - 1)
                    for t in range(NT):
                        for j in range(4):
                            hp, a = 2 * g + j % 2, j // 2
                            last = pe.matmul(po[g % 2][32 * j:32 * j + 32, 0:SEQ], v[:, t, 2 * hp + a, :],
                                             e[hp % 4][:, a, t, :], start=(t == 0), stop=(t == NT - 1))
                    last.then_inc(pv_done, 1)

                def half(loop, exists, qside, kside, v, pend, side):
                    for hp in range(NP):
                        if exists:
                            sims(loop, hp, qside, kside)
                        if hp == 0 and pend:
                            values(pend[0], 3, v1[pend[1] % RING])
                        if hp % 2 == 0 and hp and exists:
                            values(loop, hp // 2 - 1, v)
                        side(hp)

                def ot_transposes(src, done, t):
                    for g in range(NG):
                        last = pe.transpose(pm[t][:, g * P:(g + 1) * P], src[:, g, t * P:(t + 1) * P], ident[:])
                    last.then_inc(done, 1)

                def transposes6(src, done, t):
                    for hp in range(NP):
                        last = pe.transpose(pm[t][:].bitcast(BF16)[:, hp * P:(hp + 1) * P],
                                            src[:, t, 2 * hp:2 * hp + 2, :].rearrange("p h c -> p (h c)"), ident_bf[:])
                    last.then_inc(done, 1)

                def maxima(p, d, units):
                    for n in units:
                        g, j = n // 4, n % 4
                        rows = slice(32 * j, 32 * j + HD)
                        if n >= 2:
                            pe.wait_ge(mx_ready, 16 * (p.b + d) + n - 1)
                        for t in range(NT):
                            last = pe.matmul(pm[n % 2][:, t * SEQ:(t + 1) * SEQ], otb[rows, g, t * P:(t + 1) * P],
                                             kT[p.ring(d)][rows, 2 * g + j % 2, :], start=True, stop=True)
                        last.then_inc(mxs_done, 1)

                def finish_a(p):
                    pe.wait_ge(ot_copied, 4 * p.pend0[0] + 4)
                    if p.between:
                        pe.wait_ge(mx_ready, 16 * p.b)
                    for t in range(NT):
                        ot_transposes(ot1, ot1T_done, t)

                def state_transposes(p):
                    pe.wait_ge(aug_ready, p.b)
                    pe.wait_ge(s6_ready, p.b)
                    if p.finish:
                        pe.wait_ge(s1_ready, NT * (p.b - 1))
                    for t in range(NT):
                        transposes6(s6, s6T_done, t)

                def finish_b(p):
                    pe.wait_ge(s1_ready, NT * (p.b - 1))
                    if p.between:
                        pe.wait_ge(sT_ready, NT * p.b)
                    for t in range(NT):
                        last = pe.transpose(pm[0][:, t * P:(t + 1) * P], s1[:, t, :, :].rearrange("p h d -> p (h d)"), ident[:])
                    last.then_inc(s1T_done, 1)
                    pe.wait_ge(s1T_ready, p.b - 1)
                    for t in range(NT):
                        last = pe.matmul(pm[1][:, t * P:(t + 1) * P], s1T[:, t * P:(t + 1) * P], wo[:], start=True, stop=True)
                    last.then_inc(wo_done, 1)

                def run(p):
                    def side0(at):
                        if p.between:
                            if 1 <= at <= 4:
                                maxima(p, -1, range(6 + 2 * at, 8 + 2 * at))
                        if at == 5 and p.finish:
                            finish_a(p)
                        if at == 6 and p.between:
                            state_transposes(p)
                        if at == 7 and p.finish:
                            finish_b(p)

                    def side1(at):
                        if p.prepare:
                            if at == 0:
                                pe.wait_ge(z_ready, p.b + 2)
                                if p.between:
                                    pe.wait_ge(sT_ready, NT * p.b)
                                for t in range(NT):
                                    last = pe.transpose(pm[0][:, t * P:(t + 1) * P], z[:, t, :], ident[:])
                                last.then_inc(zT_done, 1)
                            if at == 1:
                                pe.wait_ge(zT_ready, p.b + 2)
                                if p.finish:
                                    pe.wait_ge(y_ready, p.b - 1)
                                for t in range(NT):
                                    pe.matmul(pm[t][:, 0:3 * P], zT[:, t * P:(t + 1) * P], wqkv[:], start=True,
                                              stop=True).then_inc(qkv_done, 1)
                        if p.first_step:
                            if at == 2:
                                pe.wait_ge(ot_copied, 4 * p.loop0 + 4)
                                if p.prepare:
                                    pe.wait_ge(qkv_ready, NT * (p.b + 2))
                                elif p.finish:
                                    pe.wait_ge(y_ready, p.b - 1)
                                for t in range(NT):
                                    ot_transposes(ot0, otT_done, t)
                            if 3 <= at <= 6:
                                if at == 3:
                                    pe.wait_ge(s0_ready, NT * (p.b + 1))
                                    pe.wait_ge(otb_ready, p.b + 1)
                                maxima(p, 0, range(2 * at - 6, 2 * at - 4))
                        if at == 7 and p.prepare:
                            pe.wait_ge(k6_ready, p.b + 2)
                            if p.first_step:
                                pe.wait_ge(mx_ready, 16 * p.b + 8)
                            for t in range(NT):
                                transposes6(k6, k6T_done, t)
                            pe.wait_ge(q6_ready, p.b + 2)
                            pe.wait_ge(kT_ready, NT * (p.b + 2))
                            for t in range(NT):
                                transposes6(q6, q6T_done, t)
                            pe.wait_ge(qT_ready, NT * (p.b + 2))

                    if p.n >= 0:
                        half(p.loop0, p.first_step, qT, kT[p.ring(0)], v1[p.ring(0)], p.pend0, side0)
                    if p.second_step:
                        pe.wait_ge(sT_ready, NT * p.b)
                    half(p.loop1, p.second_step, sT, kT[p.ring(-1)], v1[p.ring(-1)], p.pend1, side1)

                each_pass(pe, run)
                values(2 * NB - 1, 3, v1[(NB - 1) % RING])
                pe.wait_ge(ot_copied, 4 * 2 * NB)
                pe.wait_ge(y_ready, NB - 1)
                for t in range(NT):
                    ot_transposes(ot1, ot1T_done, t)
                finish_b(Pass((NB + 1) // RING, (NB + 1) % RING))

            @block.gpsimd
            def _(pool):
                split, ssplit, zln, resc = (Chain(pool, s, pool_passed) for s in (split_c, ssplit_c, zln_c, res_c))
                pool.wait_ge(consts, 16 * NCONST)
                pool.wait_ge(memsets, 2)

                def roots(p):
                    pool.wait_ge(ve1_ready, p.b + 2)
                    pool.tensor_tensor(rs1[:], ve1[:], mhalf[:].to_broadcast([P, NT]), ALU.pow).then_inc(rs1_ready, 1)
                    pool.wait_ge(ve2_ready, p.b + 2)
                    pool.tensor_tensor(rs2[:], ve2[:], mhalf[:].to_broadcast([P, NT]), ALU.pow).then_inc(rs2_ready, 1)

                def wide(t):
                    return t[:].unsqueeze(1).to_broadcast([P, NT, P])

                def second_ln(p):
                    zln.start(2 * (p.b + 1))
                    resc.start(p.b + 1)
                    pool.wait_ge(rs2_ready, p.b + 2)
                    if p.n >= 0:
                        pool.wait_ge(zT_done, p.b + 1)
                    zln.own_wait()
                    for t in range(NT):
                        last = pool.tensor_scalar(z[:, t, :], r[:, t, :], mv2[:, t, 0:1], rs2[:, t:t + 1], ALU.subtract, ALU.mult)
                    zln.step(last)
                    zln.step(pool.tensor_tensor(z[:], z[:], wide(lnw), ALU.mult))
                    pool.tensor_tensor(z[:], z[:], wide(lnb), ALU.add).then_inc(z_ready, 1)
                    u = p.ring(1)
                    if p.n + 1 >= RING:
                        pool.wait_ge(y_ready, p.b + 2 - RING)
                    resc.step(pool.tensor_tensor(xres[u][:], x[u][:], wide(bo), ALU.add))
                    pool.tensor_tensor(xres[u][:], xres[u][:], r[:], ALU.add).then_inc(xres_ready, 1)

                def cut(chain, src, dst):
                    chain.step(pool.tensor_copy(dst[:, :, :, 0, :], src[:]))
                    chain.step(pool.tensor_tensor(src[:], src[:], dst[:, :, :, 0, :], ALU.subtract), own_wait=True)
                    chain.step(pool.tensor_copy(dst[:, :, :, 1, :], src[:]))
                    chain.step(pool.tensor_tensor(src[:], src[:], dst[:, :, :, 1, :], ALU.subtract), own_wait=True)
                    chain.step(pool.tensor_copy(dst[:, :, :, 2, :], src[:]), own_wait=True)

                def place_queries(dst, src):
                    for t in range(NT):
                        d = dst[:, t, :, 0:48].rearrange("p h (n d) -> p h n d", n=6)
                        pool.tensor_copy(d[:, :, 0:3, :], src[:, t, :, 0:1, :].to_broadcast([P, NH, 3, HD]))
                        pool.tensor_copy(d[:, :, 3:5, :], src[:, t, :, 1:2, :].to_broadcast([P, NH, 2, HD]))
                        last = pool.tensor_copy(d[:, :, 5, :], src[:, t, :, 2, :])
                    return last

                def place_keys(dst, src):
                    for t in range(NT):
                        d = dst[:, t, :, 0:48].rearrange("p h (n d) -> p h n d", n=6)
                        pool.tensor_copy(d[:, :, 0:3, :], src[:, t, :, :, :])
                        pool.tensor_copy(d[:, :, 3, :], src[:, t, :, 1, :])
                        last = pool.tensor_copy(d[:, :, 4:6, :], src[:, t, :, 0:1, :].to_broadcast([P, NH, 2, HD]))
                    return last

                def run(p):
                    if p.prepare:
                        roots(p)
                        second_ln(p)
                    if p.first_step:
                        pool.wait_ge(ot_copied, 4 * p.loop0 + 4)
                        if p.n >= 1:
                            pool.wait_ge(mxs_done, 16 * p.b)
                        zln.own_wait()
                        pool.tensor_copy(otb[:], ot0[:]).then_inc(otb_ready, 1)
                    if p.prepare:
                        split.start(5 * (p.b + 1))
                        pool.wait_ge(qk_normed, p.b + 2)
                        zln.own_wait()
                        cut(split, qk, parts)
                        if p.n >= 0:
                            pool.wait_ge(k6T_done, NT * (p.b + 1))
                        zln.own_wait()
                        place_keys(k6, parts[:, :, NH:, :, :]).then_inc(k6_ready, 1)
                        if p.n >= 0:
                            pool.wait_ge(q6T_done, NT * (p.b + 1))
                        zln.own_wait()
                        place_queries(q6, parts[:, :, 0:NH, :, :]).then_inc(q6_ready, 1)
                    if p.first_step:
                        pool.wait_ge(s0_ready, NT * (p.b + 1))
                        zln.own_wait()
                        ssplit.start(5 * p.b)
                        cut(ssplit, s0, sparts)
                        if p.n >= 1:
                            pool.wait_ge(s6T_done, NT * p.b)
                        zln.own_wait()
                        place_queries(s6, sparts).then_inc(s6_ready, 1)

                each_pass(pool, run)



def program(nc, T, out):
    stages = [nc.dram_tensor(f"stage{n}", [TOK, P], F32, kind="Internal").ap() for n in range(3)]
    recurrent_mixer(nc, T, T["L0_attn_x"].rearrange("b s d -> (b s) d"), stages[0])
    expert_mixture(nc, T, stages[0], stages[1], 0)
    hopfield_mixer(nc, T, stages[1], stages[2])
    expert_mixture(nc, T, stages[2], out.rearrange("b s d -> (b s) d"), 1)


def _tables():
    import numpy as np
    eye = np.eye(128, dtype=np.float32)
    headsel = np.zeros((128, 32), np.float32)
    headsel[:64, 0] = 1
    headsel[64:, 1] = 1
    sel3 = np.zeros((32, 4, 128), np.float32)
    for part in range(3):
        for c in range(4):
            for r in range(2):
                sel3[8 * part + 2 * c + r, c, 64 * r:64 * r + 64] = 1
    bits = lambda t: np.where(t != 0, 0x3F80, 0).astype(np.uint16)
    return {"ident": eye, "ident_bf": bits(eye), "headsel": headsel, "sel3": bits(sel3),
            "m_iota": np.arange(128, dtype=np.float32), "m_before": bits(np.triu(np.ones((128, 128)), 1))}


def _layout(inputs):
    import numpy as np
    arrays = {k: np.ascontiguousarray(v) for k, v in inputs.items()}
    by_channel = lambda v: np.asarray(v).reshape(4, 128).T
    arrays["a_cols"] = np.ascontiguousarray(np.stack(
        [by_channel(arrays[f"L0_attn_{n}"]) for n in ("bq", "bk", "bv", "alpha", "aug_param")], axis=1))
    arrays["c_bqkv"] = np.concatenate([arrays[f"L1_attn_b{n}"] for n in "qkv"])
    arrays["m_gate"] = np.ascontiguousarray(arrays["L0_ffn_gate_w"].T)
    arrays["m_b1"] = np.ascontiguousarray(arrays["L0_ffn_b1"].reshape(8, 4, 128).transpose(2, 0, 1).reshape(128, 32))
    arrays["m_w2"] = np.ascontiguousarray(
        arrays["L0_ffn_W2"].reshape(8, 4, 128, 128).transpose(2, 0, 1, 3).reshape(128, 32 * 128))
    arrays["m_sb1"] = np.ascontiguousarray(by_channel(arrays["L0_ffn_sb1"]))
    arrays["m_router"] = np.concatenate([arrays[f"L1_ffn_router_w{g}"] for g in range(2)], axis=1)
    arrays["m_wgu"] = np.ascontiguousarray(np.concatenate(
        [np.concatenate([arrays[f"L1_ffn_wg{g}"], arrays[f"L1_ffn_wu{g}"]], axis=2) for g in range(2)], axis=0
    ).transpose(1, 0, 2).reshape(128, 64 * 128))
    arrays["m_wd"] = np.ascontiguousarray(np.concatenate(
        [arrays[f"L1_ffn_wd{g}"] for g in range(2)], axis=0).transpose(1, 0, 2).reshape(64, 64 * 128))
    arrays.update(_tables())
    return arrays


def kernel(**inputs):
    import concourse.bacc as bacc
    from concourse.bass_utils import run_bass_kernel_spmd

    nc = bacc.Bacc("TRN2", target_bir_lowering=False, num_devices=1)
    arrays, T = {}, {}
    for name, a in _layout(inputs).items():
        arrays[f"in_{name}"] = a
        T[name] = nc.dram_tensor(f"in_{name}", a.shape, mybir.dt.from_np(a.dtype), kind="ExternalInput").ap()
    out = nc.dram_tensor("out", [16, SEQ, P], F32, kind="ExternalOutput").ap()
    program(nc, T, out)
    return run_bass_kernel_spmd(nc, [arrays], core_ids=[0]).results[0]["out"]
```

```python
from contextlib import ExitStack

import concourse.bass as bass
from concourse import mybir

F32 = mybir.dt.float32
BF16 = mybir.dt.bfloat16
I32 = mybir.dt.int32
U32 = mybir.dt.uint32
ALU = mybir.AluOpType
ACT = mybir.ActivationFunctionType
AX = mybir.AxisListType

P = 128
TOK = 4096
SEQ = 256
SUP = 512
LN_EPS = 1e-5
LN0_EPS = 1e-6


class Chain:

    def __init__(self, eng, sem, passed=None):
        self.eng, self.sem, self.base, self.n, self.passed = eng, sem, 0, 0, passed

    def start(self, base):
        self.base, self.n = base, 0

    def own_wait(self):
        self.eng.sem_inc(self.passed, 1)

    def step(self, ins, own_wait=False):
        self.n += 1
        ins.then_inc(self.sem, 1)
        self.eng.wait_ge(self.sem, self.base + self.n)
        if own_wait:
            self.own_wait()


class Scope:

    def __init__(self, nc, tag):
        self.nc, self.tag, self.ctx, self.sems = nc, tag, ExitStack(), []

    def __enter__(self):
        return self

    def __exit__(self, *e):
        with self.nc.Block() as block:
            @block.sync
            def _(sp):
                for s in self.sems[0::3]:
                    sp.sem_clear(s)

            @block.scalar
            def _(act):
                for s in self.sems[1::3]:
                    act.sem_clear(s)

            @block.tensor
            def _(pe):
                for s in self.sems[2::3]:
                    pe.sem_clear(s)
        return self.ctx.__exit__(*e)

    def sb(self, name, shape, dt=F32):
        return self.ctx.enter_context(self.nc.sbuf_tensor(f"{self.tag}_{name}", shape, dt))

    def ps(self, name, shape, dt=F32):
        return self.ctx.enter_context(self.nc.psum_tensor(f"{self.tag}_{name}", shape, dt))

    def sem(self, name):
        s = self.ctx.enter_context(self.nc.semaphore(f"{self.tag}_{name}"))
        self.sems.append(s)
        return s



def recurrent_mixer(nc, T, x_in, x_out, clear=()):
    NS = TOK // SUP
    NT = SUP // P
    NC = 4
    with Scope(nc, "a") as S:
        sb, ps, sem = S.sb, S.ps, S.sem
        wq, wk, wv = sb("wq", [P, 512]), sb("wk", [P, 512]), sb("wv", [P, 512])
        wo, wo_h = sb("wo", [P, NC, P]), sb("wo_h", [P, NC, P])
        cols = sb("cols", [P, 5, NC])
        rows = sb("rows", [1, P])
        lns, lnb = sb("lns", [P, P]), sb("lnb", [P, P])
        ident, headsel = sb("ident", [P, P]), sb("headsel", [P, 32])
        ident_bf = sb("ident_bf", [P, P], BF16)
        sel3 = sb("sel3", [32, NC, P], BF16)
        halves, one_row = sb("halves", [P, P]), sb("one_row", [1, P])
        mhalf = sb("mhalf", [P, 1])
        decay, omd = sb("decay", [P, NC]), sb("omd", [P, NC])
        th_a, bvs = sb("th_a", [P, NC]), sb("bvs", [P, NC])
        augh, augb = sb("augh", [P, NC]), sb("augb", [P, NC])
        bo_b = sb("bo_b", [P, P])
        zero = sb("zero", [P, 1024])

        x = [sb(f"x{u}", [P, NT, P]) for u in range(2)]
        xres = [sb(f"xres{u}", [P, NT, P]) for u in range(2)]
        xn, xnT = sb("xn", [P, NT, P]), sb("xnT", [P, SUP])
        bst, mv = sb("bst", [P, NT, 6]), sb("mv", [P, NT, 2])
        veps, rstd = sb("veps", [P, NT]), sb("rstd", [P, NT])
        qT = [sb(f"qT{u}", [P, NC, SUP]) for u in range(2)]
        th = [sb(f"th{u}", [P, NC, SUP]) for u in range(2)]
        vT = [sb(f"vT{u}", [P, NC, SUP]) for u in range(2)]
        qk = sb("qk", [P, NC, SUP])
        st, g = sb("st", [P, NC, SUP]), sb("g", [P, NC, SUP])
        sc = sb("sc", [P, SUP])
        mx, e8, sm, r8 = sb("mx", [P, NT]), sb("e8", [P, NT, 8]), sb("sm", [P, NT]), sb("r8", [P, NT])
        res = sb("res", [P, NT, 8])
        a3 = sb("a3", [P, NT, 32], BF16)
        a3T = sb("a3T", [32, SUP], BF16)
        o = sb("o", [P, NT, P])
        obst, omv = sb("obst", [P, NT, 6]), sb("omv", [P, NT, 2])
        oveps, orstd = sb("oveps", [P, NT]), sb("orstd", [P, NT])
        y = [sb(f"y{u}", [P, NT, P]) for u in range(2)]

        pT = ps("pT", [P, SUP])
        pP = [ps(f"pP{n}", [P, SUP]) for n in range(4)]
        pS = ps("pS", [P, SUP])
        pA = ps("pA", [P, SUP])
        pA3 = ps("pA3", [P, 2 * SUP], BF16)

        consts = sem("consts")
        x_loaded = [sem(f"x_loaded{u}") for u in range(2)]
        stored = [sem(f"stored{u}") for u in range(2)]
        cleared = sem("cleared")
        memsets, coef_act, coef_dve = sem("memsets"), sem("coef_act"), sem("coef_dve")
        bo_done = sem("bo_done")
        dve_passed, pool_passed = sem("dve_passed"), sem("pool_passed")
        set_c, in_c, out_c, dve_c, pool_c = (sem(x) for x in ("set_c", "in_c", "out_c", "dve_c", "pool_c"))
        veps_ready, rstd_ready, xn_ready = sem("veps_ready"), sem("rstd_ready"), sem("xn_ready")
        xT_done, xnT_ready = sem("xT_done"), sem("xnT_ready")
        proj_done = sem("proj_done")
        q_ready, tanh_ready, v_ready = sem("q_ready"), sem("tanh_ready"), sem("v_ready")
        qk_ready = sem("qk_ready")
        sc_done, sc_copied, scT_done = sem("sc_done"), sem("sc_copied"), sem("scT_done")
        e_shifted, e_done, a3_ready = sem("e_shifted"), sem("e_done"), sem("a3_ready")
        a3T_done, a3T_copied, bc_done = sem("a3T_done"), sem("a3T_copied"), sem("bc_done")
        u_ready, st_ready, g_ready = sem("u_ready"), sem("st_ready"), sem("g_ready")
        wo_done, o_copied = sem("wo_done"), sem("o_copied")
        oveps_ready, orstd_ready = sem("oveps_ready"), sem("orstd_ready")
        xres_ready, y_ready = sem("xres_ready"), sem("y_ready")

        xv = x_in.rearrange("(s t p) d -> s p t d", t=NT, p=P)
        ov = x_out.rearrange("(s t p) d -> s p t d", t=NT, p=P)
        NCONST = 12

        def each_step(eng, step):
            step(0, 0, first=True)
            step(0, 1)
            step(0, 2)
            with eng.Fori(0, (NS - 4) // 2) as i:
                step(i, 3)
                step(i, 4)
            step((NS - 4) // 2, 3, last=True)

        with nc.Block() as block:
            @block.sync
            def _(sp):
                sp.dma_start(x[0][:], xv[0]).then_inc(x_loaded[0], 16)
                for dst, src in ((ident, T["ident"]), (ident_bf, T["ident_bf"].bitcast(BF16)), (wq, T["L0_attn_Wq"]), (wk, T["L0_attn_Wk"]), (wv, T["L0_attn_Wv"]),
                                 (cols, T["a_cols"]), (headsel, T["headsel"]), (sel3, T["sel3"].bitcast(BF16)),
                                 (wo, T["L0_attn_Wo"].rearrange("(c p) n -> p c n", p=P)),
                                 (rows, T["L0_attn_bo"].rearrange("(a n) -> a n", a=1)),
                                 (lns, T["L0_attn_ln_scale"].partition_broadcast(P)),
                                 (lnb, T["L0_attn_ln_bias"].partition_broadcast(P))):
                    sp.dma_start(dst[:], src).then_inc(consts, 16)

                def step(i, r, first=False, last=False):
                    s, u = 2 * i + r, r % 2
                    if not last:
                        if not first:
                            sp.wait_ge(xres_ready, s)
                        sp.dma_start(x[1 - u][:], xv[s + 1]).then_inc(x_loaded[1 - u], 16)
                    if not first:
                        store(s - 1, 1 - u)

                def store(s, u):
                    sp.wait_ge(y_ready, s + 1)
                    sp.dma_start(ov[s], y[u][:]).then_inc(stored[u], 16)

                each_step(sp, step)
                store(NS - 1, 1)
                for u in range(2):
                    sp.wait_ge(stored[u], 16 * NS // 2)

            @block.vector
            def _(dve):
                ch_set, ch, ch_in, ch_out = (Chain(dve, x, dve_passed) for x in (set_c, dve_c, in_c, out_c))
                dve.memset(halves[:], 0.5)
                dve.memset(one_row[:], 1.0)
                dve.memset(zero[:], 0.0)
                dve.memset(mhalf[:], -0.5)
                dve.memset(a3[:], 0.0).then_inc(memsets, 1)
                dve.wait_ge(coef_act, 1)
                dve.tensor_scalar(decay[:], th_a[:], 0.5, 0.5, ALU.mult, ALU.add)
                ch_set.step(dve.tensor_scalar(omd[:], th_a[:], -1.0, 1.0, ALU.mult, ALU.add))
                dve.tensor_tensor(bvs[:], omd[:], cols[:, 2, :], ALU.mult)
                ch_set.step(dve.tensor_scalar(augh[:], cols[:, 4, :], 0.5, None, ALU.mult))
                dve.tensor_tensor(augb[:], augh[:], cols[:, 0, :], ALU.mult).then_inc(coef_dve, 1)
                dve.tensor_scalar(wo_h[:], wo[:], 0.5, None, ALU.mult)
                dve.wait_ge(bo_done, 1)
                dve.tensor_copy(bo_b[:], pS[:, 0:P]).then_inc(coef_dve, 1)
                dve.wait_ge(coef_dve, 2)

                def layernorm_in(i, r, first=False):
                    s, u = 2 * i + r, r % 2
                    ch_in.start(2 * s)
                    dve.wait_ge(x_loaded[u], 16 * (i + r // 2) + 16)
                    for t in range(NT):
                        last = dve.bn_stats(bst[:, t, :], x[u][:, t, :])
                    ch_in.step(last, own_wait=True)
                    for t in range(NT):
                        last = dve.bn_aggr(mv[:, t, :], bst[:, t, :])
                    ch_in.step(last)
                    dve.tensor_scalar(veps[:], mv[:, :, 1], LN_EPS, None, ALU.add).then_inc(veps_ready, 1)
                    dve.wait_ge(rstd_ready, s + 1)
                    if not first:
                        dve.wait_ge(xT_done, s)
                    for t in range(NT):
                        last = dve.tensor_scalar(xn[:, t, :], x[u][:, t, :], mv[:, t, 0:1], rstd[:, t:t + 1],
                                                 ALU.subtract, ALU.mult)
                    last.then_inc(xn_ready, 1)

                def layernorm_out(i, r):
                    s, u = 2 * i + r, r % 2
                    ch_out.start(4 * s)
                    dve.wait_ge(wo_done, s + 1)
                    dve.tensor_tensor(o[:], pS[:].rearrange("p (t n) -> p t n", t=NT),
                                      bo_b[:].unsqueeze(1).to_broadcast([P, NT, P]), ALU.add).then_inc(o_copied, 1)
                    dve.wait_ge(o_copied, s + 1)
                    for t in range(NT):
                        last = dve.bn_stats(obst[:, t, :], o[:, t, :])
                    ch_out.step(last, own_wait=True)
                    for t in range(NT):
                        last = dve.bn_aggr(omv[:, t, :], obst[:, t, :])
                    ch_out.step(last)
                    dve.tensor_scalar(oveps[:], omv[:, :, 1], LN0_EPS, None, ALU.add).then_inc(oveps_ready, 1)
                    dve.wait_ge(orstd_ready, s + 1)
                    for t in range(NT):
                        last = dve.tensor_scalar(o[:, t, :], o[:, t, :], omv[:, t, 0:1], orstd[:, t:t + 1],
                                                 ALU.subtract, ALU.mult)
                    ch_out.step(last)
                    ch_out.step(dve.tensor_tensor(o[:], o[:], lns[:].unsqueeze(1).to_broadcast([P, NT, P]), ALU.mult))
                    dve.wait_ge(xres_ready, s + 1)
                    if r >= 2:
                        dve.wait_ge(stored[u], 16 * (i + r // 2))
                    dve.tensor_tensor(y[u][:], o[:], xres[u][:], ALU.add).then_inc(y_ready, 1)

                def step(i, r, first=False, last=False):
                    s, u = 2 * i + r, r % 2
                    if not last:
                        layernorm_in(i, r + 1)
                    for c in range(NC):
                        dve.wait_ge(proj_done, 12 * s + 3 * c + 2)
                        dve.wait_ge(q_ready, NC * s + c + 1)
                        if c == 0 and not first:
                            dve.wait_ge(sc_done, s)
                        dve.scalar_tensor_tensor(qk[:, c, :], pP[(3 * c + 1) % 4][:], cols[:, 1, c:c + 1], qT[u][:, c, :],
                                                 ALU.add, ALU.mult).then_inc(qk_ready, 1)
                    if not first:
                        layernorm_out(i, r - 1)
                    ch.start(8 * s)
                    dve.wait_ge(scT_done, s + 1)
                    scv = pA[:].rearrange("p (t c r) -> p t c r", t=NT, c=NC)[:, :, :, 0:2]
                    e4 = e8[:].rearrange("p t (c r) -> p t c r", r=2)
                    ch.step(dve.tensor_reduce(mx[:], scv, AX.XY, ALU.max))
                    dve.tensor_tensor(e4, scv, mx[:].unsqueeze(2).unsqueeze(3).to_broadcast([P, NT, NC, 2]),
                                      ALU.subtract).then_inc(e_shifted, 1)
                    dve.wait_ge(e_done, s + 1)
                    ch.step(dve.tensor_reduce(sm[:], e8[:], AX.X, ALU.add))
                    ch.step(dve.reciprocal(r8[:], sm[:]))
                    ch.step(dve.tensor_tensor(res[:], e8[:], r8[:].unsqueeze(2).to_broadcast([P, NT, 8]), ALU.mult))
                    if not first:
                        dve.wait_ge(a3T_done, s)
                    split3(dve, ch, res[:], [a3[:, :, 8 * k:8 * k + 8] for k in range(3)], a3_ready)
                    for c in range(NC):
                        dve.wait_ge(bc_done, NC * s + c + 1)
                        dve.wait_ge(v_ready, NC * s + c + 1)
                        dve.tensor_tensor(vT[u][:, c, :], pP[c][:], vT[u][:, c, :], ALU.mult).then_inc(u_ready, 1)
                    for c in range(NC):
                        dve.wait_ge(u_ready, NC * s + c + 1)
                        if not first:
                            dve.wait_ge(g_ready, NC * (s - 1) + c + 1)
                        for b in range(2):
                            w = slice(b * SEQ, (b + 1) * SEQ)
                            last_i = dve.tensor_tensor_scan(st[:, c, w], decay[:, c:c + 1].to_broadcast([P, SEQ]),
                                                            vT[u][:, c, w], 0.0, ALU.mult, ALU.add)
                        last_i.then_inc(st_ready, 1)

                layernorm_in(0, 0, first=True)
                each_step(dve, step)
                layernorm_out(0, NS - 1)

            @block.scalar
            def _(act):
                act.wait_ge(consts, 16 * NCONST)
                act.activation(th_a[:], cols[:, 3, :], ACT.Tanh, scale=0.5).then_inc(coef_act, 1)
                act.wait_ge(memsets, 1)
                for t in clear:
                    act.dma_start(t.rearrange("(p n) d -> p (n d)", p=P).rearrange("p (n c) -> p n c", c=1024),
                                  zero[:].unsqueeze(1).to_broadcast([P, t.shape[0] * P // P // 1024, 1024])
                                  ).then_inc(cleared, 16)
                act.wait_ge(coef_dve, 1)

                def copy_xnT(s, first=False):
                    act.wait_ge(xT_done, s + 1)
                    act.activation(xnT[:], pT[:], ACT.Copy).then_inc(xnT_ready, 1)

                def step(i, r, first=False, last=False):
                    s, u = 2 * i + r, r % 2
                    for c in range(NC):
                        act.wait_ge(proj_done, 12 * s + 3 * c + 1)
                        q_ps = pP[(3 * c) % 4]
                        if c == 0 and r >= 2:
                            act.wait_ge(g_ready, NC * (s - 1))
                        act.activation(qT[u][:, c, :], q_ps[:], ACT.Identity, bias=cols[:, 0, c:c + 1]).then_inc(q_ready, 1)
                        act.activation(th[u][:, c, :], q_ps[:], ACT.Tanh, scale=augh[:, c:c + 1],
                                       bias=augb[:, c:c + 1]).then_inc(tanh_ready, 1)
                        act.wait_ge(proj_done, 12 * s + 3 * c + 3)
                        act.activation(vT[u][:, c, :], pP[(3 * c + 2) % 4][:], ACT.Identity, scale=omd[:, c:c + 1],
                                       bias=bvs[:, c:c + 1]).then_inc(v_ready, 1)
                    act.wait_ge(sc_done, s + 1)
                    act.activation(sc[:], pS[:], ACT.Copy).then_inc(sc_copied, 1)
                    if not last:
                        copy_xnT(s + 1)
                    act.wait_ge(e_shifted, s + 1)
                    act.activation(e8[:], e8[:], ACT.Exp, scale=0.125).then_inc(e_done, 1)
                    act.wait_ge(a3T_done, s + 1)
                    act.activation(a3T[:], pA3[0:32, 0:SUP], ACT.Copy).then_inc(a3T_copied, 1)

                copy_xnT(0)
                each_step(act, step)
                if clear:
                    act.wait_ge(cleared, 16 * len(clear))

            @block.tensor
            def _(pe):
                pe.wait_ge(consts, 16 * NCONST)
                pe.wait_ge(memsets, 1)
                for c in range(NC):
                    pe.matmul(pS[:, 0:P], halves[:], wo[:, c, :], start=(c == 0), stop=False)
                pe.matmul(pS[:, 0:P], one_row[:], rows[:], start=False, stop=True).then_inc(bo_done, 1)

                def transpose_x(s, first=False):
                    pe.wait_ge(xn_ready, s + 1)
                    if not first:
                        pe.wait_ge(xnT_ready, s)
                    for t in range(NT):
                        last = pe.transpose(pT[:, t * P:(t + 1) * P], xn[:, t, :], ident[:])
                    last.then_inc(xT_done, 1)

                def out_proj(s):
                    pe.wait_ge(g_ready, NC * s + NC)
                    for t in range(NT):
                        for c in range(NC):
                            last = pe.matmul(pS[:, t * P:(t + 1) * P], g[:, c, t * P:(t + 1) * P], wo_h[:, c, :],
                                             start=(c == 0), stop=(c == NC - 1))
                    last.then_inc(wo_done, 1)

                def step(i, r, first=False, last=False):
                    s, u = 2 * i + r, r % 2
                    pe.wait_ge(xnT_ready, s + 1)
                    for c in range(NC):
                        for j, w in enumerate((wq, wk, wv)):
                            n = 3 * c + j
                            m = n - 4
                            if m >= 0:
                                pe.wait_ge((tanh_ready, qk_ready, v_ready)[m % 3], NC * s + m // 3 + 1)
                            elif not first:
                                pe.wait_ge(u_ready, NC * (s - 1) + n + 1)
                            pe.matmul(pP[n % 4][:], w[:, c * P:(c + 1) * P], xnT[:], start=True, stop=True).then_inc(proj_done, 1)
                    if not last:
                        transpose_x(s + 1)
                    if first:
                        pe.wait_ge(coef_dve, 2)
                    if r >= 2:
                        pe.wait_ge(o_copied, s - 1)
                    for c in range(NC):
                        pe.wait_ge(qk_ready, NC * s + c + 1)
                        last_i = pe.matmul(pS[32 * c:32 * c + 32, :], headsel[:], qk[:, c, :], start=True, stop=True)
                    last_i.then_inc(sc_done, 1)
                    pe.wait_ge(sc_copied, s + 1)
                    if not first:
                        pe.wait_ge(e_shifted, s)
                    for t in range(NT):
                        last_i = pe.transpose(pA[:, t * P:(t + 1) * P], sc[:, t * P:(t + 1) * P], ident[:])
                    last_i.then_inc(scT_done, 1)
                    if not first:
                        out_proj(s - 1)
                    pe.wait_ge(a3_ready, s + 1)
                    if not first:
                        pe.wait_ge(a3T_copied, s)
                    for t in range(NT):
                        last_i = pe.transpose(pA3[0:32, t * P:(t + 1) * P], a3[:, t, :], ident_bf[:])
                    last_i.then_inc(a3T_done, 1)
                    pe.wait_ge(a3T_copied, s + 1)
                    for c in range(NC):
                        m = 12 + c - 4
                        pe.wait_ge((tanh_ready, qk_ready, v_ready)[m % 3], NC * s + m // 3 + 1)
                        pe.matmul(pP[c][:], sel3[:, c, :], a3T[:], start=True, stop=True).then_inc(bc_done, 1)

                transpose_x(0, first=True)
                each_step(pe, step)
                pe.wait_ge(sc_copied, NS)
                out_proj(NS - 1)

            @block.gpsimd
            def _(pool):
                ch = Chain(pool, pool_c, pool_passed)
                pool.wait_ge(memsets, 1)

                def rsqrt_in(s):
                    pool.wait_ge(veps_ready, s + 1)
                    pool.tensor_tensor(rstd[:], veps[:], mhalf[:].to_broadcast([P, NT]), ALU.pow).then_inc(rstd_ready, 1)

                def rsqrt_out(s):
                    pool.wait_ge(oveps_ready, s + 1)
                    pool.tensor_tensor(orstd[:], oveps[:], mhalf[:].to_broadcast([P, NT]), ALU.pow).then_inc(orstd_ready, 1)

                def residual(i, r):
                    s, u = 2 * i + r, r % 2
                    pool.wait_ge(x_loaded[u], 16 * (i + r // 2) + 16)
                    if r >= 2:
                        pool.wait_ge(y_ready, s - 1)
                    pool.tensor_tensor(xres[u][:], x[u][:], lnb[:].unsqueeze(1).to_broadcast([P, NT, P]),
                                       ALU.add).then_inc(xres_ready, 1)

                def gate(s, u, first=False):
                    for c in range(NC):
                        pool.wait_ge(st_ready, NC * s + c + 1)
                        ch.start(NC * s)
                        ch.n = c
                        pool.wait_ge(tanh_ready, NC * s + c + 1)
                        ch.step(pool.tensor_tensor(qT[u][:, c, :], qT[u][:, c, :], st[:, c, :], ALU.mult))
                        if not first:
                            pool.wait_ge(wo_done, s)
                        pool.tensor_tensor(g[:, c, :], th[u][:, c, :], qT[u][:, c, :], ALU.add).then_inc(g_ready, 1)

                def step(i, r, first=False, last=False):
                    s, u = 2 * i + r, r % 2
                    if not last:
                        rsqrt_in(s + 1)
                    residual(i, r)
                    if not first:
                        rsqrt_out(s - 1)
                    gate(s, u, first)

                pool.wait_ge(consts, 16 * NCONST)
                rsqrt_in(0)
                each_step(pool, step)
                rsqrt_out(NS - 1)


def split3(dve, ch, res, parts, ready):
    ch.step(dve.tensor_copy(parts[0], res))
    ch.step(dve.tensor_tensor(res, res, parts[0], ALU.subtract))
    ch.step(dve.tensor_copy(parts[1], res))
    ch.step(dve.tensor_tensor(res, res, parts[1], ALU.subtract))
    dve.tensor_copy(parts[2], res).then_inc(ready, 1)



NT = SUP // P
NS = TOK // SUP
TOPK = 2
QUAD = 4


def span(eng, lo, hi, fn, least=2):
    q = lo
    while q < hi and (q < least or q % 2):
        fn(q, q % 2, q // 2)
        q += 1
    pairs = (hi - q) // 2
    if pairs > 1:
        with eng.Fori(0, pairs) as i:
            fn(2 * i + q, 0, i + q // 2)
            fn(2 * i + q + 1, 1, i + q // 2)
        q += 2 * pairs
    for q in range(q, hi):
        fn(q, q % 2, q // 2)


def from_step(q, n):
    return not isinstance(q, int) or q >= n


MIXTURES = ((1, 8), (2, 32))


def blocks_of(layer):
    return -(-(TOPK * TOK + MIXTURES[layer][1] * (P - 1)) // P // QUAD) * QUAD


def row_space(nc, layer):
    return [nc.dram_tensor(f"rows{g}_layer{layer}", [blocks_of(layer) * P, P], F32, kind="Internal").ap()
            for g in range(MIXTURES[layer][0])]


def expert_mixture(nc, T, x_in, x_out, xg, layer):
    G, E = MIXTURES[layer]
    GE = G * E
    NBLK = blocks_of(layer)
    NQG = NBLK // QUAD
    NQ = G * NQG
    TE = NS * NT * E
    new = lambda name, rows: nc.dram_tensor(f"{name}_layer{layer}", [rows, P], F32, kind="Internal").ap()
    yg = [new(f"results{g}", NBLK * P) for g in range(G)]
    xn_d = new("normed", TOK)
    with Scope(nc, "bd"[layer]) as S:
        sb, ps, sem = S.sb, S.ps, S.sem
        ident = sb("ident", [P, P])
        mhalf = sb("mhalf", [P, 1])
        bank = [ps(f"bank{n}", [P, 512]) for n in range(8)]

        best = sb("best", [P, G, NS, TOPK, NT])
        pick = sb("pick", [P, G, NS, TOPK, NT])
        wgt = sb("wgt", [P, G, NS, TOPK, NT])
        dest = sb("dest", [P, G, NS, TOPK, NT], U32)
        total = sb("total", [P, NS, G, NT])
        owner = sb("owner", [1, G * NBLK], I32)

        xnT_all = sb("xnT_all", [P, TOK]) if layer == 0 else None

        router = sb("router", [P, GE])
        if layer == 0:
            w1, w2 = sb("w1", [P, E * 512]), sb("w2", [P, E * 4 * P])
            b1, b2 = sb("b1", [P, E * 4]), sb("b2", [P, E * P])
            sw1, sw2 = sb("sw1", [P, 512]), sb("sw2", [P, 4, P])
            sb1, sb2 = sb("sb1", [P, 4]), sb("sb2", [P, P])
            expert_weights = [(w1, T["L0_ffn_W1"].rearrange("e p f -> p e f")), (w2, T["m_w2"]), (b1, T["m_b1"]),
                              (b2, T["L0_ffn_b2"].rearrange("e h -> (e h)").partition_broadcast(P))]
            loads = [(router, T["m_gate"]),
                     (sw1, T["L0_ffn_sW1"]), (sw2, T["L0_ffn_sW2"].rearrange("(c p) h -> p c h", p=P)),
                     (sb1, T["m_sb1"]), (sb2, T["L0_ffn_sb2"].partition_broadcast(P))]
        else:
            wgu, wd = sb("wgu", [P, GE * P]), sb("wd", [64, GE * P])
            expert_weights = [(wgu, T["m_wgu"]), (wd, T["m_wd"])]
            loads = [(router, T["m_router"])]
        iota, before = sb("iota", [P, P]), sb("before", [P, P], BF16)
        loads += [(iota, T["m_iota"].partition_broadcast(P)), (before, T["m_before"].bitcast(BF16))]

        consts = sem("consts")
        weights = sem("weights")
        memset = sem("memset")
        dve_passed, pool_passed = sem("dve_passed"), sem("pool_passed")
        x_loaded = [sem(f"x_loaded{u}") for u in range(2)]
        normed_stored = [sem(f"normed_stored{u}") for u in range(2)]

        with Scope(nc, "bd"[layer] + "r") as R:
            x = [R.sb(f"x{u}", [P, NT, P]) for u in range(2)]
            xn = [R.sb(f"xn{u}", [P, NT, P]) for u in range(2)]
            bst, mv = R.sb("bst", [P, NT, 6]), R.sb("mv", [P, NT, 2])
            veps, rstd = R.sb("veps", [P, NT]), R.sb("rstd", [P, NT])
            xnT = [R.sb(f"xnT{u}", [P, SUP]) for u in range(2)]
            lg, ex = R.sb("lg", [P, NT, G, E]), R.sb("ex", [P, NT, G, E])
            m8, i8 = R.sb("m8", [P, G, NT, 8]), R.sb("i8", [P, G, NT, 8], U32)
            sm = R.sb("sm", [P, G, NT])
            pT, pL = bank[0], bank[1]
            ln_c, top_c = R.sem("ln_c"), R.sem("top_c")
            veps_ready, rstd_ready, xn_ready = R.sem("veps_ready"), R.sem("rstd_ready"), R.sem("xn_ready")
            xT_done, xnT_ready, lg_done = R.sem("xT_done"), R.sem("xnT_ready"), R.sem("lg_done")
            lg_shifted, ex_ready = R.sem("lg_shifted"), R.sem("ex_ready")
            xv = x_in.rearrange("(s t p) d -> s p t d", t=NT, p=P)
            nv = xn_d.rearrange("(s t p) d -> s p t d", t=NT, p=P)

            with nc.Block() as block:
                @block.sync
                def _(sp):
                    sp.dma_start(x[0][:], xv[0]).then_inc(x_loaded[0], 16)
                    for dst, src in [(ident, T["ident"])] + loads:
                        sp.dma_start(dst[:], src).then_inc(consts, 16)

                    def step(s, u, h):
                        if not isinstance(s, int) or s + 1 < NS:
                            if from_step(s, 1):
                                sp.wait_ge(xn_ready, s)
                            sp.dma_start(x[1 - u][:], xv[s + 1]).then_inc(x_loaded[1 - u], 16)
                        sp.wait_ge(xn_ready, s + 1)
                        sp.dma_start(nv[s], xn[u][:]).then_inc(normed_stored[u], 16)

                    span(sp, 0, NS - 1, step)
                    step(NS - 1, (NS - 1) % 2, (NS - 1) // 2)
                    for u in range(2):
                        sp.wait_ge(normed_stored[u], 16 * NS // 2)

                @block.scalar
                def _(act):
                    for dst, src in expert_weights:
                        act.dma_start(dst[:], src).then_inc(weights, 16)
                    act.wait_ge(consts, 16 * (len(loads) + 1))

                    def step(s, u, h):
                        act.wait_ge(xT_done, s + 1)
                        if layer == 0:
                            act.copy(xnT_all[:, bass.ds(SUP * s, SUP)], pT[:])
                        act.copy(xnT[u][:], pT[:]).then_inc(xnT_ready, 1)
                        if layer == 1:
                            act.wait_ge(lg_shifted, s + 1)
                            act.activation(ex[:], lg[:], ACT.Exp).then_inc(ex_ready, 1)

                    span(act, 0, NS, step)

                @block.tensor
                def _(pe):
                    pe.wait_ge(consts, 16 * (len(loads) + 1))

                    def step(s, u, h):
                        pe.wait_ge(xn_ready, s + 1)
                        for t in range(NT):
                            last = pe.transpose(pT[:, t * P:(t + 1) * P], xn[u][:, t, :], ident[:])
                        last.then_inc(xT_done, 1)
                        pe.wait_ge(xnT_ready, s + 1)
                        if from_step(s, 1):
                            pe.wait_ge(lg_shifted, s)
                        for t in range(NT):
                            last = pe.matmul(pL[:, t * GE:(t + 1) * GE], xnT[u][:, t * P:(t + 1) * P], router[:],
                                             start=True, stop=True)
                        last.then_inc(lg_done, 1)

                    span(pe, 0, NS, step)

                @block.vector
                def _(dve):
                    ln, top = Chain(dve, ln_c, dve_passed), Chain(dve, top_c, dve_passed)
                    dve.memset(mhalf[:], -0.5).then_inc(memset, 1)
                    dve.wait_ge(consts, 16 * (len(loads) + 1))

                    def layernorm(s, u, h):
                        ln.start(2 * s)
                        dve.wait_ge(x_loaded[u], 16 * h + 16)
                        for t in range(NT):
                            last = dve.bn_stats(bst[:, t, :], x[u][:, t, :])
                        ln.step(last, own_wait=True)
                        for t in range(NT):
                            last = dve.bn_aggr(mv[:, t, :], bst[:, t, :])
                        ln.step(last)
                        dve.tensor_scalar(veps[:], mv[:, :, 1], LN_EPS, None, ALU.add).then_inc(veps_ready, 1)
                        dve.wait_ge(rstd_ready, s + 1)
                        if from_step(s, 2):
                            dve.wait_ge(normed_stored[u], 16 * h)
                            dve.wait_ge(xT_done, s - 1)
                        for t in range(NT):
                            last = dve.tensor_scalar(xn[u][:, t, :], x[u][:, t, :], mv[:, t, 0:1], rstd[:, t:t + 1],
                                                     ALU.subtract, ALU.mult)
                        last.then_inc(xn_ready, 1)

                    def choose(s, u, h):
                        nsteps = 3 if layer == 0 else 4
                        top.start(nsteps * s)
                        dve.wait_ge(lg_done, s + 1)
                        if layer == 1 and from_step(s, 1):
                            dve.wait_ge(ex_ready, s)
                        top.step(dve.tensor_copy(lg[:].rearrange("p t g e -> p (t g e)"), pL[:, 0:NT * GE]), own_wait=True)
                        for g in range(G):
                            for t in range(NT):
                                last = dve.max(m8[:, g, t, :], lg[:, t, g, :])
                        top.step(last, own_wait=True)
                        for g in range(G):
                            for t in range(NT):
                                last = dve.max_index(i8[:, g, t, :], m8[:, g, t, :], lg[:, t, g, :])
                        top.step(last)
                        for g in range(G):
                            dve.tensor_copy(pick[:, g].rearrange("p s k t -> p (s k) t")[:, bass.ds(2 * s, 2), :],
                                            i8[:, g, :, 0:2].rearrange("p t k -> p k t"))
                            last = dve.tensor_copy(best[:, g].rearrange("p s k t -> p (s k) t")[:, bass.ds(2 * s, 2), :],
                                                   m8[:, g, :, 0:2].rearrange("p t k -> p k t"))
                        if layer == 0:
                            last.then_inc(lg_shifted, 1)
                        else:
                            for g in range(G):
                                last = dve.tensor_tensor(lg[:, :, g, :], lg[:, :, g, :],
                                                         m8[:, g, :, 0:1].to_broadcast([P, NT, E]), ALU.subtract)
                            last.then_inc(lg_shifted, 1)
                            dve.wait_ge(ex_ready, s + 1)
                            top.step(dve.tensor_reduce(sm[:].rearrange("p g t -> p t g"), ex[:], AX.X, ALU.add))
                            dve.tensor_copy(total[:].rearrange("p s g t -> p s (g t)")[:, bass.ds(s, 1), :],
                                            sm[:].rearrange("p g t -> p (g t)").unsqueeze(1))

                    layernorm(0, 0, 0)

                    def step(s, u, h):
                        if not isinstance(s, int) or s + 1 < NS:
                            layernorm(s + 1, 1 - u, h + u)
                        choose(s, u, h)

                    span(dve, 0, NS - 1, step)
                    step(NS - 1, (NS - 1) % 2, (NS - 1) // 2)

                @block.gpsimd
                def _(pool):
                    pool.wait_ge(memset, 1)

                    def step(s, u, h):
                        pool.wait_ge(veps_ready, s + 1)
                        pool.tensor_tensor(rstd[:], veps[:], mhalf[:].to_broadcast([P, NT]), ALU.pow).then_inc(rstd_ready, 1)

                    span(pool, 0, NS, step)

        with Scope(nc, "bd"[layer] + "e") as R:
            ones = R.sb("ones", [P, P], BF16)
            NTL = NS * NT
            oh = [R.sb(f"oh{k}", [P, NS, NT, E]) for k in range(TOPK)]
            both = R.sb("both", [P, NTL * E], BF16)
            tot, run = R.sb("tot", [P, E, NTL]), R.sb("run", [P, E, NTL])
            keep = R.sb("keep", [P, E, NTL])
            one_e = R.sb("one_e", [P, E])
            nbi, nb = R.sb("nbi", [P, E], I32), R.sb("nb", [P, E])
            end, start = R.sb("end", [P, E]), R.sb("start", [P, E])
            pos = R.sb("pos", [P, NS, NT, E])
            place = R.sb("place", [P, NS, TOPK, NT])
            cmp, own = R.sb("cmp", [1, NBLK, E]), R.sb("own", [1, NBLK])
            dif, den = R.sb("dif", [P, G, NS, TOPK, NT]), R.sb("den", [P, G, NS, NT])
            route_c = R.sem("route_c")
            routed = R.sem("routed")
            both_ready, ranks_done, w_sub, w_exp = R.sem("both_ready"), R.sem("ranks_done"), R.sem("w_sub"), R.sem("w_exp")
            NB = -(-TE // 512)
            W = TE // NB
            rank_b, tot_b = bank[0:NB], bank[2:2 + NB]

            xs = R.sb("xs", [P, NS * NT, P])
            got = [R.sb(f"got{u}", [P, TOPK, NT, P]) for u in range(2)]
            got_first = [xs, R.sb("got_first", [P, NS * NT, P])] if G > 1 else None
            total_out = R.sb("total_out", [P, NS * NT, P])
            xq = [R.sb(f"xq{u}", [P, QUAD, P]) for u in range(2)]
            xqT = [R.sb(f"xqT{u}", [P, QUAD * P]) for u in range(2)]
            yq = [R.sb(f"yq{u}", [P, QUAD, P]) for u in range(2)]
            pX, pY = bank[0:2], bank[2:4]
            if layer == 0:
                wx = [R.sb(f"wx{n}", [P, 512]) for n in range(2)]
                bx = [R.sb(f"bx{n}", [P, 4]) for n in range(2)]
                hx = [R.sb(f"hx{n}", [P, 4, P]) for n in range(2)]
                pHx = bank[4:6]
                hs = [[R.sb(f"hs{u}{c}", [P, SUP]) for c in range(4)] for u in range(2)]
                pHs, pO = bank[4:8], bank[3]
                sh_done, sh_ready, so_done, so_added, so_c = (
                    R.sem(n) for n in ("sh_done", "sh_ready", "so_done", "so_added", "so_c"))
            else:
                wx = [R.sb(f"wx{u}", [P, QUAD, P]) for u in range(2)]
                gs = [R.sb(f"gs{u}", [64, QUAD * P]) for u in range(2)]
                hx = [R.sb(f"hx{u}", [64, QUAD * P]) for u in range(2)]
                pG, pU = bank[4:6], bank[6:8]

            two = lambda name: [R.sem(f"{name}{u}") for u in range(2)]
            xs_loaded, x_loaded_all, stored = R.sem("xs_loaded"), R.sem("x_loaded_all"), R.sem("stored")
            scattered = [R.sem(f"scattered{g}") for g in range(G)]
            gathered, first_gathered = two("gathered"), R.sem("first_gathered")
            dve_sum_c, added = R.sem("dve_sum_c"), R.sem("added")
            xq_loaded, results_stored = two("xq_loaded"), two("results_stored")
            xqT_done, xqT_ready, w_ready, h_done, g_ready, h_ready, y_done, y_ready = (
                R.sem(n) for n in ("xqT_done", "xqT_ready", "w_ready", "hx_done", "g_ready", "hx_ready", "y_done", "y_ready"))
            nv = xn_d.rearrange("(s t p) d -> s p t d", t=NT, p=P)
            outv = x_out.rearrange("(s t p) d -> s p t d", t=NT, p=P)

            def each_quad(eng, fn, lo=0):
                span(eng, lo, NQ, fn)

            with nc.Block() as block:
                @block.gpsimd
                def _(pool):
                    def scatter(g):
                        for s in range(NS):
                            for k in range(TOPK):
                                for t in range(NT):
                                    pool.indirect_dma_start(
                                        xg[g], bass.IndirectOffsetOnAxis(ap=dest[:, g, s, k, t:t + 1], axis=0),
                                        xs[:, s * NT + t, :], None).then_inc(scattered[g], 16)

                    def gather(g, s):
                        for k in range(TOPK):
                            for t in range(NT):
                                last = g == G - 1
                                pool.indirect_dma_start(
                                    got[s % 2][:, k, t, :] if last else got_first[k][:, s * NT + t, :], None, yg[g],
                                    bass.IndirectOffsetOnAxis(ap=dest[:, g, s, k, t:t + 1], axis=0)
                                ).then_inc(gathered[s % 2] if last else first_gathered, 16)

                    pool.wait_ge(xs_loaded, 16)
                    for g in range(G):
                        pool.wait_ge(routed, g + 1)
                        scatter(g)
                    for g in range(G):
                        if g < G - 1:
                            for n in range(G):
                                pool.wait_ge(scattered[n], 16 * TOPK * NS * NT)
                        for u in range(2):
                            pool.wait_ge(results_stored[u], 16 * ((NQG * (g + 1) + 1 - u) // 2))
                        for s in range(NS):
                            if g == G - 1 and s >= 2:
                                pool.wait_ge(added, s - 1)
                            gather(g, s)

                @block.sync
                def _(sp):
                    rows = [t.rearrange("(n b p) d -> n p b d", b=QUAD, p=P) for t in xg]
                    def load(g, q, u):
                        if from_step(q, 2):
                            sp.wait_ge(xqT_done, q - 1)
                        sp.dma_start(xq[u][:], rows[g][q - g * NQG]).then_inc(xq_loaded[u], 16)

                    sp.dma_start(xs[:], xn_d.rearrange("(n p) d -> p n d", p=P)).then_inc(xs_loaded, 16)
                    sp.dma_start(total_out[:], x_in.rearrange("(n p) d -> p n d", p=P)).then_inc(x_loaded_all, 16)
                    for g in range(G):
                        sp.wait_ge(scattered[g], 16 * TOPK * NS * NT)
                        span(sp, g * NQG, (g + 1) * NQG, lambda q, u, h: load(g, q, u))

                    def store_final(s, u, h):
                        sp.wait_ge(added, s + 1)
                        sp.dma_start(outv[s], total_out[:, bass.ds(NT * s, NT), :]).then_inc(stored, 16)

                    span(sp, 0, NS, store_final)
                    sp.wait_ge(stored, 16 * NS)

                def owner_of(eng, n):
                    at = owner[0:1, n:n + 1] if isinstance(n, int) else owner[0:1, bass.ds(n, 1)]
                    return eng.value_load(at, min_val=0, max_val=GE - 1)

                @block.scalar
                def _(act):
                    results = [t.rearrange("(n b p) d -> n p b d", b=QUAD, p=P) for t in yg]

                    def turn(q, u):
                        act.wait_ge(xqT_done, q + 1)
                        act.copy(xqT[u][:], pX[u][:]).then_inc(xqT_ready, 1)

                    def store(q, u, g):
                        act.wait_ge(y_ready, q + 1)
                        act.dma_start(results[g][q - g * NQG], yq[u][:]).then_inc(results_stored[u], 16)

                    def step0(q, u, h, g):
                        for j in range(QUAD):
                            act.wait_ge(h_done, QUAD * q + j + 1)
                            for c in range(4):
                                last = act.activation(hx[j % 2][:, c, :], pHx[j % 2][:, c * P:(c + 1) * P], ACT.Gelu,
                                                      bias=bx[j % 2][:, c:c + 1])
                            last.then_inc(h_ready, 1)
                            if j == 1 and (not isinstance(q, int) or q + 1 < NQ):
                                turn(q + 1, 1 - u)
                        if g is not None:
                            store(q - 2, u, g)

                    def step1(q, u, h, g):
                        if not isinstance(q, int) or q + 1 < NQ:
                            turn(q + 1, 1 - u)
                        act.wait_ge(h_done, q + 1)
                        act.activation(gs[u][:], pG[u][0:64, :], ACT.Silu).then_inc(g_ready, 1)
                        if g is not None:
                            store(q - 2, u, g)

                    act.wait_ge(w_sub, 1)
                    act.activation(dif[:], dif[:], ACT.Exp).then_inc(w_exp, 1)
                    if layer == 0:
                        def shared(s, u, h):
                            for c in range(4):
                                act.wait_ge(sh_done, 4 * s + c + 1)
                                if from_step(s, 2):
                                    act.wait_ge(so_done, s - 1)
                                act.activation(hs[u][c][:], pHs[c][:], ACT.Gelu, bias=sb1[:, c:c + 1]).then_inc(sh_ready, 1)

                        span(act, 0, NS, shared)
                    act.wait_ge(weights, 16 * len(expert_weights))
                    turn(0, 0)
                    step_ = step0 if layer == 0 else step1
                    for q in range(2):
                        step_(q, q, 0, None)
                    for g in range(G):
                        span(act, g * NQG + 2, (g + 1) * NQG + (-1 if g == G - 1 else 2),
                             lambda q, u, h: step_(q, u, h, g))
                    step_(NQ - 1, (NQ - 1) % 2, 0, G - 1)
                    for q in (NQ - 2, NQ - 1):
                        store(q, q % 2, G - 1)
                    for u in range(2):
                        act.wait_ge(results_stored[u], 16 * ((NQ + 1 - u) // 2))

                @block.vector
                def _(dve):
                    def route():
                        ch = Chain(dve, route_c)
                        dve.memset(ones[:], 1.0)
                        dve.memset(one_e[:], 1.0)
                        ch.step(dve.memset(keep[:], 1.0))
                        ch.step(dve.memset(keep[:, :, 0:1], 0.0))
                        dve.tensor_tensor(dif[:].rearrange("p g s k t -> p (g s) k t"),
                                          best[:].rearrange("p g s k t -> p (g s) k t"),
                                          best[:].rearrange("p g s k t -> p (g s) k t")[:, :, 0:1, :].to_broadcast(
                                              [P, G * NS, TOPK, NT]), ALU.subtract).then_inc(w_sub, 1)
                        dve.wait_ge(w_exp, 1)
                        if layer == 0:
                            ch.step(dve.tensor_tensor(den[:], dif[:, :, :, 0, :], dif[:, :, :, 1, :], ALU.add))
                        else:
                            ch.step(dve.tensor_scalar(den[:], total[:].rearrange("p s g t -> p g s t"), 2.0, None, ALU.mult))
                        ch.step(dve.reciprocal(den[:], den[:]))
                        for k in range(TOPK):
                            last = dve.tensor_tensor(wgt[:, :, :, k, :], dif[:, :, :, k, :], den[:], ALU.mult)
                        ch.step(last)
                        for g in range(G):
                            for k in range(TOPK):
                                last = dve.tensor_tensor(oh[k][:].rearrange("p s t e -> p s t e"),
                                                         iota[:, 0:E].unsqueeze(1).unsqueeze(1).to_broadcast([P, NS, NT, E]),
                                                         pick[:, g, :, k, :].unsqueeze(3).to_broadcast([P, NS, NT, E]), ALU.is_equal)
                            ch.step(last)
                            dve.tensor_tensor(both[:], oh[0][:].rearrange("p s t e -> p (s t e)"),
                                              oh[1][:].rearrange("p s t e -> p (s t e)"), ALU.add).then_inc(both_ready, 1)
                            dve.wait_ge(ranks_done, g + 1)
                            ntb = NTL // NB
                            for n in range(NB):
                                last = dve.tensor_copy(tot[:, :, n * ntb:(n + 1) * ntb],
                                                       tot_b[n][:, 0:W].rearrange("p (t e) -> p e t", e=E))
                            ch.step(last)
                            ch.step(dve.tensor_tensor_scan(run[:].rearrange("p e t -> p (e t)"), keep[:].rearrange("p e t -> p (e t)"),
                                                           tot[:].rearrange("p e t -> p (e t)"), 0.0, ALU.mult, ALU.add))
                            ch.step(dve.tensor_scalar(nbi[:], run[:, :, NTL - 1], float(P - 1), None, ALU.add))
                            ch.step(dve.tensor_scalar(nbi[:], nbi[:], 7, None, ALU.logical_shift_right))
                            ch.step(dve.tensor_copy(nb[:], nbi[:]))
                            ch.step(dve.tensor_tensor_scan(end[:], one_e[:], nb[:], 0.0, ALU.mult, ALU.add))
                            ch.step(dve.tensor_tensor(start[:], end[:], nb[:], ALU.subtract))
                            ch.step(dve.scalar_tensor_tensor(run[:], start[:].unsqueeze(2).to_broadcast([P, E, NTL]), float(P),
                                                             run[:], ALU.mult, ALU.add))
                            ch.step(dve.tensor_tensor(run[:], run[:], tot[:], ALU.subtract))
                            posf = pos[:].rearrange("p s t e -> p (s t) e")
                            for n in range(NB):
                                last = dve.tensor_tensor(posf[:, n * ntb:(n + 1) * ntb, :],
                                                         rank_b[n][:, 0:W].rearrange("p (t e) -> p t e", e=E),
                                                         run[:, :, n * ntb:(n + 1) * ntb].rearrange("p e t -> p t e"), ALU.add)
                            ch.step(last)
                            for k in range(TOPK):
                                last = dve.tensor_tensor(oh[k][:], oh[k][:], pos[:], ALU.mult)
                            ch.step(last)
                            for k in range(TOPK):
                                last = dve.tensor_reduce(place[:, :, k, :], oh[k][:], AX.X, ALU.add)
                            ch.step(last)
                            ch.step(dve.tensor_copy(dest[:, g], place[:]))
                            ch.step(dve.tensor_tensor(cmp[:], end[0:1, :].unsqueeze(1).to_broadcast([1, NBLK, E]),
                                                      iota[0:1, 0:NBLK].unsqueeze(2).to_broadcast([1, NBLK, E]), ALU.is_le))
                            ch.step(dve.tensor_reduce(own[:], cmp[:], AX.X, ALU.add))
                            ch.step(dve.tensor_scalar(own[:], own[:], float(E - 1), float(g * E), ALU.min, ALU.add))
                            dve.tensor_copy(owner[0:1, g * NBLK:(g + 1) * NBLK], own[:]).then_inc(routed, 1)

                    def weights0(q, j):
                        e = owner_of(dve, QUAD * q + j)
                        if from_step(q, 1) or j >= 2:
                            dve.wait_ge(h_done, QUAD * q + j - 1)
                        dve.tensor_copy(wx[j % 2][:], w1[:, bass.ds(e * 512, 512)])
                        if from_step(q, 1) or j >= 2:
                            dve.wait_ge(h_ready, QUAD * q + j - 1)
                        dve.tensor_copy(bx[j % 2][:], b1[:, bass.ds(e * 4, 4)]).then_inc(w_ready, 1)

                    def results0(q, u, h):
                        es = [owner_of(dve, QUAD * q + j) for j in range(QUAD)]
                        if from_step(q, 2):
                            dve.wait_ge(results_stored[u], 16 * h)
                        dve.wait_ge(y_done, q + 1)
                        for j in range(QUAD):
                            last = dve.tensor_tensor(yq[u][:, j, :], pY[u][:, j * P:(j + 1) * P],
                                                     b2[:, bass.ds(es[j] * P, P)], ALU.add)
                        last.then_inc(y_ready, 1)

                    def step0(q, u, h):
                        for j in range(QUAD):
                            weights0(q, j)
                            if j == 1 and from_step(q, 1):
                                results0(q - 1, 1 - u, h - 1 + u)

                    def weights1(q, u):
                        es = [owner_of(dve, QUAD * q + j) for j in range(QUAD)]
                        if from_step(q, 2):
                            dve.wait_ge(h_done, q - 1)
                        for j in range(QUAD):
                            last = dve.tensor_copy(wx[u][:, j, :], wgu[:, bass.ds(es[j] * P, P)])
                        last.then_inc(w_ready, 1)

                    def results1(q, u, h):
                        if from_step(q, 2):
                            dve.wait_ge(results_stored[u], 16 * h)
                        dve.wait_ge(y_done, q + 1)
                        dve.tensor_copy(yq[u][:].rearrange("p b d -> p (b d)"), pY[u][:]).then_inc(y_ready, 1)

                    def step1(q, u, h):
                        if not isinstance(q, int) or q + 1 < NQ:
                            weights1(q + 1, 1 - u)
                        dve.wait_ge(g_ready, q + 1)
                        if from_step(q, 2):
                            dve.wait_ge(y_done, q - 1)
                        dve.tensor_tensor(hx[u][:], gs[u][:], pU[u][0:64, :], ALU.mult).then_inc(h_ready, 1)
                        if from_step(q, 1):
                            results1(q - 1, 1 - u, h - 1 + u)

                    route()
                    if layer == 0:
                        so = Chain(dve, so_c)
                        dve.wait_ge(x_loaded_all, 16)

                        def shared(s, u, h):
                            so.start(s)
                            out = total_out[:, bass.ds(NT * s, NT), :]
                            dve.wait_ge(so_done, s + 1)
                            so.step(dve.tensor_tensor(out, out, pO[:].rearrange("p (t n) -> p t n", t=NT), ALU.add))
                            dve.tensor_tensor(out, out, sb2[:].unsqueeze(1).to_broadcast([P, NT, P]),
                                              ALU.add).then_inc(so_added, 1)

                        span(dve, 0, NS, shared)
                    dve.wait_ge(weights, 16 * len(expert_weights))
                    dve.wait_ge(routed, G)
                    if layer == 0:
                        each_quad(dve, step0)
                        results0(NQ - 1, (NQ - 1) % 2, (NQ - 1) // 2)
                    else:
                        weights1(0, 0)
                        span(dve, 0, NQ - 1, step1)
                        step1(NQ - 1, (NQ - 1) % 2, (NQ - 1) // 2)
                        results1(NQ - 1, (NQ - 1) % 2, (NQ - 1) // 2)

                    add = Chain(dve, dve_sum_c)
                    flat_wgt = wgt[:].rearrange("p g s k t -> p (g s k t)")

                    def combine(s, u, h):
                        add.start((6 if G > 1 else 2) * s)
                        out = total_out[:, bass.ds(NT * s, NT), :]
                        if G > 1:
                            part = [t[:, bass.ds(NT * s, NT), :] for t in got_first]
                            for k in range(TOPK):
                                last = dve.tensor_tensor(part[k], part[k], flat_wgt[:, bass.ds(8 * s + NT * k, NT)]
                                                         .unsqueeze(2).to_broadcast([P, NT, P]), ALU.mult)
                                add.step(last)
                            for k in range(TOPK):
                                add.step(dve.tensor_tensor(out, out, part[k], ALU.add))
                        dve.wait_ge(gathered[u], 16 * 8 * h + 16 * 8)
                        add.step(dve.tensor_tensor(got[u][:].rearrange("p k t d -> p (k t) d"),
                                                   got[u][:].rearrange("p k t d -> p (k t) d"),
                                                   flat_wgt[:, bass.ds(8 * s + 8 * NS * (G - 1), 8)]
                                                   .unsqueeze(2).to_broadcast([P, 8, P]), ALU.mult))
                        add.step(dve.tensor_tensor(out, out, got[u][:, 0], ALU.add))
                        dve.tensor_tensor(out, out, got[u][:, 1], ALU.add).then_inc(added, 1)

                    if layer == 0:
                        dve.wait_ge(so_added, NS)
                    else:
                        dve.wait_ge(x_loaded_all, 16)
                        dve.wait_ge(first_gathered, 16 * TOPK * NS * NT)
                    span(dve, 0, NS, combine)

                @block.tensor
                def _(pe):
                    def turn(q, u, h):
                        if isinstance(q, int) and q >= NQ:
                            return
                        pe.wait_ge(xq_loaded[u], 16 * h + 16)
                        if from_step(q, 2):
                            pe.wait_ge(xqT_ready, q - 1)
                        for j in range(QUAD):
                            last = pe.transpose(pX[u][:, j * P:(j + 1) * P], xq[u][:, j, :], ident[:])
                        last.then_inc(xqT_done, 1)

                    def hidden0(q, u, j):
                        pe.wait_ge(w_ready, QUAD * q + j + 1)
                        if j == 0:
                            pe.wait_ge(xqT_ready, q + 1)
                        if from_step(q, 1) or j >= 2:
                            pe.wait_ge(h_ready, QUAD * q + j - 1)
                        for c in range(4):
                            last = pe.matmul(pHx[j % 2][:, c * P:(c + 1) * P], wx[j % 2][:, c * P:(c + 1) * P],
                                             xqT[u][:, j * P:(j + 1) * P], start=True, stop=True)
                        last.then_inc(h_done, 1)

                    def out0(q, u, j):
                        e = owner_of(pe, QUAD * q + j)
                        pe.wait_ge(h_ready, QUAD * q + j + 1)
                        if j == 0 and from_step(q, 2):
                            pe.wait_ge(y_ready, q - 1)
                        for c in range(4):
                            last = pe.matmul(pY[u][:, j * P:(j + 1) * P], hx[j % 2][:, c, :],
                                             w2[:, bass.ds(e * 512 + c * P, P)], start=(c == 0), stop=(c == 3))
                        if j == QUAD - 1:
                            last.then_inc(y_done, 1)

                    def step0(q, u, h):
                        for j in range(QUAD):
                            hidden0(q, u, j)
                            if j == 1:
                                turn(q + 1, 1 - u, h + u)
                            if j:
                                out0(q, u, j - 1)
                            elif from_step(q, 1):
                                out0(q - 1, 1 - u, QUAD - 1)

                    def hidden1(q, u):
                        pe.wait_ge(w_ready, q + 1)
                        pe.wait_ge(xqT_ready, q + 1)
                        if from_step(q, 2):
                            pe.wait_ge(h_ready, q - 1)
                        for j in range(QUAD):
                            cols = slice(j * P, (j + 1) * P)
                            pe.matmul(pG[u][0:64, cols], wx[u][:, j, 0:64], xqT[u][:, cols], start=True, stop=True)
                            last = pe.matmul(pU[u][0:64, cols], wx[u][:, j, 64:128], xqT[u][:, cols], start=True, stop=True)
                        last.then_inc(h_done, 1)

                    def out1(q, u):
                        es = [owner_of(pe, QUAD * q + j) for j in range(QUAD)]
                        pe.wait_ge(h_ready, q + 1)
                        if from_step(q, 2):
                            pe.wait_ge(y_ready, q - 1)
                        for j in range(QUAD):
                            cols = slice(j * P, (j + 1) * P)
                            last = pe.matmul(pY[u][:, cols], hx[u][:, cols], wd[:, bass.ds(es[j] * P, P)], start=True, stop=True)
                        last.then_inc(y_done, 1)

                    def step1(q, u, h):
                        turn(q + 1, 1 - u, h + u)
                        hidden1(q, u)
                        if from_step(q, 1):
                            out1(q - 1, 1 - u)

                    for g in range(G):
                        pe.wait_ge(both_ready, g + 1)
                        for n in range(NB):
                            pe.matmul(rank_b[n][:, 0:W], before[:], both[:, n * W:(n + 1) * W], start=True, stop=True)
                            last = pe.matmul(tot_b[n][:, 0:W], ones[:], both[:, n * W:(n + 1) * W], start=True, stop=True)
                        last.then_inc(ranks_done, 1)
                    if layer == 0:
                        def shared_hidden(s):
                            for c in range(4):
                                if from_step(s, 1):
                                    pe.wait_ge(sh_ready, 4 * s + c - 3)
                                pe.matmul(pHs[c][:], sw1[:, c * P:(c + 1) * P], xnT_all[:, bass.ds(SUP * s, SUP)],
                                          start=True, stop=True).then_inc(sh_done, 1)

                        def shared(s, u, h):
                            if not isinstance(s, int) or s + 1 < NS:
                                shared_hidden(s + 1)
                            pe.wait_ge(sh_ready, 4 * s + 4)
                            if from_step(s, 1):
                                pe.wait_ge(so_added, s)
                            for t in range(NT):
                                for c in range(4):
                                    last = pe.matmul(pO[:, t * P:(t + 1) * P], hs[u][c][:, t * P:(t + 1) * P], sw2[:, c, :],
                                                     start=(c == 0), stop=(c == 3))
                            last.then_inc(so_done, 1)

                        shared_hidden(0)
                        span(pe, 0, NS - 1, shared)
                        shared(NS - 1, (NS - 1) % 2, (NS - 1) // 2)
                        pe.wait_ge(so_added, NS)
                    pe.wait_ge(weights, 16 * len(expert_weights))
                    pe.wait_ge(routed, G)
                    turn(0, 0, 0)
                    quads = step0 if layer == 0 else step1
                    span(pe, 0, NQ - 1, quads)
                    quads(NQ - 1, (NQ - 1) % 2, (NQ - 1) // 2)
                    if layer == 0:
                        out0(NQ - 1, (NQ - 1) % 2, QUAD - 1)
                    else:
                        out1(NQ - 1, (NQ - 1) % 2)



def hopfield_mixer(nc, T, x_in, x_out):
    NB = TOK // SEQ
    NT = SEQ // P
    NH, HD, NP, NG = 16, 8, 8, 4
    RING = 3
    with Scope(nc, "c") as S:
        sb, ps, sem = S.sb, S.ps, S.sem
        wqkv, wo = sb("wqkv", [P, 3 * P]), sb("wo", [P, P])
        bqkv, bo = sb("bqkv", [P, 3 * P]), sb("bo", [P, P])
        lnw, lnb = sb("lnw", [P, P]), sb("lnb", [P, P])
        ident, ident_bf = sb("ident", [P, P]), sb("ident_bf", [P, P], BF16)
        mhalf = sb("mhalf", [P, 1])

        x = [sb(f"x{u}", [P, NT, P]) for u in range(RING)]
        xres = [sb(f"xres{u}", [P, NT, P]) for u in range(RING)]
        y = [sb(f"y{u}", [P, NT, P]) for u in range(RING)]
        r = [sb(f"r{u}", [P, NT, P]) for u in range(RING)]
        z = sb("z", [P, NT, P])
        st1, mv1, ve1, rs1 = sb("st1", [P, NT, 6]), sb("mv1", [P, NT, 2]), sb("ve1", [P, NT]), sb("rs1", [P, NT])
        st2, mv2, ve2, rs2 = sb("st2", [P, NT, 6]), sb("mv2", [P, NT, 2]), sb("ve2", [P, NT]), sb("rs2", [P, NT])
        zT = sb("zT", [P, SEQ])
        qk = sb("qk", [P, 2, NT, NH, HD])
        sq, ss = sb("sq", [P, 2, NT, NH, HD]), sb("ss", [P, NT * 2 * NH])
        rn = sb("rn", [P, NT * 2 * NH])
        q6, k6 = sb("q6", [P, NT, NH, 64], BF16), sb("k6", [P, NT, NH, 64], BF16)
        qT = sb("qT", [P, NP, SEQ], BF16)
        kT = [sb(f"kT{u}", [P, NP, SEQ], BF16) for u in range(RING)]
        v1 = [sb(f"v1{u}", [P, NT, NH, 32]) for u in range(RING)]
        e = [sb(f"e{n}", [P, 2, NT, SEQ]) for n in range(4)]
        ot0, ot1 = sb("ot0", [P, NG, SEQ]), sb("ot1", [P, NG, SEQ])
        otb = [sb(f"otb{u}", [P, NG, SEQ], BF16) for u in range(RING)]
        rec, s0, mx = sb("rec", [P, NT, NH]), sb("s0", [P, NT, NH, HD]), sb("mx", [P, NT, NH])
        s6 = sb("s6", [P, NT, NH, 64], BF16)
        sT = sb("sT", [P, NP, SEQ], BF16)
        rec1, s1 = sb("rec1", [P, NT, NH]), sb("s1", [P, NT, NH, HD])
        s1T = sb("s1T", [P, SEQ])

        px = [ps(f"px{n}", [P, 2, NT * SEQ]) for n in range(2)]
        po = [ps(f"po{n}", [P, 512]) for n in range(2)]
        pm = [ps(f"pm{n}", [P, 512]) for n in range(2)]

        consts, memsets, memsets_pool = sem("consts"), sem("memsets"), sem("memsets_pool")
        x_loaded = [sem(f"x_loaded{u}") for u in range(RING)]
        stored = [sem(f"stored{u}") for u in range(RING)]
        ln_c, norm_c, mid_c, out_c = (sem(n) for n in ("ln_c", "norm_c", "mid_c", "out_c"))
        split_c, ssplit_c, zln_c, res_c = (sem(n) for n in ("split_c", "ssplit_c", "zln_c", "res_c"))
        ve1_ready, rs1_ready, r_ready = sem("ve1_ready"), sem("rs1_ready"), sem("r_ready")
        ve2_ready, z_ready, xres_ready = sem("ve2_ready"), sem("z_ready"), sem("xres_ready")
        zT_done, zT_ready, qkv_done, qkv_ready = sem("zT_done"), sem("zT_ready"), sem("qkv_done"), sem("qkv_ready")
        ss_ready, rn_ready = sem("ss_ready"), sem("rn_ready")
        qk_normed, q6_ready, k6_ready = sem("qk_normed"), sem("q6_ready"), sem("k6_ready")
        k6T_done, kT_ready, q6T_done, qT_ready = sem("k6T_done"), sem("kT_ready"), sem("q6T_done"), sem("qT_ready")
        sim_done, exp_done, pv_done, ot_copied = sem("sim_done"), sem("exp_done"), sem("pv_done"), sem("ot_copied")
        otT_done, s0_ready, otb_ready = sem("otT_done"), sem("s0_ready"), sem("otb_ready")
        mxs_done, mx_ready = sem("mxs_done"), sem("mx_ready")
        s6_ready, aug_ready, s6T_done, sT_ready = sem("s6_ready"), sem("aug_ready"), sem("s6T_done"), sem("sT_ready")
        ot1T_done, s1_ready, s1T_done, s1T_ready = sem("ot1T_done"), sem("s1_ready"), sem("s1T_done"), sem("s1T_ready")
        dve_passed, pool_passed = sem("dve_passed"), sem("pool_passed")
        wo_done, y_ready = sem("wo_done"), sem("y_ready")

        xv = x_in.rearrange("(b t p) d -> b p t d", t=NT, p=P)
        yv = x_out.rearrange("(b t p) d -> b p t d", t=NT, p=P)
        NCONST = 10

        class Pass:

            def __init__(self, i, k):
                self.i, self.k, self.b = i, k, 3 * i + k
                b = self.b if isinstance(i, int) else RING + 1
                self.first_step = 0 <= b < NB
                self.second_step = 1 <= b <= NB
                self.prepare = 0 <= b + 1 < NB
                self.ahead = b + 2 < NB
                self.between = 1 <= b <= NB
                self.finish = b >= 2
                self.n = b
                self.loop0 = 2 * self.b - 1 if b >= 1 else 0
                self.loop1 = 2 * self.b if b < NB else 2 * self.b - 1
                self.pend0 = None if b < 2 else (2 * self.b - 2, k - 2)
                self.pend1 = (self.loop0, k) if self.first_step else None

            def ring(self, d=0):
                return (self.k + d) % RING

            def turn(self, d=0):
                return self.i + (self.k + d) // RING

        def each_pass(eng, run):
            run(Pass(0, -2))
            run(Pass(0, -1))
            for k in range(RING + 1):
                run(Pass(0, k))
            with eng.Fori(0, (NB - 4) // RING - 1) as i:
                for k in range(RING):
                    run(Pass(i, RING + 1 + k))
            for k in range(RING + 1, RING + 5):
                run(Pass((NB - 4) // RING - 1, k))

        with nc.Block() as block:
            @block.sync
            def _(sp):
                for dst, src in ((ident, T["ident"]), (ident_bf, T["ident_bf"].bitcast(BF16)),
                                 (lnw, T["L1_attn_ln_w"].partition_broadcast(P)),
                                 (lnb, T["L1_attn_ln_b"].partition_broadcast(P)),
                                 (bo, T["L1_attn_bo"].partition_broadcast(P)), (wo, T["L1_attn_Wo"])):
                    sp.dma_start(dst[:], src).then_inc(consts, 16)
                for n, name in enumerate("qkv"):
                    sp.dma_start(wqkv[:, n * P:(n + 1) * P], T[f"L1_attn_W{name}"]).then_inc(consts, 16)
                sp.dma_start(bqkv[:], T["c_bqkv"].partition_broadcast(P)).then_inc(consts, 16)

                def load(p, d):
                    if p.n + d >= RING:
                        sp.wait_ge(xres_ready, p.b + d - RING + 1)
                    sp.dma_start(x[p.ring(d)][:], xv[p.b + d]).then_inc(x_loaded[p.ring(d)], 16)

                def run(p):
                    if p.n == -2:
                        load(p, 2)
                    if p.n + 3 < NB:
                        load(p, 3)
                    if p.finish:
                        sp.wait_ge(y_ready, p.b - 1)
                        sp.dma_start(yv[p.b - 2], y[p.ring(-2)][:]).then_inc(stored[p.ring(-2)], 16)

                each_pass(sp, run)
                sp.wait_ge(y_ready, NB)
                sp.dma_start(yv[NB - 1], y[(NB - 1) % RING][:]).then_inc(stored[(NB - 1) % RING], 16)
                for u in range(RING):
                    sp.wait_ge(stored[u], 16 * len(range(u, NB, RING)))

            @block.vector
            def _(dve):
                ln, norm, mid, fin, split, ssplit = (
                    Chain(dve, s, dve_passed) for s in (ln_c, norm_c, mid_c, out_c, split_c, ssplit_c))
                for t in (q6, k6, s6):
                    dve.memset(t[:].rearrange("p t h c -> p (t h c)").bitcast(U32), 0)
                for u in range(RING):
                    dve.memset(v1[u][:], 0.0)
                dve.memset(mhalf[:], -0.5).then_inc(memsets, 1)
                dve.wait_ge(memsets, 1)
                dve.memset(k6[:, :, :, 48:51], 1.0)
                for u in range(RING):
                    last = dve.memset(v1[u][:, :, :, HD:HD + 1], 1.0)
                last.then_inc(memsets, 1)
                dve.wait_ge(consts, 16 * NCONST)
                dve.wait_ge(memsets, 2)

                def first_statistics(p):
                    ln.start(4 * (p.b + 2))
                    xb = x[p.ring(2)]
                    dve.wait_ge(x_loaded[p.ring(2)], 16 * p.turn(2) + 16)
                    for t in range(NT):
                        last = dve.bn_stats(st1[:, t, :], xb[:, t, :])
                    ln.step(last, own_wait=True)
                    for t in range(NT):
                        last = dve.bn_aggr(mv1[:, t, :], st1[:, t, :])
                    ln.step(last)
                    dve.tensor_scalar(ve1[:], mv1[:, :, 1], LN_EPS, None, ALU.add).then_inc(ve1_ready, 1)

                def second_statistics(p):
                    ln.start(4 * (p.b + 2) + 2)
                    xb, rb = x[p.ring(2)], r[p.ring(2)]
                    dve.wait_ge(rs1_ready, p.b + 3)
                    if p.n >= 1:
                        dve.wait_ge(xres_ready, p.b)
                    for t in range(NT):
                        last = dve.tensor_scalar(rb[:, t, :], xb[:, t, :], mv1[:, t, 0:1], rs1[:, t:t + 1],
                                                 ALU.subtract, ALU.mult)
                    last.then_inc(r_ready, 1)
                    dve.wait_ge(r_ready, p.b + 3)
                    for t in range(NT):
                        last = dve.bn_stats(st2[:, t, :], rb[:, t, :])
                    ln.step(last, own_wait=True)
                    for t in range(NT):
                        last = dve.bn_aggr(mv2[:, t, :], st2[:, t, :])
                    ln.step(last)
                    dve.tensor_scalar(ve2[:], mv2[:, :, 1], LN_EPS, None, ALU.add).then_inc(ve2_ready, 1)

                def qkv_bias(p):
                    for t in range(NT):
                        dve.wait_ge(qkv_done, NT * (p.b + 1) + t + 1)
                        dve.tensor_tensor(qk[:, :, t].rearrange("p s h d -> p s (h d)"),
                                          pm[t][:, 0:2 * P].rearrange("p (s c) -> p s c", s=2),
                                          bqkv[:, 0:2 * P].rearrange("p (s c) -> p s c", s=2), ALU.add)
                        dve.tensor_tensor(v1[p.ring(1)][:, t, :, 0:HD],
                                          pm[t][:, 2 * P:3 * P].rearrange("p (h d) -> p h d", h=NH),
                                          bqkv[:, 2 * P:3 * P].rearrange("p (h d) -> p h d", h=NH),
                                          ALU.add).then_inc(qkv_ready, 1)

                def square_sums(p):
                    norm.start(2 * (p.b + 1))
                    dve.wait_ge(qkv_ready, NT * (p.b + 2))
                    norm.step(dve.tensor_tensor(sq[:], qk[:], qk[:], ALU.mult))
                    norm.step(dve.tensor_reduce(ss[:], sq[:].rearrange("p s t h d -> p (s t h) d"), AX.X, ALU.add))
                    dve.tensor_scalar(ss[:], ss[:], 1e-24, None, ALU.max).then_inc(ss_ready, 1)

                def normalise_queries_keys(p):
                    dve.wait_ge(rn_ready, p.b + 2)
                    qkf = qk[:].rearrange("p s t h d -> p (s t h) d")
                    dve.tensor_tensor(qkf, qkf, rn[:].unsqueeze(2).to_broadcast([P, NT * 2 * NH, HD]),
                                      ALU.mult).then_inc(qk_normed, 1)

                QUERY_PLACES = (slice(0, 3), slice(4, 6), slice(3, 4))
                KEY_PLACES = (slice(2, 5), slice(1, 6, 4), slice(0, 1))

                def place(chain, src, dst, places, ready):
                    rest = src.rearrange("p t h d -> p (t h) d")
                    to = dst[:].rearrange("p t h c -> p (t h) c")[:, :, 0:48].rearrange("p n (m d) -> p n m d", m=6)
                    for n, at in enumerate(places):
                        count = len(range(6)[at])
                        ins = dve.tensor_copy(to[:, :, at, :], rest.unsqueeze(2).to_broadcast([P, NT * NH, count, HD]))
                        if n < 2:
                            chain.step(ins)
                            chain.step(dve.tensor_tensor(rest, rest, to[:, :, at.start, :], ALU.subtract))
                    ins.then_inc(ready, 1)

                def place_keys_queries(p):
                    split.start(8 * (p.b + 1))
                    dve.wait_ge(qk_normed, p.b + 2)
                    if p.n >= 0:
                        dve.wait_ge(k6T_done, NT * (p.b + 1))
                    place(split, qk[:, 1], k6, KEY_PLACES, k6_ready)
                    if p.n >= 0:
                        dve.wait_ge(q6T_done, NT * (p.b + 1))
                    place(split, qk[:, 0], q6, QUERY_PLACES, q6_ready)

                def place_state(p):
                    ssplit.start(4 * p.b)
                    dve.wait_ge(s0_ready, NT * (p.b + 1))
                    if p.n >= 1:
                        dve.wait_ge(s6T_done, NT * p.b)
                    place(ssplit, s0[:], s6, QUERY_PLACES, s6_ready)

                def normalise(chain, t, recip, s):
                    v = pm[t][:].rearrange("p (g j2 j1 c) -> p g j1 j2 c", g=NG, j2=2, j1=2)
                    rv = recip[:, t, :].rearrange("p (g j1 j2) -> p g j1 j2", g=NG, j1=2)
                    chain.step(dve.reciprocal(rv, v[:, :, :, :, HD]))
                    sv = s[:, t, :, :].rearrange("p (g j1 j2) d -> p g j1 j2 d", g=NG, j1=2)
                    for j1 in range(2):
                        last = dve.tensor_tensor(sv[:, :, j1], v[:, :, j1, :, 0:HD],
                                                 rv[:, :, j1, :].unsqueeze(3).to_broadcast([P, NG, 2, HD]), ALU.mult)
                    return last

                def state(p):
                    mid.start(7 * p.b)
                    for t in range(NT):
                        dve.wait_ge(otT_done, NT * p.b + t + 1)
                        normalise(mid, t, rec, s0).then_inc(s0_ready, 1)

                def maxima(p, d, units):
                    for n in units:
                        head = (n // 4) * 4 + 2 * (n % 4 % 2) + n % 4 // 2
                        dve.wait_ge(mxs_done, 16 * (p.b + d) + n + 1)
                        dve.tensor_reduce(mx[:, :, head], pm[n % 2][:].rearrange("p (t k) -> p t k", t=NT), AX.X,
                                          ALU.max).then_inc(mx_ready, 1)

                def shifts(p):
                    mid.start(7 * (p.b - 1) + 2)
                    dve.wait_ge(mx_ready, 16 * p.b)
                    mid.step(dve.scalar_tensor_tensor(mx[:], mx[:], -1.0, rec[:], ALU.mult, ALU.mult))
                    split3(dve, mid, mx[:], [s6[:, :, :, 48 + n] for n in range(3)], aug_ready)

                def s6T_copy(p):
                    for t in range(NT):
                        dve.wait_ge(s6T_done, NT * (p.b - 1) + t + 1)
                        dve.tensor_copy(sT[:, :, t * P:(t + 1) * P],
                                        pm[t][:].bitcast(BF16).rearrange("p (h q) -> p h q", h=NP)).then_inc(sT_ready, 1)

                def final_state(p):
                    fin.start(2 * (p.b - 2))
                    for t in range(NT):
                        dve.wait_ge(ot1T_done, NT * (p.b - 2) + t + 1)
                        normalise(fin, t, rec1, s1).then_inc(s1_ready, 1)

                def output(p):
                    u = p.ring(-2)
                    dve.wait_ge(wo_done, p.b - 1)
                    dve.wait_ge(xres_ready, p.b - 1)
                    if p.n - 2 >= RING:
                        dve.wait_ge(stored[u], 16 * p.turn(-2))
                    dve.tensor_tensor(y[u][:], pm[1][:, 0:NT * P].rearrange("p (t n) -> p t n", t=NT), xres[u][:],
                                      ALU.add).then_inc(y_ready, 1)

                def kT_copy(p):
                    for t in range(NT):
                        dve.wait_ge(k6T_done, NT * (p.b + 1) + t + 1)
                        dve.tensor_copy(kT[p.ring(1)][:, :, t * P:(t + 1) * P],
                                        pm[t][:].bitcast(BF16).rearrange("p (h q) -> p h q", h=NP)).then_inc(kT_ready, 1)

                def run(p):
                    if p.prepare:
                        qkv_bias(p)
                        square_sums(p)
                    if p.between:
                        maxima(p, -1, range(8, 10))
                    if p.ahead:
                        first_statistics(p)
                    if p.between:
                        maxima(p, -1, range(10, 14))
                    if p.ahead:
                        second_statistics(p)
                    if p.between:
                        maxima(p, -1, range(14, 16))
                        shifts(p)
                    if p.finish:
                        final_state(p)
                    if p.between:
                        s6T_copy(p)
                    if p.finish:
                        output(p)
                    if p.prepare:
                        normalise_queries_keys(p)
                        place_keys_queries(p)
                    if p.first_step:
                        state(p)
                        place_state(p)
                        maxima(p, 0, range(8))
                    if p.prepare:
                        kT_copy(p)

                each_pass(dve, run)
                p = Pass((NB + 1) // RING, (NB + 1) % RING)
                final_state(p)
                output(p)

            @block.scalar
            def _(act):
                def exp(loop, hp):
                    n = 8 * loop + hp
                    act.wait_ge(sim_done, n + 1)
                    if hp >= 4 or not isinstance(loop, int) or loop >= 1:
                        act.wait_ge(pv_done, 4 * loop + hp // 2 - 1)
                    act.activation(e[hp % 4][:].rearrange("p a t q -> p (a t q)"), px[hp % 2][:].rearrange("p a q -> p (a q)"),
                                   ACT.Exp).then_inc(exp_done, 1)

                def copy_ot(loop, g, step, slot=None):
                    act.wait_ge(pv_done, 4 * loop + g + 1)
                    if step == 0:
                        act.activation(otb[slot][:, g, :], po[g % 2][:, 0:SEQ], ACT.Copy).then_inc(otb_ready, 1)
                    act.activation((ot0, ot1)[step][:, g, :], po[g % 2][:, 0:SEQ], ACT.Copy).then_inc(ot_copied, 1)

                def half(loop, step, exists, pend, pend_step, side, slot):
                    for hp in range(NP):
                        if exists:
                            exp(loop, hp)
                        if hp == 0 and pend:
                            copy_ot(pend[0], 3, pend_step, slot)
                        if hp % 2 == 0 and hp and exists:
                            if hp == 2 and step == 0:
                                side("ot0")
                            copy_ot(loop, hp // 2 - 1, step, slot)
                        side(hp)

                def run(p):
                    def side0(at):
                        if at == "ot0" and p.n >= 1:
                            act.wait_ge(otT_done, NT * p.b)
                            if p.n >= RING:
                                act.wait_ge(mxs_done, 16 * (p.b - RING + 1))
                        if at == 0 and p.prepare:
                            act.wait_ge(zT_done, p.b + 2)
                            act.activation(zT[:], pm[0][:, 0:SEQ], ACT.Copy).then_inc(zT_ready, 1)
                        if at == 7 and p.finish:
                            act.wait_ge(s1T_done, p.b - 1)
                            act.activation(s1T[:], pm[0][:, 0:SEQ], ACT.Copy).then_inc(s1T_ready, 1)

                    def side1(at):
                        if at == 7 and p.prepare:
                            for t in range(NT):
                                act.wait_ge(q6T_done, NT * (p.b + 1) + t + 1)
                                act.activation(qT[:, :, t * P:(t + 1) * P],
                                               pm[t][:].bitcast(BF16).rearrange("p (h q) -> p h q", h=NP),
                                               ACT.Copy).then_inc(qT_ready, 1)

                    if p.n >= -1:
                        half(p.loop0, 0, p.first_step, p.pend0, 1, side0, p.ring())
                        half(p.loop1, 1, p.second_step, p.pend1, 0, side1, p.ring())

                each_pass(act, run)
                copy_ot(2 * NB - 1, 3, 1)
                act.wait_ge(s1T_done, NB)
                act.activation(s1T[:], pm[0][:, 0:SEQ], ACT.Copy).then_inc(s1T_ready, 1)

            @block.tensor
            def _(pe):
                pe.wait_ge(consts, 16 * NCONST)
                pe.wait_ge(memsets, 2)

                def sims(loop, hp, qside, kside):
                    n = 8 * loop + hp
                    if hp >= 2 or not isinstance(loop, int) or loop >= 1:
                        pe.wait_ge(exp_done, n - 1)
                    for a in range(2):
                        rows = slice(64 * a, 64 * a + 64)
                        for t in range(NT):
                            last = pe.matmul(px[hp % 2][:, a, t * SEQ:(t + 1) * SEQ], kside[rows, hp, t * P:(t + 1) * P],
                                             qside[rows, hp, :], start=True, stop=True)
                    last.then_inc(sim_done, 1)

                def values(loop, g, v):
                    pe.wait_ge(exp_done, 8 * loop + 2 * g + 2)
                    if g >= 2 or not isinstance(loop, int) or loop >= 1:
                        pe.wait_ge(ot_copied, 4 * loop + g - 1)
                    for t in range(NT):
                        for j in range(4):
                            hp, a = 2 * g + j % 2, j // 2
                            last = pe.matmul(po[g % 2][32 * j:32 * j + 32, 0:SEQ], v[:, t, 2 * hp + a, :],
                                             e[hp % 4][:, a, t, :], start=(t == 0), stop=(t == NT - 1))
                    last.then_inc(pv_done, 1)

                def half(loop, exists, qside, kside, v, pend, side):
                    for hp in range(NP):
                        if exists:
                            sims(loop, hp, qside, kside)
                        if hp == 0 and pend:
                            values(pend[0], 3, v1[pend[1] % RING])
                        if hp % 2 == 0 and hp and exists:
                            values(loop, hp // 2 - 1, v)
                        side(hp)

                def ot_transposes(src, done, t):
                    for g in range(NG):
                        last = pe.transpose(pm[t][:, g * P:(g + 1) * P], src[:, g, t * P:(t + 1) * P], ident[:])
                    last.then_inc(done, 1)

                def transposes6(src, done, t):
                    for hp in range(NP):
                        last = pe.transpose(pm[t][:].bitcast(BF16)[:, hp * P:(hp + 1) * P],
                                            src[:, t, 2 * hp:2 * hp + 2, :].rearrange("p h c -> p (h c)"), ident_bf[:])
                    last.then_inc(done, 1)

                def maxima(p, d, units):
                    for n in units:
                        g, j = n // 4, n % 4
                        rows = slice(32 * j, 32 * j + HD)
                        if n >= 2:
                            pe.wait_ge(mx_ready, 16 * (p.b + d) + n - 1)
                        for t in range(NT):
                            last = pe.matmul(pm[n % 2][:, t * SEQ:(t + 1) * SEQ], otb[p.ring(d)][rows, g, t * P:(t + 1) * P],
                                             kT[p.ring(d)][rows, 2 * g + j % 2, :], start=True, stop=True)
                        last.then_inc(mxs_done, 1)

                def finish_a(p):
                    pe.wait_ge(ot_copied, 4 * p.pend0[0] + 4)
                    if p.between:
                        pe.wait_ge(mx_ready, 16 * p.b)
                    for t in range(NT):
                        ot_transposes(ot1, ot1T_done, t)

                def state_transposes(p):
                    pe.wait_ge(aug_ready, p.b)
                    pe.wait_ge(s6_ready, p.b)
                    if p.finish:
                        pe.wait_ge(s1_ready, NT * (p.b - 1))
                    for t in range(NT):
                        transposes6(s6, s6T_done, t)

                def finish_b(p):
                    pe.wait_ge(s1_ready, NT * (p.b - 1))
                    if p.between:
                        pe.wait_ge(sT_ready, NT * p.b)
                    for t in range(NT):
                        last = pe.transpose(pm[0][:, t * P:(t + 1) * P], s1[:, t, :, :].rearrange("p h d -> p (h d)"), ident[:])
                    last.then_inc(s1T_done, 1)
                    pe.wait_ge(s1T_ready, p.b - 1)
                    for t in range(NT):
                        last = pe.matmul(pm[1][:, t * P:(t + 1) * P], s1T[:, t * P:(t + 1) * P], wo[:], start=True, stop=True)
                    last.then_inc(wo_done, 1)

                def run(p):
                    def side0(at):
                        if p.prepare:
                            if at == 0:
                                pe.wait_ge(z_ready, p.b + 2)
                                for t in range(NT):
                                    last = pe.transpose(pm[0][:, t * P:(t + 1) * P], z[:, t, :], ident[:])
                                last.then_inc(zT_done, 1)
                            if at == 1:
                                pe.wait_ge(zT_ready, p.b + 2)
                                for t in range(NT):
                                    pe.matmul(pm[t][:, 0:3 * P], zT[:, t * P:(t + 1) * P], wqkv[:], start=True,
                                              stop=True).then_inc(qkv_done, 1)
                        if p.between:
                            if at == 2 and p.prepare:
                                pe.wait_ge(qkv_ready, NT * (p.b + 2))
                            if 2 <= at <= 5:
                                maxima(p, -1, range(4 + 2 * at, 6 + 2 * at))
                        if at == 6 and p.finish:
                            finish_a(p)
                        if at == 7:
                            if p.between:
                                state_transposes(p)
                            if p.finish:
                                finish_b(p)

                    def side1(at):
                        if p.first_step:
                            if at == 2:
                                pe.wait_ge(ot_copied, 4 * p.loop0 + 4)
                                if p.finish:
                                    pe.wait_ge(y_ready, p.b - 1)
                                elif p.between:
                                    pe.wait_ge(sT_ready, NT * p.b)
                                else:
                                    pe.wait_ge(qkv_ready, NT * (p.b + 2))
                                for t in range(NT):
                                    ot_transposes(ot0, otT_done, t)
                            if 3 <= at <= 6:
                                if at == 3:
                                    pe.wait_ge(s0_ready, NT * (p.b + 1))
                                    pe.wait_ge(otb_ready, NG * (p.b + 1))
                                maxima(p, 0, range(2 * at - 6, 2 * at - 4))
                        if at == 7 and p.prepare:
                            pe.wait_ge(k6_ready, p.b + 2)
                            if p.first_step:
                                pe.wait_ge(mx_ready, 16 * p.b + 8)
                            for t in range(NT):
                                transposes6(k6, k6T_done, t)
                            pe.wait_ge(q6_ready, p.b + 2)
                            pe.wait_ge(kT_ready, NT * (p.b + 2))
                            for t in range(NT):
                                transposes6(q6, q6T_done, t)
                            pe.wait_ge(qT_ready, NT * (p.b + 2))

                    if p.n >= -1:
                        half(p.loop0, p.first_step, qT, kT[p.ring(0)], v1[p.ring(0)], p.pend0, side0)
                        if p.second_step:
                            pe.wait_ge(sT_ready, NT * p.b)
                        half(p.loop1, p.second_step, sT, kT[p.ring(-1)], v1[p.ring(-1)], p.pend1, side1)

                each_pass(pe, run)
                values(2 * NB - 1, 3, v1[(NB - 1) % RING])
                pe.wait_ge(ot_copied, 4 * 2 * NB)
                pe.wait_ge(y_ready, NB - 1)
                for t in range(NT):
                    ot_transposes(ot1, ot1T_done, t)
                finish_b(Pass((NB + 1) // RING, (NB + 1) % RING))

            @block.gpsimd
            def _(pool):
                zln, resc = (Chain(pool, s, pool_passed) for s in (zln_c, res_c))
                pool.wait_ge(consts, 16 * NCONST)
                pool.wait_ge(memsets, 2)

                def wide(t):
                    return t[:].unsqueeze(1).to_broadcast([P, NT, P])

                def norms(p):
                    pool.wait_ge(ss_ready, p.b + 2)
                    pool.tensor_tensor(rn[:], ss[:], mhalf[:].to_broadcast([P, NT * 2 * NH]), ALU.pow).then_inc(rn_ready, 1)

                def residual(p):
                    resc.start(p.b + 1)
                    u = p.ring(1)
                    pool.wait_ge(r_ready, p.b + 2)
                    if p.n + 1 >= RING:
                        pool.wait_ge(y_ready, p.b + 2 - RING)
                    resc.step(pool.tensor_tensor(xres[u][:], x[u][:], wide(bo), ALU.add))
                    pool.tensor_tensor(xres[u][:], xres[u][:], r[u][:], ALU.add).then_inc(xres_ready, 1)

                def first_roots(p):
                    pool.wait_ge(ve1_ready, p.b + 3)
                    pool.tensor_tensor(rs1[:], ve1[:], mhalf[:].to_broadcast([P, NT]), ALU.pow).then_inc(rs1_ready, 1)

                def second_ln(p):
                    zln.start(3 * (p.b + 2))
                    rb = r[p.ring(2)]
                    pool.wait_ge(ve2_ready, p.b + 3)
                    zln.step(pool.tensor_tensor(rs2[:], ve2[:], mhalf[:].to_broadcast([P, NT]), ALU.pow))
                    if p.n >= -1:
                        pool.wait_ge(zT_done, p.b + 2)
                    zln.own_wait()
                    for t in range(NT):
                        last = pool.tensor_scalar(z[:, t, :], rb[:, t, :], mv2[:, t, 0:1], rs2[:, t:t + 1], ALU.subtract, ALU.mult)
                    zln.step(last)
                    zln.step(pool.tensor_tensor(z[:], z[:], wide(lnw), ALU.mult))
                    pool.tensor_tensor(z[:], z[:], wide(lnb), ALU.add).then_inc(z_ready, 1)

                def run(p):
                    if p.ahead:
                        first_roots(p)
                    if p.prepare:
                        norms(p)
                    if p.ahead:
                        second_ln(p)
                    if p.prepare:
                        residual(p)

                each_pass(pool, run)



def program(nc, T, out):
    stages = [nc.dram_tensor(f"stage{n}", [TOK, P], F32, kind="Internal").ap() for n in range(3)]
    rows = [row_space(nc, layer) for layer in range(2)]
    recurrent_mixer(nc, T, T["L0_attn_x"].rearrange("b s d -> (b s) d"), stages[0], clear=rows[0] + rows[1])
    expert_mixture(nc, T, stages[0], stages[1], rows[0], 0)
    hopfield_mixer(nc, T, stages[1], stages[2])
    expert_mixture(nc, T, stages[2], out.rearrange("b s d -> (b s) d"), rows[1], 1)


def _tables():
    import numpy as np
    eye = np.eye(128, dtype=np.float32)
    headsel = np.zeros((128, 32), np.float32)
    headsel[:64, 0] = 1
    headsel[64:, 1] = 1
    sel3 = np.zeros((32, 4, 128), np.float32)
    for part in range(3):
        for c in range(4):
            for r in range(2):
                sel3[8 * part + 2 * c + r, c, 64 * r:64 * r + 64] = 1
    bits = lambda t: np.where(t != 0, 0x3F80, 0).astype(np.uint16)
    return {"ident": eye, "ident_bf": bits(eye), "headsel": headsel, "sel3": bits(sel3),
            "m_iota": np.arange(128, dtype=np.float32), "m_before": bits(np.triu(np.ones((128, 128)), 1))}


def _layout(inputs):
    import numpy as np
    arrays = {k: np.ascontiguousarray(v) for k, v in inputs.items()}
    by_channel = lambda v: np.asarray(v).reshape(4, 128).T
    arrays["a_cols"] = np.ascontiguousarray(np.stack(
        [by_channel(arrays[f"L0_attn_{n}"]) for n in ("bq", "bk", "bv", "alpha", "aug_param")], axis=1))
    arrays["c_bqkv"] = np.concatenate([arrays[f"L1_attn_b{n}"] for n in "qkv"])
    arrays["m_gate"] = np.ascontiguousarray(arrays["L0_ffn_gate_w"].T)
    arrays["m_b1"] = np.ascontiguousarray(arrays["L0_ffn_b1"].reshape(8, 4, 128).transpose(2, 0, 1).reshape(128, 32))
    arrays["m_w2"] = np.ascontiguousarray(
        arrays["L0_ffn_W2"].reshape(8, 4, 128, 128).transpose(2, 0, 1, 3).reshape(128, 32 * 128))
    arrays["m_sb1"] = np.ascontiguousarray(by_channel(arrays["L0_ffn_sb1"]))
    arrays["m_router"] = np.concatenate([arrays[f"L1_ffn_router_w{g}"] for g in range(2)], axis=1)
    group = lambda name: np.concatenate([arrays[f"L1_ffn_{name}{g}"] for g in range(2)], axis=0)
    arrays["m_wgu"] = np.ascontiguousarray(
        np.concatenate([group("wg"), group("wu")], axis=2).transpose(1, 0, 2).reshape(128, 64 * 128))
    arrays["m_wd"] = np.ascontiguousarray(group("wd").transpose(1, 0, 2).reshape(64, 64 * 128))
    arrays.update(_tables())
    return arrays


def kernel(**inputs):
    import concourse.bacc as bacc
    from concourse.bass_utils import run_bass_kernel_spmd

    nc = bacc.Bacc("TRN2", target_bir_lowering=False, num_devices=1)
    arrays, T = {}, {}
    for name, a in _layout(inputs).items():
        arrays[f"in_{name}"] = a
        T[name] = nc.dram_tensor(f"in_{name}", a.shape, mybir.dt.from_np(a.dtype), kind="ExternalInput").ap()
    out = nc.dram_tensor("out", [16, SEQ, P], F32, kind="ExternalOutput").ap()
    program(nc, T, out)
    return run_bass_kernel_spmd(nc, [arrays], core_ids=[0]).results[0]["out"]
```

```python
from contextlib import ExitStack

import concourse.bass as bass
from concourse import mybir

F32 = mybir.dt.float32
BF16 = mybir.dt.bfloat16
I32 = mybir.dt.int32
U32 = mybir.dt.uint32
ALU = mybir.AluOpType
ACT = mybir.ActivationFunctionType
AX = mybir.AxisListType

P = 128
TOK = 4096
SEQ = 256
SUP = 512
LN_EPS = 1e-5
LN0_EPS = 1e-6


class Chain:

    def __init__(self, eng, sem, passed=None):
        self.eng, self.sem, self.base, self.n, self.passed = eng, sem, 0, 0, passed

    def start(self, base):
        self.base, self.n = base, 0

    def own_wait(self):
        self.eng.sem_inc(self.passed, 1)

    def step(self, ins, own_wait=False):
        self.n += 1
        ins.then_inc(self.sem, 1)
        self.eng.wait_ge(self.sem, self.base + self.n)
        if own_wait:
            self.own_wait()


class Scope:

    def __init__(self, nc, tag):
        self.nc, self.tag, self.ctx, self.sems = nc, tag, ExitStack(), []

    def __enter__(self):
        return self

    def __exit__(self, *e):
        with self.nc.Block() as block:
            @block.sync
            def _(sp):
                for s in self.sems[0::3]:
                    sp.sem_clear(s)

            @block.scalar
            def _(act):
                for s in self.sems[1::3]:
                    act.sem_clear(s)

            @block.tensor
            def _(pe):
                for s in self.sems[2::3]:
                    pe.sem_clear(s)
        return self.ctx.__exit__(*e)

    def sb(self, name, shape, dt=F32):
        return self.ctx.enter_context(self.nc.sbuf_tensor(f"{self.tag}_{name}", shape, dt))

    def ps(self, name, shape, dt=F32):
        return self.ctx.enter_context(self.nc.psum_tensor(f"{self.tag}_{name}", shape, dt))

    def sem(self, name):
        s = self.ctx.enter_context(self.nc.semaphore(f"{self.tag}_{name}"))
        self.sems.append(s)
        return s



def recurrent_mixer(nc, T, x_in, x_out, clear=()):
    NS = TOK // SUP
    NT = SUP // P
    NC = 4
    with Scope(nc, "a") as S:
        sb, ps, sem = S.sb, S.ps, S.sem
        wq, wk, wv = sb("wq", [P, 512]), sb("wk", [P, 512]), sb("wv", [P, 512])
        wo, wo_h = sb("wo", [P, NC, P]), sb("wo_h", [P, NC, P])
        cols = sb("cols", [P, 5, NC])
        rows = sb("rows", [1, P])
        lns, lnb = sb("lns", [P, P]), sb("lnb", [P, P])
        ident, headsel = sb("ident", [P, P]), sb("headsel", [P, 32])
        ident_bf = sb("ident_bf", [P, P], BF16)
        sel3 = sb("sel3", [32, NC, P], BF16)
        halves, one_row = sb("halves", [P, P]), sb("one_row", [1, P])
        mhalf = sb("mhalf", [P, 1])
        decay, omd = sb("decay", [P, NC]), sb("omd", [P, NC])
        th_a, bvs = sb("th_a", [P, NC]), sb("bvs", [P, NC])
        augh, augb = sb("augh", [P, NC]), sb("augb", [P, NC])
        bo_b = sb("bo_b", [P, P])
        zero = sb("zero", [P, 1024])

        x = [sb(f"x{u}", [P, NT, P]) for u in range(2)]
        xres = [sb(f"xres{u}", [P, NT, P]) for u in range(2)]
        xn, xnT = sb("xn", [P, NT, P]), sb("xnT", [P, SUP])
        bst, mv = sb("bst", [P, NT, 6]), sb("mv", [P, NT, 2])
        veps, rstd = sb("veps", [P, NT]), sb("rstd", [P, NT])
        qT = [sb(f"qT{u}", [P, NC, SUP]) for u in range(2)]
        th = [sb(f"th{u}", [P, NC, SUP]) for u in range(2)]
        vT = [sb(f"vT{u}", [P, NC, SUP]) for u in range(2)]
        qk = sb("qk", [P, NC, SUP])
        st, g = sb("st", [P, NC, SUP]), sb("g", [P, NC, SUP])
        sc = sb("sc", [P, SUP])
        mx, e8, sm, r8 = sb("mx", [P, NT]), sb("e8", [P, NT, 8]), sb("sm", [P, NT]), sb("r8", [P, NT])
        res = sb("res", [P, NT, 8])
        a3 = sb("a3", [P, NT, 32], BF16)
        a3T = sb("a3T", [32, SUP], BF16)
        o = sb("o", [P, NT, P])
        obst, omv = sb("obst", [P, NT, 6]), sb("omv", [P, NT, 2])
        oveps, orstd = sb("oveps", [P, NT]), sb("orstd", [P, NT])
        y = [sb(f"y{u}", [P, NT, P]) for u in range(2)]

        pT = ps("pT", [P, SUP])
        pP = [ps(f"pP{n}", [P, SUP]) for n in range(4)]
        pS = ps("pS", [P, SUP])
        pA = ps("pA", [P, SUP])
        pA3 = ps("pA3", [P, 2 * SUP], BF16)

        consts = sem("consts")
        x_loaded = [sem(f"x_loaded{u}") for u in range(2)]
        stored = sem("stored")
        cleared = sem("cleared")
        memsets, coef_act, coef_dve = sem("memsets"), sem("coef_act"), sem("coef_dve")
        bo_done = sem("bo_done")
        dve_passed, pool_passed = sem("dve_passed"), sem("pool_passed")
        set_c, in_c, out_c, dve_c, pool_c = (sem(x) for x in ("set_c", "in_c", "out_c", "dve_c", "pool_c"))
        veps_ready, rstd_ready, xn_ready = sem("veps_ready"), sem("rstd_ready"), sem("xn_ready")
        xT_done, xnT_ready = sem("xT_done"), sem("xnT_ready")
        proj_done = sem("proj_done")
        q_ready, tanh_ready, v_ready = sem("q_ready"), sem("tanh_ready"), sem("v_ready")
        qk_ready = sem("qk_ready")
        sc_done, sc_copied, scT_done = sem("sc_done"), sem("sc_copied"), sem("scT_done")
        e_shifted, e_done, a3_ready = sem("e_shifted"), sem("e_done"), sem("a3_ready")
        a3T_done, a3T_copied, bc_done = sem("a3T_done"), sem("a3T_copied"), sem("bc_done")
        u_ready, st_ready, gated_ready, g_ready = (sem(x) for x in ("u_ready", "st_ready", "gated_ready", "g_ready"))
        wo_done, o_copied = sem("wo_done"), sem("o_copied")
        oveps_ready, orstd_ready = sem("oveps_ready"), sem("orstd_ready")
        xres_ready, y_ready = sem("xres_ready"), sem("y_ready")

        xv = x_in.rearrange("(s t p) d -> s p t d", t=NT, p=P)
        ov = x_out.rearrange("(s t p) d -> s p t d", t=NT, p=P)
        NCONST = 12

        def each_step(eng, step):
            step(0, 0, first=True)
            step(0, 1)
            step(0, 2)
            with eng.Fori(0, (NS - 4) // 2) as i:
                step(i, 3)
                step(i, 4)
            step((NS - 4) // 2, 3, last=True)

        with nc.Block() as block:
            @block.sync
            def _(sp):
                sp.dma_start(x[0][:], xv[0]).then_inc(x_loaded[0], 16)
                for dst, src in ((ident, T["ident"]), (ident_bf, T["ident_bf"].bitcast(BF16)), (wq, T["L0_attn_Wq"]), (wk, T["L0_attn_Wk"]), (wv, T["L0_attn_Wv"]),
                                 (cols, T["a_cols"]), (headsel, T["headsel"]), (sel3, T["sel3"].bitcast(BF16)),
                                 (wo, T["L0_attn_Wo"].rearrange("(c p) n -> p c n", p=P)),
                                 (rows, T["L0_attn_bo"].rearrange("(a n) -> a n", a=1)),
                                 (lns, T["L0_attn_ln_scale"].partition_broadcast(P)),
                                 (lnb, T["L0_attn_ln_bias"].partition_broadcast(P))):
                    sp.dma_start(dst[:], src).then_inc(consts, 16)

                def step(i, r, first=False, last=False):
                    s, u = 2 * i + r, r % 2
                    if not last:
                        if not first:
                            sp.wait_ge(xres_ready, s)
                        sp.dma_start(x[1 - u][:], xv[s + 1]).then_inc(x_loaded[1 - u], 16)

                each_step(sp, step)

            @block.vector
            def _(dve):
                ch_set, ch, ch_in, ch_out = (Chain(dve, x, dve_passed) for x in (set_c, dve_c, in_c, out_c))
                dve.memset(halves[:], 0.5)
                dve.memset(one_row[:], 1.0)
                dve.memset(zero[:], 0.0)
                dve.memset(mhalf[:], -0.5)
                dve.memset(a3[:], 0.0).then_inc(memsets, 1)
                dve.wait_ge(coef_act, 1)
                dve.tensor_scalar(decay[:], th_a[:], 0.5, 0.5, ALU.mult, ALU.add)
                ch_set.step(dve.tensor_scalar(omd[:], th_a[:], -1.0, 1.0, ALU.mult, ALU.add))
                dve.tensor_tensor(bvs[:], omd[:], cols[:, 2, :], ALU.mult)
                ch_set.step(dve.tensor_scalar(augh[:], cols[:, 4, :], 0.5, None, ALU.mult))
                dve.tensor_tensor(augb[:], augh[:], cols[:, 0, :], ALU.mult).then_inc(coef_dve, 1)
                dve.tensor_scalar(wo_h[:], wo[:], 0.5, None, ALU.mult)
                dve.wait_ge(bo_done, 1)
                dve.tensor_copy(bo_b[:], pS[:, 0:P]).then_inc(coef_dve, 1)
                dve.wait_ge(coef_dve, 2)

                def statistics_in(i, r):
                    s, u = 2 * i + r, r % 2
                    ch_in.start(2 * s)
                    dve.wait_ge(x_loaded[u], 16 * (i + r // 2) + 16)
                    for t in range(NT):
                        last = dve.bn_stats(bst[:, t, :], x[u][:, t, :])
                    ch_in.step(last, own_wait=True)
                    for t in range(NT):
                        last = dve.bn_aggr(mv[:, t, :], bst[:, t, :])
                    ch_in.step(last)
                    dve.tensor_scalar(veps[:], mv[:, :, 1], LN_EPS, None, ALU.add).then_inc(veps_ready, 1)

                def normalise_in(i, r, first=False):
                    s, u = 2 * i + r, r % 2
                    dve.wait_ge(rstd_ready, s + 1)
                    if not first:
                        dve.wait_ge(xT_done, s)
                    for t in range(NT):
                        last = dve.tensor_scalar(xn[:, t, :], x[u][:, t, :], mv[:, t, 0:1], rstd[:, t:t + 1],
                                                 ALU.subtract, ALU.mult)
                    last.then_inc(xn_ready, 1)

                def statistics_out(i, r):
                    s, u = 2 * i + r, r % 2
                    ch_out.start(4 * s)
                    dve.wait_ge(wo_done, s + 1)
                    dve.tensor_tensor(o[:], pS[:].rearrange("p (t n) -> p t n", t=NT),
                                      bo_b[:].unsqueeze(1).to_broadcast([P, NT, P]), ALU.add).then_inc(o_copied, 1)
                    dve.wait_ge(o_copied, s + 1)
                    for t in range(NT):
                        last = dve.bn_stats(obst[:, t, :], o[:, t, :])
                    ch_out.step(last, own_wait=True)
                    for t in range(NT):
                        last = dve.bn_aggr(omv[:, t, :], obst[:, t, :])
                    ch_out.step(last)
                    dve.tensor_scalar(oveps[:], omv[:, :, 1], LN0_EPS, None, ALU.add).then_inc(oveps_ready, 1)

                def normalise_out(i, r):
                    s, u = 2 * i + r, r % 2
                    ch_out.start(4 * s + 2)
                    dve.wait_ge(orstd_ready, s + 1)
                    for t in range(NT):
                        last = dve.tensor_scalar(o[:, t, :], o[:, t, :], omv[:, t, 0:1], orstd[:, t:t + 1],
                                                 ALU.subtract, ALU.mult)
                    ch_out.step(last)
                    ch_out.step(dve.tensor_tensor(o[:], o[:], lns[:].unsqueeze(1).to_broadcast([P, NT, P]), ALU.mult))
                    dve.wait_ge(xres_ready, s + 1)
                    if r >= 1:
                        dve.wait_ge(stored, 16 * s)
                    dve.tensor_tensor(y[u][:], o[:], xres[u][:], ALU.add).then_inc(y_ready, 1)

                def step(i, r, first=False, last=False):
                    s, u = 2 * i + r, r % 2
                    for c in range(NC):
                        dve.wait_ge(proj_done, 12 * s + 3 * c + 2)
                        dve.wait_ge(q_ready, NC * s + c + 1)
                        if c == 0 and not first:
                            dve.wait_ge(sc_done, s)
                        dve.scalar_tensor_tensor(qk[:, c, :], pP[(3 * c + 1) % 4][:], cols[:, 1, c:c + 1], qT[u][:, c, :],
                                                 ALU.add, ALU.mult).then_inc(qk_ready, 1)
                        if c == 2 and not last:
                            normalise_in(i, r + 1)
                        if not first:
                            recurrence(i, r - 1, c)
                        if c == 0 and not last:
                            statistics_in(i, r + 1)
                        if c == 1 and r >= 2:
                            statistics_out(i, r - 2)
                        if c == 2 and r >= 2:
                            normalise_out(i, r - 2)
                    ch.start(8 * s)
                    dve.wait_ge(scT_done, s + 1)
                    scv = pA[:].rearrange("p (t c r) -> p t c r", t=NT, c=NC)[:, :, :, 0:2]
                    e4 = e8[:].rearrange("p t (c r) -> p t c r", r=2)
                    ch.step(dve.tensor_reduce(mx[:], scv, AX.XY, ALU.max))
                    dve.tensor_tensor(e4, scv, mx[:].unsqueeze(2).unsqueeze(3).to_broadcast([P, NT, NC, 2]),
                                      ALU.subtract).then_inc(e_shifted, 1)
                    dve.wait_ge(e_done, s + 1)
                    ch.step(dve.tensor_reduce(sm[:], e8[:], AX.X, ALU.add))
                    ch.step(dve.reciprocal(r8[:], sm[:]))
                    ch.step(dve.tensor_tensor(res[:], e8[:], r8[:].unsqueeze(2).to_broadcast([P, NT, 8]), ALU.mult))
                    if not first:
                        dve.wait_ge(a3T_done, s)
                    split3(dve, ch, res[:], [a3[:, :, 8 * k:8 * k + 8] for k in range(3)], a3_ready)
                    for c in range(NC):
                        dve.wait_ge(bc_done, NC * s + c + 1)
                        dve.wait_ge(v_ready, NC * s + c + 1)
                        dve.tensor_tensor(vT[u][:, c, :], pP[c][:], vT[u][:, c, :], ALU.mult).then_inc(u_ready, 1)

                def recurrence(i, r, c):
                    s, u = 2 * i + r, r % 2
                    dve.wait_ge(u_ready, NC * s + c + 1)
                    if r >= 1:
                        dve.wait_ge(gated_ready, NC * (s - 1) + c + 1)
                    for b in range(2):
                        w = slice(b * SEQ, (b + 1) * SEQ)
                        last_i = dve.tensor_tensor_scan(st[:, c, w], decay[:, c:c + 1].to_broadcast([P, SEQ]),
                                                        vT[u][:, c, w], 0.0, ALU.mult, ALU.add)
                    last_i.then_inc(st_ready, 1)
                    dve.wait_ge(st_ready, NC * s + c + 1)
                    dve.tensor_tensor(qT[u][:, c, :], qT[u][:, c, :], st[:, c, :], ALU.mult).then_inc(gated_ready, 1)

                statistics_in(0, 0)
                normalise_in(0, 0, first=True)
                each_step(dve, step)
                statistics_out((NS - 2) // 2, (NS - 2) % 2)
                normalise_out((NS - 2) // 2, (NS - 2) % 2)
                for c in range(NC):
                    recurrence((NS - 1) // 2, (NS - 1) % 2, c)
                statistics_out((NS - 1) // 2, (NS - 1) % 2)
                normalise_out((NS - 1) // 2, (NS - 1) % 2)

            @block.scalar
            def _(act):
                act.wait_ge(consts, 16 * NCONST)
                act.activation(th_a[:], cols[:, 3, :], ACT.Tanh, scale=0.5).then_inc(coef_act, 1)
                act.wait_ge(memsets, 1)
                for t in clear:
                    act.dma_start(t.rearrange("(p n) d -> p (n d)", p=P).rearrange("p (n c) -> p n c", c=1024),
                                  zero[:].unsqueeze(1).to_broadcast([P, t.shape[0] * P // P // 1024, 1024])
                                  ).then_inc(cleared, 16)
                act.wait_ge(coef_dve, 1)

                def copy_xnT(s, first=False):
                    act.wait_ge(xT_done, s + 1)
                    act.activation(xnT[:], pT[:], ACT.Copy).then_inc(xnT_ready, 1)

                def step(i, r, first=False, last=False):
                    s, u = 2 * i + r, r % 2
                    for c in range(NC):
                        act.wait_ge(proj_done, 12 * s + 3 * c + 1)
                        q_ps = pP[(3 * c) % 4]
                        if c == 0 and r >= 2:
                            act.wait_ge(g_ready, NC * (s - 1))
                        act.activation(qT[u][:, c, :], q_ps[:], ACT.Identity, bias=cols[:, 0, c:c + 1]).then_inc(q_ready, 1)
                        act.activation(th[u][:, c, :], q_ps[:], ACT.Tanh, scale=augh[:, c:c + 1],
                                       bias=augb[:, c:c + 1]).then_inc(tanh_ready, 1)
                        act.wait_ge(proj_done, 12 * s + 3 * c + 3)
                        act.activation(vT[u][:, c, :], pP[(3 * c + 2) % 4][:], ACT.Identity, scale=omd[:, c:c + 1],
                                       bias=bvs[:, c:c + 1]).then_inc(v_ready, 1)
                    act.wait_ge(sc_done, s + 1)
                    act.activation(sc[:], pS[:], ACT.Copy).then_inc(sc_copied, 1)
                    if not last:
                        copy_xnT(s + 1)
                    act.wait_ge(e_shifted, s + 1)
                    act.activation(e8[:], e8[:], ACT.Exp, scale=0.125).then_inc(e_done, 1)
                    act.wait_ge(a3T_done, s + 1)
                    act.activation(a3T[:], pA3[0:32, 0:SUP], ACT.Copy).then_inc(a3T_copied, 1)
                    if r >= 2:
                        store(s - 2, u)

                def store(s, u):
                    act.wait_ge(y_ready, s + 1)
                    act.dma_start(ov[s], y[u][:]).then_inc(stored, 16)

                copy_xnT(0)
                each_step(act, step)
                store(NS - 2, (NS - 2) % 2)
                store(NS - 1, (NS - 1) % 2)
                act.wait_ge(stored, 16 * NS)
                if clear:
                    act.wait_ge(cleared, 16 * len(clear))

            @block.tensor
            def _(pe):
                pe.wait_ge(consts, 16 * NCONST)
                pe.wait_ge(memsets, 1)
                for c in range(NC):
                    pe.matmul(pS[:, 0:P], halves[:], wo[:, c, :], start=(c == 0), stop=False)
                pe.matmul(pS[:, 0:P], one_row[:], rows[:], start=False, stop=True).then_inc(bo_done, 1)

                def transpose_x(s, first=False):
                    pe.wait_ge(xn_ready, s + 1)
                    if not first:
                        pe.wait_ge(xnT_ready, s)
                    for t in range(NT):
                        last = pe.transpose(pT[:, t * P:(t + 1) * P], xn[:, t, :], ident[:])
                    last.then_inc(xT_done, 1)

                def out_proj(s, tiles):
                    if tiles[0] == 0:
                        pe.wait_ge(g_ready, NC * s + NC)
                    for t in tiles:
                        for c in range(NC):
                            last = pe.matmul(pS[:, t * P:(t + 1) * P], g[:, c, t * P:(t + 1) * P], wo_h[:, c, :],
                                             start=(c == 0), stop=(c == NC - 1))
                    if tiles[-1] == NT - 1:
                        last.then_inc(wo_done, 1)

                def step(i, r, first=False, last=False):
                    s, u = 2 * i + r, r % 2
                    pe.wait_ge(xnT_ready, s + 1)
                    for c in range(NC):
                        for j, w in enumerate((wq, wk, wv)):
                            n = 3 * c + j
                            m = n - 4
                            if m >= 0:
                                pe.wait_ge((tanh_ready, qk_ready, v_ready)[m % 3], NC * s + m // 3 + 1)
                            elif not first:
                                pe.wait_ge(u_ready, NC * (s - 1) + n + 1)
                            pe.matmul(pP[n % 4][:], w[:, c * P:(c + 1) * P], xnT[:], start=True, stop=True).then_inc(proj_done, 1)
                    if not last:
                        transpose_x(s + 1)
                    if first:
                        pe.wait_ge(coef_dve, 2)
                    if r >= 2:
                        pe.wait_ge(o_copied, s - 1)
                    for c in range(NC):
                        pe.wait_ge(qk_ready, NC * s + c + 1)
                        last_i = pe.matmul(pS[32 * c:32 * c + 32, :], headsel[:], qk[:, c, :], start=True, stop=True)
                    last_i.then_inc(sc_done, 1)
                    pe.wait_ge(sc_copied, s + 1)
                    if not first:
                        pe.wait_ge(e_shifted, s)
                    for t in range(NT):
                        last_i = pe.transpose(pA[:, t * P:(t + 1) * P], sc[:, t * P:(t + 1) * P], ident[:])
                    last_i.then_inc(scT_done, 1)
                    if not first:
                        out_proj(s - 1, (0, 1))
                    pe.wait_ge(a3_ready, s + 1)
                    if not first:
                        pe.wait_ge(a3T_copied, s)
                    for t in range(NT):
                        last_i = pe.transpose(pA3[0:32, t * P:(t + 1) * P], a3[:, t, :], ident_bf[:])
                    last_i.then_inc(a3T_done, 1)
                    if not first:
                        out_proj(s - 1, (2,))
                    pe.wait_ge(a3T_copied, s + 1)
                    for c in range(NC):
                        m = 12 + c - 4
                        pe.wait_ge((tanh_ready, qk_ready, v_ready)[m % 3], NC * s + m // 3 + 1)
                        pe.matmul(pP[c][:], sel3[:, c, :], a3T[:], start=True, stop=True).then_inc(bc_done, 1)
                    if not first:
                        out_proj(s - 1, (3,))

                transpose_x(0, first=True)
                each_step(pe, step)
                pe.wait_ge(sc_copied, NS)
                pe.wait_ge(o_copied, NS - 1)
                out_proj(NS - 1, range(NT))

            @block.gpsimd
            def _(pool):
                pool.wait_ge(memsets, 1)

                def rsqrt_in(s):
                    pool.wait_ge(veps_ready, s + 1)
                    pool.tensor_tensor(rstd[:], veps[:], mhalf[:].to_broadcast([P, NT]), ALU.pow).then_inc(rstd_ready, 1)

                def rsqrt_out(s):
                    pool.wait_ge(oveps_ready, s + 1)
                    pool.tensor_tensor(orstd[:], oveps[:], mhalf[:].to_broadcast([P, NT]), ALU.pow).then_inc(orstd_ready, 1)

                def residual(i, r):
                    s, u = 2 * i + r, r % 2
                    pool.wait_ge(x_loaded[u], 16 * (i + r // 2) + 16)
                    if r >= 2:
                        pool.wait_ge(y_ready, s - 1)
                    pool.tensor_tensor(xres[u][:], x[u][:], lnb[:].unsqueeze(1).to_broadcast([P, NT, P]),
                                       ALU.add).then_inc(xres_ready, 1)

                def gate(s, u, c, first=False):
                    pool.wait_ge(gated_ready, NC * s + c + 1)
                    pool.wait_ge(tanh_ready, NC * s + c + 1)
                    if not first:
                        pool.wait_ge(wo_done, s)
                    pool.tensor_tensor(g[:, c, :], th[u][:, c, :], qT[u][:, c, :], ALU.add).then_inc(g_ready, 1)

                def step(i, r, first=False, last=False):
                    s, u = 2 * i + r, r % 2
                    for c in range(NC):
                        if not first:
                            gate(s - 1, 1 - u, c, first=(r == 1 and isinstance(i, int) and i == 0))
                        if c == 0 and not last:
                            rsqrt_in(s + 1)
                        if c == 1 and r >= 2:
                            rsqrt_out(s - 2)
                        if c == 2:
                            residual(i, r)

                pool.wait_ge(consts, 16 * NCONST)
                rsqrt_in(0)
                each_step(pool, step)
                rsqrt_out(NS - 2)
                for c in range(NC):
                    gate(NS - 1, (NS - 1) % 2, c)
                rsqrt_out(NS - 1)


def split3(dve, ch, res, parts, ready):
    ch.step(dve.tensor_copy(parts[0], res))
    ch.step(dve.tensor_tensor(res, res, parts[0], ALU.subtract))
    ch.step(dve.tensor_copy(parts[1], res))
    ch.step(dve.tensor_tensor(res, res, parts[1], ALU.subtract))
    dve.tensor_copy(parts[2], res).then_inc(ready, 1)



NT = SUP // P
NS = TOK // SUP
TOPK = 2
QUAD = 4


def span(eng, lo, hi, fn, least=2):
    q = lo
    while q < hi and (q < least or q % 2):
        fn(q, q % 2, q // 2)
        q += 1
    pairs = (hi - q) // 2
    if pairs > 1:
        with eng.Fori(0, pairs) as i:
            fn(2 * i + q, 0, i + q // 2)
            fn(2 * i + q + 1, 1, i + q // 2)
        q += 2 * pairs
    for q in range(q, hi):
        fn(q, q % 2, q // 2)


def from_step(q, n):
    return not isinstance(q, int) or q >= n


MIXTURES = ((1, 8), (2, 32))


def blocks_of(layer):
    return -(-(TOPK * TOK + MIXTURES[layer][1] * (P - 1)) // P // QUAD) * QUAD


def row_space(nc, layer):
    return [nc.dram_tensor(f"rows{g}_layer{layer}", [blocks_of(layer) * P, P], F32, kind="Internal").ap()
            for g in range(MIXTURES[layer][0])]


def expert_mixture(nc, T, x_in, x_out, xg, layer):
    G, E = MIXTURES[layer]
    GE = G * E
    NBLK = blocks_of(layer)
    NQG = NBLK // QUAD
    NQ = G * NQG
    TE = NS * NT * E
    new = lambda name, rows: nc.dram_tensor(f"{name}_layer{layer}", [rows, P], F32, kind="Internal").ap()
    yg = [new(f"results{g}", NBLK * P) for g in range(G)]
    xn_d = new("normed", TOK)
    with Scope(nc, "bd"[layer]) as S:
        sb, ps, sem = S.sb, S.ps, S.sem
        ident = sb("ident", [P, P])
        mhalf = sb("mhalf", [P, 1])
        bank = [ps(f"bank{n}", [P, 512]) for n in range(8)]

        best = sb("best", [P, G, NS, TOPK, NT])
        pick = sb("pick", [P, G, NS, TOPK, NT])
        wgt = sb("wgt", [P, G, NS, TOPK, NT])
        dest = sb("dest", [P, G, NS, TOPK, NT], U32)
        total = sb("total", [P, NS, G, NT])
        OWNER_AT = QUAD - 1 if layer == 0 else 0
        owner = sb("owner", [1, G * NBLK + 2 * QUAD], I32)

        xnT_all = sb("xnT_all", [P, TOK]) if layer == 0 else None

        router = sb("router", [P, GE])
        if layer == 0:
            HID, W2_AT, B1_AT, B2_AT, WCOLS = 512, 512, 1024, 1028, 1028 + P
            sw1, sw2 = sb("sw1", [P, 512]), sb("sw2", [P, 4, P])
            sb1, sb2 = sb("sb1", [P, 4]), sb("sb2", [P, P])
            loads = [(router, T["m_gate"]),
                     (sw1, T["L0_ffn_sW1"]), (sw2, T["L0_ffn_sW2"].rearrange("(c p) h -> p c h", p=P)),
                     (sb1, T["m_sb1"]), (sb2, T["L0_ffn_sb2"].partition_broadcast(P))]
        else:
            WCOLS = 2 * P
            loads = [(router, T["m_router"])]
        all_w = sb("all_w", [P, GE, WCOLS])
        if layer == 0:
            expert_weights = [(all_w[:, :, 0:HID], T["L0_ffn_W1"].rearrange("e p f -> p e f")),
                              (all_w[:, :, W2_AT:B1_AT], T["m_w2"]), (all_w[:, :, B1_AT:B2_AT], T["m_b1"]),
                              (all_w[:, :, B2_AT:WCOLS], T["L0_ffn_b2"].partition_broadcast(P))]
        else:
            expert_weights = [(all_w[:], T["m_w"])]
        iota, before = sb("iota", [P, P]), sb("before", [P, P], BF16)
        loads += [(iota, T["m_iota"].partition_broadcast(P)), (before, T["m_before"].bitcast(BF16))]

        consts = sem("consts")
        weights = sem("weights")
        memset = sem("memset")
        dve_passed, pool_passed = sem("dve_passed"), sem("pool_passed")
        x_loaded = [sem(f"x_loaded{u}") for u in range(2)]
        normed_stored = [sem(f"normed_stored{u}") for u in range(2)]

        with Scope(nc, "bd"[layer] + "r") as R:
            x = [R.sb(f"x{u}", [P, NT, P]) for u in range(2)]
            xn = [R.sb(f"xn{u}", [P, NT, P]) for u in range(2)]
            bst, mv = R.sb("bst", [P, NT, 6]), R.sb("mv", [P, NT, 2])
            veps, rstd = R.sb("veps", [P, NT]), R.sb("rstd", [P, NT])
            xnT = [R.sb(f"xnT{u}", [P, SUP]) for u in range(2)]
            lg, ex = R.sb("lg", [P, NT, G, E]), R.sb("ex", [P, NT, G, E])
            m8, i8 = R.sb("m8", [P, G, NT, 8]), R.sb("i8", [P, G, NT, 8], U32)
            sm = R.sb("sm", [P, G, NT])
            pT, pL = bank[0], bank[1]
            ln_c, top_c = R.sem("ln_c"), R.sem("top_c")
            veps_ready, rstd_ready, xn_ready = R.sem("veps_ready"), R.sem("rstd_ready"), R.sem("xn_ready")
            xT_done, xnT_ready, lg_done = R.sem("xT_done"), R.sem("xnT_ready"), R.sem("lg_done")
            lg_shifted, ex_ready = R.sem("lg_shifted"), R.sem("ex_ready")
            xv = x_in.rearrange("(s t p) d -> s p t d", t=NT, p=P)
            nv = xn_d.rearrange("(s t p) d -> s p t d", t=NT, p=P)

            with nc.Block() as block:
                @block.sync
                def _(sp):
                    sp.dma_start(x[0][:], xv[0]).then_inc(x_loaded[0], 16)
                    for dst, src in [(ident, T["ident"])] + loads:
                        sp.dma_start(dst[:], src).then_inc(consts, 16)

                    def step(s, u, h):
                        if not isinstance(s, int) or s + 1 < NS:
                            if from_step(s, 1):
                                sp.wait_ge(xn_ready, s)
                            sp.dma_start(x[1 - u][:], xv[s + 1]).then_inc(x_loaded[1 - u], 16)
                        sp.wait_ge(xn_ready, s + 1)
                        sp.dma_start(nv[s], xn[u][:]).then_inc(normed_stored[u], 16)

                    span(sp, 0, NS - 1, step)
                    step(NS - 1, (NS - 1) % 2, (NS - 1) // 2)
                    for u in range(2):
                        sp.wait_ge(normed_stored[u], 16 * NS // 2)

                @block.scalar
                def _(act):
                    for dst, src in expert_weights:
                        act.dma_start(dst, src).then_inc(weights, 16)
                    act.wait_ge(consts, 16 * (len(loads) + 1))

                    def step(s, u, h):
                        act.wait_ge(xT_done, s + 1)
                        if layer == 0:
                            act.copy(xnT_all[:, bass.ds(SUP * s, SUP)], pT[:])
                        act.copy(xnT[u][:], pT[:]).then_inc(xnT_ready, 1)
                        if layer == 1:
                            act.wait_ge(lg_shifted, s + 1)
                            act.activation(ex[:], lg[:], ACT.Exp).then_inc(ex_ready, 1)

                    span(act, 0, NS, step)

                @block.tensor
                def _(pe):
                    pe.wait_ge(consts, 16 * (len(loads) + 1))

                    def step(s, u, h):
                        pe.wait_ge(xn_ready, s + 1)
                        for t in range(NT):
                            last = pe.transpose(pT[:, t * P:(t + 1) * P], xn[u][:, t, :], ident[:])
                        last.then_inc(xT_done, 1)
                        pe.wait_ge(xnT_ready, s + 1)
                        if from_step(s, 1):
                            pe.wait_ge(lg_shifted, s)
                        for t in range(NT):
                            last = pe.matmul(pL[:, t * GE:(t + 1) * GE], xnT[u][:, t * P:(t + 1) * P], router[:],
                                             start=True, stop=True)
                        last.then_inc(lg_done, 1)

                    span(pe, 0, NS, step)

                @block.vector
                def _(dve):
                    ln, top = Chain(dve, ln_c, dve_passed), Chain(dve, top_c, dve_passed)
                    dve.memset(mhalf[:], -0.5).then_inc(memset, 1)
                    dve.wait_ge(consts, 16 * (len(loads) + 1))

                    def statistics(s, u, h):
                        ln.start(2 * s)
                        dve.wait_ge(x_loaded[u], 16 * h + 16)
                        for t in range(NT):
                            last = dve.bn_stats(bst[:, t, :], x[u][:, t, :])
                        ln.step(last, own_wait=True)
                        for t in range(NT):
                            last = dve.bn_aggr(mv[:, t, :], bst[:, t, :])
                        ln.step(last)
                        dve.tensor_scalar(veps[:], mv[:, :, 1], LN_EPS, None, ALU.add).then_inc(veps_ready, 1)
                    def normalise(s, u, h):
                        dve.wait_ge(rstd_ready, s + 1)
                        if from_step(s, 2):
                            dve.wait_ge(normed_stored[u], 16 * h)
                            dve.wait_ge(xT_done, s - 1)
                        for t in range(NT):
                            last = dve.tensor_scalar(xn[u][:, t, :], x[u][:, t, :], mv[:, t, 0:1], rstd[:, t:t + 1],
                                                     ALU.subtract, ALU.mult)
                        last.then_inc(xn_ready, 1)

                    nsteps = 3 if layer == 0 else 4

                    def choose(s, u, h):
                        top.start(nsteps * s)
                        dve.wait_ge(lg_done, s + 1)
                        if layer == 1 and from_step(s, 1):
                            dve.wait_ge(ex_ready, s)
                        top.step(dve.tensor_copy(lg[:].rearrange("p t g e -> p (t g e)"), pL[:, 0:NT * GE]), own_wait=True)
                        for g in range(G):
                            for t in range(NT):
                                last = dve.max(m8[:, g, t, :], lg[:, t, g, :])
                        top.step(last, own_wait=True)
                        for g in range(G):
                            for t in range(NT):
                                last = dve.max_index(i8[:, g, t, :], m8[:, g, t, :], lg[:, t, g, :])
                        top.step(last)
                        for g in range(G):
                            dve.tensor_copy(pick[:, g].rearrange("p s k t -> p (s k) t")[:, bass.ds(2 * s, 2), :],
                                            i8[:, g, :, 0:2].rearrange("p t k -> p k t"))
                            last = dve.tensor_copy(best[:, g].rearrange("p s k t -> p (s k) t")[:, bass.ds(2 * s, 2), :],
                                                   m8[:, g, :, 0:2].rearrange("p t k -> p k t"))
                        if layer == 0:
                            last.then_inc(lg_shifted, 1)
                        else:
                            for g in range(G):
                                last = dve.tensor_tensor(lg[:, :, g, :], lg[:, :, g, :],
                                                         m8[:, g, :, 0:1].to_broadcast([P, NT, E]), ALU.subtract)
                            last.then_inc(lg_shifted, 1)

                    def add_up(s):
                        top.start(nsteps * s + nsteps - 1)
                        dve.wait_ge(ex_ready, s + 1)
                        top.step(dve.tensor_reduce(sm[:].rearrange("p g t -> p t g"), ex[:], AX.X, ALU.add))
                        dve.tensor_copy(total[:].rearrange("p s g t -> p s (g t)")[:, bass.ds(s, 1), :],
                                        sm[:].rearrange("p g t -> p (g t)").unsqueeze(1))

                    statistics(0, 0, 0)
                    normalise(0, 0, 0)

                    def step(s, u, h):
                        more = not isinstance(s, int) or s + 1 < NS
                        if more:
                            statistics(s + 1, 1 - u, h + u)
                        if layer == 1 and from_step(s, 1):
                            add_up(s - 1)
                        if more:
                            normalise(s + 1, 1 - u, h + u)
                        choose(s, u, h)

                    span(dve, 0, NS - 1, step)
                    step(NS - 1, (NS - 1) % 2, (NS - 1) // 2)
                    if layer == 1:
                        add_up(NS - 1)

                @block.gpsimd
                def _(pool):
                    pool.wait_ge(memset, 1)

                    def step(s, u, h):
                        pool.wait_ge(veps_ready, s + 1)
                        pool.tensor_tensor(rstd[:], veps[:], mhalf[:].to_broadcast([P, NT]), ALU.pow).then_inc(rstd_ready, 1)

                    span(pool, 0, NS, step)

        with Scope(nc, "bd"[layer] + "e") as R:
            ones = R.sb("ones", [P, P], BF16)
            NTL = NS * NT
            oh = [R.sb(f"oh{k}", [P, NS, NT, E]) for k in range(TOPK)]
            both = R.sb("both", [P, NTL * E], BF16)
            tot, run = R.sb("tot", [P, E, NTL]), R.sb("run", [P, E, NTL])
            keep = R.sb("keep", [P, E, NTL])
            one_e = R.sb("one_e", [P, E])
            nbi, nb = R.sb("nbi", [P, E], I32), R.sb("nb", [P, E])
            end, start = R.sb("end", [P, E]), R.sb("start", [P, E])
            pos = R.sb("pos", [P, NS, NT, E])
            place = R.sb("place", [P, NS, TOPK, NT])
            cmp, own = R.sb("cmp", [1, NBLK, E]), R.sb("own", [1, NBLK])
            dif, den = R.sb("dif", [P, G, NS, TOPK, NT]), R.sb("den", [P, G, NS, NT])
            route_c = R.sem("route_c")
            placed = R.sem("placed")
            routed = R.sem("routed")
            keep_c = R.sem("keep_c")
            both_ready, ranks_done, w_sub, w_exp = R.sem("both_ready"), R.sem("ranks_done"), R.sem("w_sub"), R.sem("w_exp")
            NB = -(-TE // 512)
            W = TE // NB
            rank_b, tot_b = bank[0:NB], bank[2:2 + NB]

            xs = R.sb("xs", [P, NS * NT, P])
            got = [R.sb(f"got{u}", [P, TOPK, NT, P]) for u in range(2)]
            got_first = [xs, R.sb("got_first", [P, NS * NT, P])] if G > 1 else None
            total_out = R.sb("total_out", [P, NS * NT, P])
            xq = [R.sb(f"xq{u}", [P, QUAD, P]) for u in range(2)]
            xqT = [R.sb(f"xqT{u}", [P, QUAD * P]) for u in range(2)]
            yq = [R.sb(f"yq{u}", [P, QUAD, P]) for u in range(2)]
            pX, pY = bank[0:2], bank[2:4]
            if layer == 0:
                wx = [R.sb(f"wx{n}", [P, WCOLS]) for n in range(QUAD)]
                hx = [R.sb(f"hx{n}", [P, 4, P]) for n in range(QUAD)]
                pHx = bank[4:8]
                hs = [[R.sb(f"hs{u}{c}", [P, SUP]) for c in range(4)] for u in range(2)]
                pHs, pO = bank[4:8], bank[3]
                out_done = R.sem("out_done")
                sh_done, sh_ready, so_done, so_added, so_c = (
                    R.sem(n) for n in ("sh_done", "sh_ready", "so_done", "so_added", "so_c"))
            else:
                wgu = [R.sb(f"wgu{u}", [P, QUAD, P]) for u in range(2)]
                wd = [R.sb(f"wd{u}", [64, QUAD, P]) for u in range(2)]
                gs = [R.sb(f"gs{u}", [64, QUAD * P]) for u in range(2)]
                hx = [R.sb(f"hx{u}", [64, QUAD * P]) for u in range(2)]
                pG, pU = bank[4:6], bank[6:8]

            two = lambda name: [R.sem(f"{name}{u}") for u in range(2)]
            xs_loaded, x_loaded_all, stored = R.sem("xs_loaded"), R.sem("x_loaded_all"), R.sem("stored")
            scattered = [R.sem(f"scattered{g}") for g in range(G)]
            gathered, first_gathered = two("gathered"), R.sem("first_gathered")
            dve_sum_c, added = R.sem("dve_sum_c"), R.sem("added")
            xq_loaded, results_stored = two("xq_loaded"), two("results_stored")
            xqT_done, xqT_ready, w_ready, h_done, g_ready, h_ready, y_done, y_ready = (
                R.sem(n) for n in ("xqT_done", "xqT_ready", "w_ready", "hx_done", "g_ready", "hx_ready", "y_done", "y_ready"))
            nv = xn_d.rearrange("(s t p) d -> s p t d", t=NT, p=P)
            outv = x_out.rearrange("(s t p) d -> s p t d", t=NT, p=P)

            with nc.Block() as block:
                @block.gpsimd
                def _(pool):
                    def scatter(g):
                        for s in range(NS):
                            for k in range(TOPK):
                                for t in range(NT):
                                    pool.indirect_dma_start(
                                        xg[g], bass.IndirectOffsetOnAxis(ap=dest[:, g, s, k, t:t + 1], axis=0),
                                        xs[:, s * NT + t, :], None).then_inc(scattered[g], 16)

                    def gather(g, s):
                        for k in range(TOPK):
                            for t in range(NT):
                                last = g == G - 1
                                pool.indirect_dma_start(
                                    got[s % 2][:, k, t, :] if last else got_first[k][:, s * NT + t, :], None, yg[g],
                                    bass.IndirectOffsetOnAxis(ap=dest[:, g, s, k, t:t + 1], axis=0)
                                ).then_inc(gathered[s % 2] if last else first_gathered, 16)

                    Chain(pool, keep_c).step(pool.memset(keep[:], 1.0))
                    pool.memset(keep[:, :, 0:1], 0.0).then_inc(keep_c, 1)
                    pool.wait_ge(xs_loaded, 16)
                    for g in range(G):
                        pool.wait_ge(placed, g + 1)
                        scatter(g)
                    for g in range(G):
                        if g < G - 1:
                            for n in range(G):
                                pool.wait_ge(scattered[n], 16 * TOPK * NS * NT)
                        for u in range(2):
                            pool.wait_ge(results_stored[u], 16 * ((NQG * (g + 1) + 1 - u) // 2))
                        for s in range(NS):
                            if g == G - 1 and s >= 2:
                                pool.wait_ge(added, s - 1)
                            gather(g, s)

                @block.sync
                def _(sp):
                    rows = [t.rearrange("(n b p) d -> n p b d", b=QUAD, p=P) for t in xg]
                    def load(g, q, u):
                        if from_step(q, 2):
                            sp.wait_ge(xqT_done, q - 1)
                        sp.dma_start(xq[u][:], rows[g][q - g * NQG]).then_inc(xq_loaded[u], 16)

                    sp.dma_start(xs[:], xn_d.rearrange("(n p) d -> p n d", p=P)).then_inc(xs_loaded, 16)
                    sp.dma_start(total_out[:], x_in.rearrange("(n p) d -> p n d", p=P)).then_inc(x_loaded_all, 16)
                    for g in range(G):
                        sp.wait_ge(scattered[g], 16 * TOPK * NS * NT)
                        span(sp, g * NQG, (g + 1) * NQG, lambda q, u, h: load(g, q, u))

                    def store_final(s, u, h):
                        sp.wait_ge(added, s + 1)
                        sp.dma_start(outv[s], total_out[:, bass.ds(NT * s, NT), :]).then_inc(stored, 16)

                    span(sp, 0, NS, store_final)
                    sp.wait_ge(stored, 16 * NS)

                def owners(n):
                    return nc.values_load_multi_w_load_instructions(
                        owner[0:1, n + OWNER_AT:n + OWNER_AT + QUAD] if isinstance(n, int)
                        else owner[0:1, bass.ds(n + OWNER_AT, QUAD)],
                        engines=[mybir.EngineType.DVE], min_val=0, max_val=(GE - 1) * WCOLS,
                        skip_runtime_bounds_check_because="the expert is clamped to the last one where it is worked out")[1]

                @block.scalar
                def _(act):
                    results = [t.rearrange("(n b p) d -> n p b d", b=QUAD, p=P) for t in yg]

                    def turn(q, u):
                        act.wait_ge(xqT_done, q + 1)
                        act.copy(xqT[u][:], pX[u][:]).then_inc(xqT_ready, 1)

                    def store(q, u, g):
                        act.wait_ge(y_ready, (QUAD * q + QUAD) if layer == 0 else (q + 1))
                        act.dma_start(results[g][q - g * NQG], yq[u][:]).then_inc(results_stored[u], 16)

                    def step0(q, u, h, g):
                        for j in range(QUAD):
                            act.wait_ge(h_done, QUAD * q + j + 1)
                            if from_step(q, 1):
                                act.wait_ge(out_done, QUAD * q + j - 3)
                            for c in range(4):
                                last = act.activation(hx[j][:, c, :], pHx[j][:, c * P:(c + 1) * P], ACT.Gelu,
                                                      bias=wx[j][:, B1_AT + c:B1_AT + c + 1])
                            last.then_inc(h_ready, 1)
                            if j == 1 and (not isinstance(q, int) or q + 1 < NQ):
                                turn(q + 1, 1 - u)
                        if from_step(q, 1):
                            store(q - 1, 1 - u, g)

                    def step1(q, u, h, g):
                        if not isinstance(q, int) or q + 1 < NQ:
                            turn(q + 1, 1 - u)
                        act.wait_ge(h_done, q + 1)
                        act.activation(gs[u][:], pG[u][0:64, :], ACT.Silu).then_inc(g_ready, 1)
                        if g is not None:
                            store(q - 2, u, g)

                    act.wait_ge(w_sub, 1)
                    act.activation(dif[:], dif[:], ACT.Exp).then_inc(w_exp, 1)
                    if layer == 0:
                        def shared(s, u, h):
                            for c in range(4):
                                act.wait_ge(sh_done, 4 * s + c + 1)
                                if from_step(s, 2):
                                    act.wait_ge(so_done, s - 1)
                                act.activation(hs[u][c][:], pHs[c][:], ACT.Gelu, bias=sb1[:, c:c + 1]).then_inc(sh_ready, 1)

                        span(act, 0, NS, shared)
                    act.wait_ge(weights, 16 * len(expert_weights))
                    turn(0, 0)
                    if layer == 0:
                        span(act, 0, NQ - 1, lambda q, u, h: step0(q, u, h, 0))
                        step0(NQ - 1, (NQ - 1) % 2, 0, 0)
                        store(NQ - 1, (NQ - 1) % 2, 0)
                    else:
                        for q in range(2):
                            step1(q, q, 0, None)
                        for g in range(G):
                            span(act, g * NQG + 2, (g + 1) * NQG + (-1 if g == G - 1 else 2),
                                 lambda q, u, h: step1(q, u, h, g))
                        step1(NQ - 1, (NQ - 1) % 2, 0, G - 1)
                        for q in (NQ - 2, NQ - 1):
                            store(q, q % 2, G - 1)
                    for u in range(2):
                        act.wait_ge(results_stored[u], 16 * ((NQ + 1 - u) // 2))

                @block.vector
                def _(dve):
                    def route():
                        ch = Chain(dve, route_c)
                        dve.memset(owner[:], 0)
                        dve.memset(ones[:], 1.0)
                        dve.memset(one_e[:], 1.0)
                        dve.tensor_tensor(dif[:].rearrange("p g s k t -> p (g s) k t"),
                                          best[:].rearrange("p g s k t -> p (g s) k t"),
                                          best[:].rearrange("p g s k t -> p (g s) k t")[:, :, 0:1, :].to_broadcast(
                                              [P, G * NS, TOPK, NT]), ALU.subtract).then_inc(w_sub, 1)
                        for g in range(G):
                            for k in range(TOPK):
                                last = dve.tensor_tensor(oh[k][:].rearrange("p s t e -> p s t e"),
                                                         iota[:, 0:E].unsqueeze(1).unsqueeze(1).to_broadcast([P, NS, NT, E]),
                                                         pick[:, g, :, k, :].unsqueeze(3).to_broadcast([P, NS, NT, E]), ALU.is_equal)
                            ch.step(last)
                            dve.tensor_tensor(both[:], oh[0][:].rearrange("p s t e -> p (s t e)"),
                                              oh[1][:].rearrange("p s t e -> p (s t e)"), ALU.add).then_inc(both_ready, 1)
                            dve.wait_ge(ranks_done, g + 1)
                            dve.wait_ge(keep_c, 2)
                            ntb = NTL // NB
                            for n in range(NB):
                                last = dve.tensor_copy(tot[:, :, n * ntb:(n + 1) * ntb],
                                                       tot_b[n][:, 0:W].rearrange("p (t e) -> p e t", e=E))
                            ch.step(last)
                            ch.step(dve.tensor_tensor_scan(run[:].rearrange("p e t -> p (e t)"), keep[:].rearrange("p e t -> p (e t)"),
                                                           tot[:].rearrange("p e t -> p (e t)"), 0.0, ALU.mult, ALU.add))
                            ch.step(dve.tensor_scalar(nbi[:], run[:, :, NTL - 1], float(P - 1), None, ALU.add))
                            ch.step(dve.tensor_scalar(nbi[:], nbi[:], 7, None, ALU.logical_shift_right))
                            ch.step(dve.tensor_copy(nb[:], nbi[:]))
                            ch.step(dve.tensor_tensor_scan(end[:], one_e[:], nb[:], 0.0, ALU.mult, ALU.add))
                            ch.step(dve.tensor_tensor(start[:], end[:], nb[:], ALU.subtract))
                            ch.step(dve.scalar_tensor_tensor(run[:], start[:].unsqueeze(2).to_broadcast([P, E, NTL]), float(P),
                                                             run[:], ALU.mult, ALU.add))
                            ch.step(dve.tensor_tensor(run[:], run[:], tot[:], ALU.subtract))
                            posf = pos[:].rearrange("p s t e -> p (s t) e")
                            for n in range(NB):
                                last = dve.tensor_tensor(posf[:, n * ntb:(n + 1) * ntb, :],
                                                         rank_b[n][:, 0:W].rearrange("p (t e) -> p t e", e=E),
                                                         run[:, :, n * ntb:(n + 1) * ntb].rearrange("p e t -> p t e"), ALU.add)
                            ch.step(last)
                            for k in range(TOPK):
                                last = dve.tensor_tensor(oh[k][:], oh[k][:], pos[:], ALU.mult)
                            ch.step(last)
                            for k in range(TOPK):
                                last = dve.tensor_reduce(place[:, :, k, :], oh[k][:], AX.X, ALU.add)
                            ch.step(last)
                            dve.tensor_copy(dest[:, g], place[:]).then_inc(placed, 1)
                            ch.step(dve.tensor_tensor(cmp[:], end[0:1, :].unsqueeze(1).to_broadcast([1, NBLK, E]),
                                                      iota[0:1, 0:NBLK].unsqueeze(2).to_broadcast([1, NBLK, E]), ALU.is_le))
                            ch.step(dve.tensor_reduce(own[:], cmp[:], AX.X, ALU.add))
                            ch.step(dve.tensor_scalar(own[:], own[:], float(E - 1), float(g * E), ALU.min, ALU.add))
                            ch.step(dve.tensor_scalar(own[:], own[:], float(WCOLS), None, ALU.mult))
                            dve.tensor_copy(owner[0:1, OWNER_AT + g * NBLK:OWNER_AT + (g + 1) * NBLK], own[:]).then_inc(routed, 1)
                        dve.wait_ge(w_exp, 1)
                        if layer == 0:
                            ch.step(dve.tensor_tensor(den[:], dif[:, :, :, 0, :], dif[:, :, :, 1, :], ALU.add))
                        else:
                            ch.step(dve.tensor_scalar(den[:], total[:].rearrange("p s g t -> p g s t"), 2.0, None, ALU.mult))
                        ch.step(dve.reciprocal(den[:], den[:]))
                        for k in range(TOPK):
                            last = dve.tensor_tensor(wgt[:, :, :, k, :], dif[:, :, :, k, :], den[:], ALU.mult)
                        ch.step(last)

                    flat_w = all_w[:].rearrange("p e c -> p (e c)")

                    def weights0(q, j, at):
                        if from_step(q, 1):
                            dve.wait_ge(y_ready, QUAD * q + j - 3)
                        dve.tensor_copy(wx[j][:], flat_w[:, bass.ds(at, WCOLS)]).then_inc(w_ready, 1)

                    def result0(q, u, h, j):
                        if j == 0 and from_step(q, 2):
                            dve.wait_ge(results_stored[u], 16 * h)
                        dve.wait_ge(out_done, QUAD * q + j + 1)
                        dve.tensor_tensor(yq[u][:, j, :], pY[j % 2][:, 0:P], wx[j][:, B2_AT:WCOLS], ALU.add).then_inc(y_ready, 1)

                    def step0(q, u, h):
                        at = owners(QUAD * q + 1)
                        for j in range(QUAD):
                            if j == QUAD - 1:
                                result0(q, u, h, 0)
                                weights0(q + 1, 0, at[j])
                            else:
                                if from_step(q, 1):
                                    result0(q - 1, 1 - u, h - 1 + u, j + 1)
                                weights0(q, j + 1, at[j])

                    def weights_in(q, u):
                        at = owners(QUAD * q)
                        if from_step(q, 2):
                            dve.wait_ge(h_done, q - 1)
                        for j in range(QUAD):
                            last = dve.tensor_copy(wgu[u][:, j, :], flat_w[:, bass.ds(at[j], P)])
                        last.then_inc(w_ready, 1)
                        return at

                    def weights_out(q, u, at):
                        if from_step(q, 2):
                            dve.wait_ge(y_done, q - 1)
                        for j in range(QUAD):
                            dve.tensor_copy(wd[u][:, j, :], flat_w[0:64, bass.ds(at[j] + P, P)])

                    def results1(q, u, h):
                        if from_step(q, 2):
                            dve.wait_ge(results_stored[u], 16 * h)
                        dve.wait_ge(y_done, q + 1)
                        dve.tensor_copy(yq[u][:].rearrange("p b d -> p (b d)"), pY[u][:]).then_inc(y_ready, 1)

                    def step1(q, u, h):
                        more = not isinstance(q, int) or q + 1 < NQ
                        if more:
                            at = weights_in(q + 1, 1 - u)
                        dve.wait_ge(g_ready, q + 1)
                        dve.tensor_tensor(hx[u][:], gs[u][:], pU[u][0:64, :], ALU.mult).then_inc(h_ready, 1)
                        if from_step(q, 1):
                            results1(q - 1, 1 - u, h - 1 + u)
                        if more:
                            weights_out(q + 1, 1 - u, at)

                    route()
                    if layer == 0:
                        so = Chain(dve, so_c)
                        dve.wait_ge(x_loaded_all, 16)

                        def shared(s, u, h):
                            so.start(s)
                            out = total_out[:, bass.ds(NT * s, NT), :]
                            dve.wait_ge(so_done, s + 1)
                            so.step(dve.tensor_tensor(out, out, pO[:].rearrange("p (t n) -> p t n", t=NT), ALU.add))
                            dve.tensor_tensor(out, out, sb2[:].unsqueeze(1).to_broadcast([P, NT, P]),
                                              ALU.add).then_inc(so_added, 1)

                        span(dve, 0, NS, shared)
                    dve.wait_ge(weights, 16 * len(expert_weights))
                    dve.wait_ge(routed, G)
                    if layer == 0:
                        weights0(0, 0, owners(-OWNER_AT)[OWNER_AT])
                        span(dve, 0, NQ - 1, step0)
                        last = (NQ - 1, (NQ - 1) % 2, (NQ - 1) // 2)
                        at = owners(QUAD * (NQ - 1) + 1)
                        for j in range(QUAD - 1):
                            result0(NQ - 2, (NQ - 2) % 2, (NQ - 2) // 2, j + 1)
                            weights0(NQ - 1, j + 1, at[j])
                        for j in range(QUAD):
                            result0(*last, j)
                    else:
                        weights_out(0, 0, weights_in(0, 0))
                        span(dve, 0, NQ - 1, step1)
                        step1(NQ - 1, (NQ - 1) % 2, (NQ - 1) // 2)
                        results1(NQ - 1, (NQ - 1) % 2, (NQ - 1) // 2)

                    add = Chain(dve, dve_sum_c)
                    flat_wgt = wgt[:].rearrange("p g s k t -> p (g s k t)")

                    def combine(s, u, h):
                        add.start((6 if G > 1 else 2) * s)
                        out = total_out[:, bass.ds(NT * s, NT), :]
                        if G > 1:
                            part = [t[:, bass.ds(NT * s, NT), :] for t in got_first]
                            for k in range(TOPK):
                                last = dve.tensor_tensor(part[k], part[k], flat_wgt[:, bass.ds(8 * s + NT * k, NT)]
                                                         .unsqueeze(2).to_broadcast([P, NT, P]), ALU.mult)
                                add.step(last)
                            for k in range(TOPK):
                                add.step(dve.tensor_tensor(out, out, part[k], ALU.add))
                        dve.wait_ge(gathered[u], 16 * 8 * h + 16 * 8)
                        add.step(dve.tensor_tensor(got[u][:].rearrange("p k t d -> p (k t) d"),
                                                   got[u][:].rearrange("p k t d -> p (k t) d"),
                                                   flat_wgt[:, bass.ds(8 * s + 8 * NS * (G - 1), 8)]
                                                   .unsqueeze(2).to_broadcast([P, 8, P]), ALU.mult))
                        add.step(dve.tensor_tensor(out, out, got[u][:, 0], ALU.add))
                        dve.tensor_tensor(out, out, got[u][:, 1], ALU.add).then_inc(added, 1)

                    if layer == 0:
                        dve.wait_ge(so_added, NS)
                    else:
                        dve.wait_ge(x_loaded_all, 16)
                        dve.wait_ge(first_gathered, 16 * TOPK * NS * NT)
                    span(dve, 0, NS, combine)

                @block.tensor
                def _(pe):
                    def turn(q, u, h):
                        if isinstance(q, int) and q >= NQ:
                            return
                        pe.wait_ge(xq_loaded[u], 16 * h + 16)
                        if from_step(q, 2):
                            pe.wait_ge(xqT_ready, q - 1)
                        for j in range(QUAD):
                            last = pe.transpose(pX[u][:, j * P:(j + 1) * P], xq[u][:, j, :], ident[:])
                        last.then_inc(xqT_done, 1)

                    def hidden0(q, u, j):
                        pe.wait_ge(w_ready, QUAD * q + j + 1)
                        if j == 0:
                            pe.wait_ge(xqT_ready, q + 1)
                        if from_step(q, 1):
                            pe.wait_ge(h_ready, QUAD * q + j - 3)
                        for c in range(4):
                            last = pe.matmul(pHx[j][:, c * P:(c + 1) * P], wx[j][:, c * P:(c + 1) * P],
                                             xqT[u][:, j * P:(j + 1) * P], start=True, stop=True)
                        last.then_inc(h_done, 1)

                    def out0(q, u, j):
                        pe.wait_ge(h_ready, QUAD * q + j + 1)
                        if from_step(q, 1) or j >= 2:
                            pe.wait_ge(y_ready, QUAD * q + j - 1)
                        for c in range(4):
                            last = pe.matmul(pY[j % 2][:, 0:P], hx[j][:, c, :],
                                             wx[j][:, W2_AT + c * P:W2_AT + (c + 1) * P], start=(c == 0), stop=(c == 3))
                        last.then_inc(out_done, 1)

                    def step0(q, u, h):
                        for j in range(QUAD):
                            hidden0(q, u, j)
                            if j == 1:
                                turn(q + 1, 1 - u, h + u)
                            if j >= 2:
                                out0(q, u, j - 2)
                            elif from_step(q, 1):
                                out0(q - 1, 1 - u, j + 2)

                    def hidden1(q, u):
                        pe.wait_ge(w_ready, q + 1)
                        pe.wait_ge(xqT_ready, q + 1)
                        if from_step(q, 2):
                            pe.wait_ge(h_ready, q - 1)
                        for j in range(QUAD):
                            cols = slice(j * P, (j + 1) * P)
                            pe.matmul(pG[u][0:64, cols], wgu[u][:, j, 0:64], xqT[u][:, cols], start=True, stop=True)
                            last = pe.matmul(pU[u][0:64, cols], wgu[u][:, j, 64:128], xqT[u][:, cols], start=True, stop=True)
                        last.then_inc(h_done, 1)

                    def out1(q, u):
                        pe.wait_ge(h_ready, q + 1)
                        if from_step(q, 2):
                            pe.wait_ge(y_ready, q - 1)
                        for j in range(QUAD):
                            cols = slice(j * P, (j + 1) * P)
                            last = pe.matmul(pY[u][:, cols], hx[u][:, cols], wd[u][:, j, :], start=True, stop=True)
                        last.then_inc(y_done, 1)

                    def step1(q, u, h):
                        turn(q + 1, 1 - u, h + u)
                        hidden1(q, u)
                        if from_step(q, 1):
                            out1(q - 1, 1 - u)

                    for g in range(G):
                        pe.wait_ge(both_ready, g + 1)
                        for n in range(NB):
                            pe.matmul(rank_b[n][:, 0:W], before[:], both[:, n * W:(n + 1) * W], start=True, stop=True)
                            last = pe.matmul(tot_b[n][:, 0:W], ones[:], both[:, n * W:(n + 1) * W], start=True, stop=True)
                        last.then_inc(ranks_done, 1)
                    if layer == 0:
                        def shared_hidden(s):
                            for c in range(4):
                                if from_step(s, 1):
                                    pe.wait_ge(sh_ready, 4 * s + c - 3)
                                pe.matmul(pHs[c][:], sw1[:, c * P:(c + 1) * P], xnT_all[:, bass.ds(SUP * s, SUP)],
                                          start=True, stop=True).then_inc(sh_done, 1)

                        def shared(s, u, h):
                            if not isinstance(s, int) or s + 1 < NS:
                                shared_hidden(s + 1)
                            pe.wait_ge(sh_ready, 4 * s + 4)
                            if from_step(s, 1):
                                pe.wait_ge(so_added, s)
                            for t in range(NT):
                                for c in range(4):
                                    last = pe.matmul(pO[:, t * P:(t + 1) * P], hs[u][c][:, t * P:(t + 1) * P], sw2[:, c, :],
                                                     start=(c == 0), stop=(c == 3))
                            last.then_inc(so_done, 1)

                        shared_hidden(0)
                        span(pe, 0, NS - 1, shared)
                        shared(NS - 1, (NS - 1) % 2, (NS - 1) // 2)
                        pe.wait_ge(so_added, NS)
                    pe.wait_ge(weights, 16 * len(expert_weights))
                    pe.wait_ge(routed, G)
                    turn(0, 0, 0)
                    quads = step0 if layer == 0 else step1
                    span(pe, 0, NQ - 1, quads)
                    quads(NQ - 1, (NQ - 1) % 2, (NQ - 1) // 2)
                    if layer == 0:
                        for j in (2, 3):
                            out0(NQ - 1, (NQ - 1) % 2, j)
                    else:
                        out1(NQ - 1, (NQ - 1) % 2)



def hopfield_mixer(nc, T, x_in, x_out):
    NB = TOK // SEQ
    NT = SEQ // P
    NH, HD, NP, NG = 16, 8, 8, 4
    RING = 3
    with Scope(nc, "c") as S:
        sb, ps, sem = S.sb, S.ps, S.sem
        wqkv, wo = sb("wqkv", [P, 3 * P]), sb("wo", [P, P])
        bqkv, bo = sb("bqkv", [P, 3 * P]), sb("bo", [P, P])
        lnw, lnb = sb("lnw", [P, P]), sb("lnb", [P, P])
        ident, ident_bf = sb("ident", [P, P]), sb("ident_bf", [P, P], BF16)
        mhalf = sb("mhalf", [P, 1])

        x = [sb(f"x{u}", [P, NT, P]) for u in range(RING)]
        xres = [sb(f"xres{u}", [P, NT, P]) for u in range(RING)]
        y = [sb(f"y{u}", [P, NT, P]) for u in range(RING)]
        r = [sb(f"r{u}", [P, NT, P]) for u in range(RING)]
        z = sb("z", [P, NT, P])
        st1, mv1, ve1, rs1 = sb("st1", [P, NT, 6]), sb("mv1", [P, NT, 2]), sb("ve1", [P, NT]), sb("rs1", [P, NT])
        st2, mv2, ve2, rs2 = sb("st2", [P, NT, 6]), sb("mv2", [P, NT, 2]), sb("ve2", [P, NT]), sb("rs2", [P, NT])
        zT = sb("zT", [P, SEQ])
        qk = sb("qk", [P, 2, NT, NH, HD])
        sq, ss = sb("sq", [P, 2, NT, NH, HD]), sb("ss", [P, NT * 2 * NH])
        rn = sb("rn", [P, NT * 2 * NH])
        q6, k6 = sb("q6", [P, NT, NH, 64], BF16), sb("k6", [P, NT, NH, 64], BF16)
        qT = sb("qT", [P, NP, SEQ], BF16)
        kT = [sb(f"kT{u}", [P, NP, SEQ], BF16) for u in range(RING)]
        v1 = [sb(f"v1{u}", [P, NT, NH, 32]) for u in range(RING)]
        e = [sb(f"e{n}", [P, 2, NT, SEQ]) for n in range(4)]
        ot0, ot1 = sb("ot0", [P, NG, SEQ]), sb("ot1", [P, NG, SEQ])
        otb = [sb(f"otb{u}", [P, NG, SEQ], BF16) for u in range(RING)]
        rec, s0, mx = sb("rec", [P, NT, NH]), sb("s0", [P, NT, NH, HD]), sb("mx", [P, NT, NH])
        s6 = sb("s6", [P, NT, NH, 64], BF16)
        sT = sb("sT", [P, NP, SEQ], BF16)
        rec1, s1 = sb("rec1", [P, NT, NH]), sb("s1", [P, NT, NH, HD])
        s1T = sb("s1T", [P, SEQ])

        px = [ps(f"px{n}", [P, 2, NT * SEQ]) for n in range(2)]
        po = [ps(f"po{n}", [P, 512]) for n in range(2)]
        pm = [ps(f"pm{n}", [P, 512]) for n in range(2)]

        consts, memsets, memsets_pool = sem("consts"), sem("memsets"), sem("memsets_pool")
        x_loaded = [sem(f"x_loaded{u}") for u in range(RING)]
        stored = [sem(f"stored{u}") for u in range(RING)]
        ln_c, norm_c, mid_c, out_c = (sem(n) for n in ("ln_c", "norm_c", "mid_c", "out_c"))
        split_c, ssplit_c, zln_c, res_c = (sem(n) for n in ("split_c", "ssplit_c", "zln_c", "res_c"))
        ve1_ready, rs1_ready, r_ready = sem("ve1_ready"), sem("rs1_ready"), sem("r_ready")
        ve2_ready, z_ready, xres_ready = sem("ve2_ready"), sem("z_ready"), sem("xres_ready")
        zT_done, zT_ready, qkv_done, qkv_ready = sem("zT_done"), sem("zT_ready"), sem("qkv_done"), sem("qkv_ready")
        ss_ready, rn_ready = sem("ss_ready"), sem("rn_ready")
        qk_normed, q6_ready, k6_ready = sem("qk_normed"), sem("q6_ready"), sem("k6_ready")
        k6T_done, kT_ready, q6T_done, qT_ready = sem("k6T_done"), sem("kT_ready"), sem("q6T_done"), sem("qT_ready")
        sim_done, exp_done, pv_done, ot_copied = sem("sim_done"), sem("exp_done"), sem("pv_done"), sem("ot_copied")
        otT_done, s0_ready, otb_ready = sem("otT_done"), sem("s0_ready"), sem("otb_ready")
        mxs_done, mx_ready = sem("mxs_done"), sem("mx_ready")
        s6_ready, aug_ready, s6T_done, sT_ready = sem("s6_ready"), sem("aug_ready"), sem("s6T_done"), sem("sT_ready")
        ot1T_done, s1_ready, s1T_done, s1T_ready = sem("ot1T_done"), sem("s1_ready"), sem("s1T_done"), sem("s1T_ready")
        dve_passed, pool_passed = sem("dve_passed"), sem("pool_passed")
        wo_done, y_ready = sem("wo_done"), sem("y_ready")

        xv = x_in.rearrange("(b t p) d -> b p t d", t=NT, p=P)
        yv = x_out.rearrange("(b t p) d -> b p t d", t=NT, p=P)
        NCONST = 10

        class Pass:

            def __init__(self, i, k):
                self.i, self.k, self.b = i, k, 3 * i + k
                b = self.b if isinstance(i, int) else RING + 1
                self.first_step = 0 <= b < NB
                self.second_step = 1 <= b <= NB
                self.prepare = 0 <= b + 1 < NB
                self.ahead = b + 2 < NB
                self.between = 1 <= b <= NB
                self.finish = b >= 2
                self.n = b
                self.loop0 = 2 * self.b - 1 if b >= 1 else 0
                self.loop1 = 2 * self.b if b < NB else 2 * self.b - 1
                self.pend0 = None if b < 2 else (2 * self.b - 2, k - 2)
                self.pend1 = (self.loop0, k) if self.first_step else None

            def ring(self, d=0):
                return (self.k + d) % RING

            def turn(self, d=0):
                return self.i + (self.k + d) // RING

        def each_pass(eng, run):
            run(Pass(0, -2))
            run(Pass(0, -1))
            for k in range(RING + 1):
                run(Pass(0, k))
            with eng.Fori(0, (NB - 4) // RING - 1) as i:
                for k in range(RING):
                    run(Pass(i, RING + 1 + k))
            for k in range(RING + 1, RING + 5):
                run(Pass((NB - 4) // RING - 1, k))

        with nc.Block() as block:
            @block.sync
            def _(sp):
                for dst, src in ((ident, T["ident"]), (ident_bf, T["ident_bf"].bitcast(BF16)),
                                 (lnw, T["L1_attn_ln_w"].partition_broadcast(P)),
                                 (lnb, T["L1_attn_ln_b"].partition_broadcast(P)),
                                 (bo, T["L1_attn_bo"].partition_broadcast(P)), (wo, T["L1_attn_Wo"])):
                    sp.dma_start(dst[:], src).then_inc(consts, 16)
                for n, name in enumerate("qkv"):
                    sp.dma_start(wqkv[:, n * P:(n + 1) * P], T[f"L1_attn_W{name}"]).then_inc(consts, 16)
                sp.dma_start(bqkv[:], T["c_bqkv"].partition_broadcast(P)).then_inc(consts, 16)

                def load(p, d):
                    if p.n + d >= RING:
                        sp.wait_ge(xres_ready, p.b + d - RING + 1)
                    sp.dma_start(x[p.ring(d)][:], xv[p.b + d]).then_inc(x_loaded[p.ring(d)], 16)

                def run(p):
                    if p.n == -2:
                        load(p, 2)
                    if p.n + 3 < NB:
                        load(p, 3)
                    if p.finish:
                        sp.wait_ge(y_ready, p.b - 1)
                        sp.dma_start(yv[p.b - 2], y[p.ring(-2)][:]).then_inc(stored[p.ring(-2)], 16)

                each_pass(sp, run)
                sp.wait_ge(y_ready, NB)
                sp.dma_start(yv[NB - 1], y[(NB - 1) % RING][:]).then_inc(stored[(NB - 1) % RING], 16)
                for u in range(RING):
                    sp.wait_ge(stored[u], 16 * len(range(u, NB, RING)))

            @block.vector
            def _(dve):
                ln, norm, mid, fin, split, ssplit = (
                    Chain(dve, s, dve_passed) for s in (ln_c, norm_c, mid_c, out_c, split_c, ssplit_c))
                for t in (q6, k6, s6):
                    dve.memset(t[:].rearrange("p t h c -> p (t h c)").bitcast(U32), 0)
                for u in range(RING):
                    dve.memset(v1[u][:], 0.0)
                dve.memset(mhalf[:], -0.5).then_inc(memsets, 1)
                dve.wait_ge(memsets, 1)
                dve.memset(k6[:, :, :, 48:51], 1.0)
                for u in range(RING):
                    last = dve.memset(v1[u][:, :, :, HD:HD + 1], 1.0)
                last.then_inc(memsets, 1)
                dve.wait_ge(consts, 16 * NCONST)
                dve.wait_ge(memsets, 2)

                def first_statistics(p):
                    ln.start(4 * (p.b + 2))
                    xb = x[p.ring(2)]
                    dve.wait_ge(x_loaded[p.ring(2)], 16 * p.turn(2) + 16)
                    for t in range(NT):
                        last = dve.bn_stats(st1[:, t, :], xb[:, t, :])
                    ln.step(last, own_wait=True)
                    for t in range(NT):
                        last = dve.bn_aggr(mv1[:, t, :], st1[:, t, :])
                    ln.step(last)
                    dve.tensor_scalar(ve1[:], mv1[:, :, 1], LN_EPS, None, ALU.add).then_inc(ve1_ready, 1)

                def second_statistics(p):
                    ln.start(4 * (p.b + 2) + 2)
                    xb, rb = x[p.ring(2)], r[p.ring(2)]
                    dve.wait_ge(rs1_ready, p.b + 3)
                    if p.n >= 1:
                        dve.wait_ge(xres_ready, p.b)
                    for t in range(NT):
                        last = dve.tensor_scalar(rb[:, t, :], xb[:, t, :], mv1[:, t, 0:1], rs1[:, t:t + 1],
                                                 ALU.subtract, ALU.mult)
                    last.then_inc(r_ready, 1)
                    dve.wait_ge(r_ready, p.b + 3)
                    for t in range(NT):
                        last = dve.bn_stats(st2[:, t, :], rb[:, t, :])
                    ln.step(last, own_wait=True)
                    for t in range(NT):
                        last = dve.bn_aggr(mv2[:, t, :], st2[:, t, :])
                    ln.step(last)
                    dve.tensor_scalar(ve2[:], mv2[:, :, 1], LN_EPS, None, ALU.add).then_inc(ve2_ready, 1)

                def qkv_bias(p):
                    for t in range(NT):
                        dve.wait_ge(qkv_done, NT * (p.b + 1) + t + 1)
                        dve.tensor_tensor(qk[:, :, t].rearrange("p s h d -> p s (h d)"),
                                          pm[t][:, 0:2 * P].rearrange("p (s c) -> p s c", s=2),
                                          bqkv[:, 0:2 * P].rearrange("p (s c) -> p s c", s=2), ALU.add)
                        dve.tensor_tensor(v1[p.ring(1)][:, t, :, 0:HD],
                                          pm[t][:, 2 * P:3 * P].rearrange("p (h d) -> p h d", h=NH),
                                          bqkv[:, 2 * P:3 * P].rearrange("p (h d) -> p h d", h=NH),
                                          ALU.add).then_inc(qkv_ready, 1)

                def square_sums(p):
                    norm.start(2 * (p.b + 1))
                    dve.wait_ge(qkv_ready, NT * (p.b + 2))
                    norm.step(dve.tensor_tensor(sq[:], qk[:], qk[:], ALU.mult))
                    norm.step(dve.tensor_reduce(ss[:], sq[:].rearrange("p s t h d -> p (s t h) d"), AX.X, ALU.add))
                    dve.tensor_scalar(ss[:], ss[:], 1e-24, None, ALU.max).then_inc(ss_ready, 1)

                def normalise_queries_keys(p):
                    dve.wait_ge(rn_ready, p.b + 2)
                    qkf = qk[:].rearrange("p s t h d -> p (s t h) d")
                    dve.tensor_tensor(qkf, qkf, rn[:].unsqueeze(2).to_broadcast([P, NT * 2 * NH, HD]),
                                      ALU.mult).then_inc(qk_normed, 1)

                QUERY_PLACES = (slice(0, 3), slice(4, 6), slice(3, 4))
                KEY_PLACES = (slice(2, 5), slice(1, 6, 4), slice(0, 1))

                def place(chain, src, dst, places, ready):
                    rest = src.rearrange("p t h d -> p (t h) d")
                    to = dst[:].rearrange("p t h c -> p (t h) c")[:, :, 0:48].rearrange("p n (m d) -> p n m d", m=6)
                    for n, at in enumerate(places):
                        count = len(range(6)[at])
                        ins = dve.tensor_copy(to[:, :, at, :], rest.unsqueeze(2).to_broadcast([P, NT * NH, count, HD]))
                        if n < 2:
                            chain.step(ins)
                            chain.step(dve.tensor_tensor(rest, rest, to[:, :, at.start, :], ALU.subtract))
                    ins.then_inc(ready, 1)

                def place_keys(p):
                    split.start(8 * (p.b + 1))
                    dve.wait_ge(qk_normed, p.b + 2)
                    if p.n >= 0:
                        dve.wait_ge(k6T_done, NT * (p.b + 1))
                    place(split, qk[:, 1], k6, KEY_PLACES, k6_ready)

                def place_queries(p):
                    split.start(8 * (p.b + 1) + 4)
                    if p.n >= 0:
                        dve.wait_ge(q6T_done, NT * (p.b + 1))
                    place(split, qk[:, 0], q6, QUERY_PLACES, q6_ready)

                def place_state(p):
                    ssplit.start(4 * p.b)
                    dve.wait_ge(s0_ready, NT * (p.b + 1))
                    if p.n >= 1:
                        dve.wait_ge(s6T_done, NT * p.b)
                    place(ssplit, s0[:], s6, QUERY_PLACES, s6_ready)

                def normalise(chain, t, recip, s):
                    v = pm[t][:].rearrange("p (g j2 j1 c) -> p g j1 j2 c", g=NG, j2=2, j1=2)
                    rv = recip[:, t, :].rearrange("p (g j1 j2) -> p g j1 j2", g=NG, j1=2)
                    chain.step(dve.reciprocal(rv, v[:, :, :, :, HD]))
                    sv = s[:, t, :, :].rearrange("p (g j1 j2) d -> p g j1 j2 d", g=NG, j1=2)
                    for j1 in range(2):
                        last = dve.tensor_tensor(sv[:, :, j1], v[:, :, j1, :, 0:HD],
                                                 rv[:, :, j1, :].unsqueeze(3).to_broadcast([P, NG, 2, HD]), ALU.mult)
                    return last

                def state(p):
                    mid.start(7 * p.b)
                    for t in range(NT):
                        dve.wait_ge(otT_done, NT * p.b + t + 1)
                        normalise(mid, t, rec, s0).then_inc(s0_ready, 1)

                def maxima(p, d, units):
                    for n in units:
                        head = (n // 4) * 4 + 2 * (n % 4 % 2) + n % 4 // 2
                        dve.wait_ge(mxs_done, 16 * (p.b + d) + n + 1)
                        dve.tensor_reduce(mx[:, :, head], pm[n % 2][:].rearrange("p (t k) -> p t k", t=NT), AX.X,
                                          ALU.max).then_inc(mx_ready, 1)

                def shifts(p):
                    mid.start(7 * (p.b - 1) + 2)
                    dve.wait_ge(mx_ready, 16 * p.b)
                    mid.step(dve.scalar_tensor_tensor(mx[:], mx[:], -1.0, rec[:], ALU.mult, ALU.mult))
                    split3(dve, mid, mx[:], [s6[:, :, :, 48 + n] for n in range(3)], aug_ready)

                def s6T_copy(p):
                    for t in range(NT):
                        dve.wait_ge(s6T_done, NT * (p.b - 1) + t + 1)
                        dve.tensor_copy(sT[:, :, t * P:(t + 1) * P],
                                        px[0][:, t, :].bitcast(BF16).rearrange("p (h q) -> p h q", h=NP)).then_inc(sT_ready, 1)

                def final_state(p):
                    fin.start(2 * (p.b - 2))
                    for t in range(NT):
                        dve.wait_ge(ot1T_done, NT * (p.b - 2) + t + 1)
                        normalise(fin, t, rec1, s1).then_inc(s1_ready, 1)

                def output(p):
                    u = p.ring(-2)
                    dve.wait_ge(wo_done, p.b - 1)
                    dve.wait_ge(xres_ready, p.b - 1)
                    if p.n - 2 >= RING:
                        dve.wait_ge(stored[u], 16 * p.turn(-2))
                    dve.tensor_tensor(y[u][:], pm[1][:, 0:NT * P].rearrange("p (t n) -> p t n", t=NT), xres[u][:],
                                      ALU.add).then_inc(y_ready, 1)

                def kT_copy(p):
                    for t in range(NT):
                        dve.wait_ge(k6T_done, NT * (p.b + 1) + t + 1)
                        dve.tensor_copy(kT[p.ring(1)][:, :, t * P:(t + 1) * P],
                                        pm[t][:].bitcast(BF16).rearrange("p (h q) -> p h q", h=NP)).then_inc(kT_ready, 1)

                def run(p):
                    if p.prepare:
                        qkv_bias(p)
                        square_sums(p)
                    if p.between:
                        maxima(p, -1, range(8, 10))
                    if p.ahead:
                        first_statistics(p)
                    if p.between:
                        maxima(p, -1, range(10, 14))
                    if p.ahead:
                        second_statistics(p)
                    if p.between:
                        maxima(p, -1, range(14, 16))
                        shifts(p)
                    if p.finish:
                        final_state(p)
                    if p.between:
                        s6T_copy(p)
                    if p.prepare:
                        normalise_queries_keys(p)
                        place_keys(p)
                    if p.finish:
                        output(p)
                    if p.first_step:
                        state(p)
                        maxima(p, 0, range(2))
                    if p.prepare:
                        place_queries(p)
                    if p.first_step:
                        maxima(p, 0, range(2, 4))
                        place_state(p)
                        maxima(p, 0, range(4, 8))
                    if p.prepare:
                        kT_copy(p)

                each_pass(dve, run)
                p = Pass((NB + 1) // RING, (NB + 1) % RING)
                final_state(p)
                output(p)

            @block.scalar
            def _(act):
                def exp(loop, hp):
                    n = 8 * loop + hp
                    act.wait_ge(sim_done, n + 1)
                    if hp >= 4 or not isinstance(loop, int) or loop >= 1:
                        act.wait_ge(pv_done, 4 * loop + hp // 2 - 1)
                    act.activation(e[hp % 4][:].rearrange("p a t q -> p (a t q)"), px[hp % 2][:].rearrange("p a q -> p (a q)"),
                                   ACT.Exp).then_inc(exp_done, 1)

                def copy_ot(loop, g, step, slot=None):
                    act.wait_ge(pv_done, 4 * loop + g + 1)
                    if step == 0:
                        act.activation(otb[slot][:, g, :], po[g % 2][:, 0:SEQ], ACT.Copy).then_inc(otb_ready, 1)
                    act.activation((ot0, ot1)[step][:, g, :], po[g % 2][:, 0:SEQ], ACT.Copy).then_inc(ot_copied, 1)

                def half(loop, step, exists, pend, pend_step, side, slot):
                    for hp in range(NP):
                        if exists:
                            exp(loop, hp)
                        if hp == 0 and pend:
                            copy_ot(pend[0], 3, pend_step, slot)
                        if hp % 2 == 0 and hp and exists:
                            if hp == 2 and step == 0:
                                side("ot0")
                            copy_ot(loop, hp // 2 - 1, step, slot)
                        side(hp)

                def run(p):
                    def side0(at):
                        if at == "ot0" and p.n >= 1:
                            act.wait_ge(otT_done, NT * p.b)
                            if p.n >= RING:
                                act.wait_ge(mxs_done, 16 * (p.b - RING + 1))
                        if at == 0 and p.prepare:
                            act.wait_ge(zT_done, p.b + 2)
                            act.activation(zT[:], pm[0][:, 0:SEQ], ACT.Copy).then_inc(zT_ready, 1)
                        if at == 7 and p.finish:
                            act.wait_ge(s1T_done, p.b - 1)
                            act.activation(s1T[:], pm[0][:, 0:SEQ], ACT.Copy).then_inc(s1T_ready, 1)

                    def side1(at):
                        if at == 7 and p.prepare:
                            for t in range(NT):
                                act.wait_ge(q6T_done, NT * (p.b + 1) + t + 1)
                                act.activation(qT[:, :, t * P:(t + 1) * P],
                                               px[0][:, t, :].bitcast(BF16).rearrange("p (h q) -> p h q", h=NP),
                                               ACT.Copy).then_inc(qT_ready, 1)

                    if p.n >= -1:
                        half(p.loop0, 0, p.first_step, p.pend0, 1, side0, p.ring())
                        half(p.loop1, 1, p.second_step, p.pend1, 0, side1, p.ring())

                each_pass(act, run)
                copy_ot(2 * NB - 1, 3, 1)
                act.wait_ge(s1T_done, NB)
                act.activation(s1T[:], pm[0][:, 0:SEQ], ACT.Copy).then_inc(s1T_ready, 1)

            @block.tensor
            def _(pe):
                pe.wait_ge(consts, 16 * NCONST)
                pe.wait_ge(memsets, 2)

                def sims(loop, hp, qside, kside):
                    n = 8 * loop + hp
                    if hp >= 2 or not isinstance(loop, int) or loop >= 1:
                        pe.wait_ge(exp_done, n - 1)
                    for a in range(2):
                        rows = slice(64 * a, 64 * a + 64)
                        for t in range(NT):
                            last = pe.matmul(px[hp % 2][:, a, t * SEQ:(t + 1) * SEQ], kside[rows, hp, t * P:(t + 1) * P],
                                             qside[rows, hp, :], start=True, stop=True)
                    last.then_inc(sim_done, 1)

                def values(loop, g, v):
                    pe.wait_ge(exp_done, 8 * loop + 2 * g + 2)
                    if g >= 2 or not isinstance(loop, int) or loop >= 1:
                        pe.wait_ge(ot_copied, 4 * loop + g - 1)
                    for t in range(NT):
                        for j in range(4):
                            hp, a = 2 * g + j % 2, j // 2
                            last = pe.matmul(po[g % 2][32 * j:32 * j + 32, 0:SEQ], v[:, t, 2 * hp + a, :],
                                             e[hp % 4][:, a, t, :], start=(t == 0), stop=(t == NT - 1))
                    last.then_inc(pv_done, 1)

                def half(loop, exists, qside, kside, v, pend, side):
                    for hp in range(NP):
                        if exists:
                            sims(loop, hp, qside, kside)
                        if hp == 0 and pend:
                            values(pend[0], 3, v1[pend[1] % RING])
                        if hp % 2 == 0 and hp and exists:
                            values(loop, hp // 2 - 1, v)
                        side(hp)

                def ot_transposes(src, done, t):
                    for g in range(NG):
                        last = pe.transpose(pm[t][:, g * P:(g + 1) * P], src[:, g, t * P:(t + 1) * P], ident[:])
                    last.then_inc(done, 1)

                def transposes6(src, done, t, bank=None):
                    bank = pm[t][:] if bank is None else bank
                    for hp in range(NP):
                        last = pe.transpose(bank.bitcast(BF16)[:, hp * P:(hp + 1) * P],
                                            src[:, t, 2 * hp:2 * hp + 2, :].rearrange("p h c -> p (h c)"), ident_bf[:])
                    last.then_inc(done, 1)

                def maxima(p, d, units):
                    for n in units:
                        g, j = n // 4, n % 4
                        rows = slice(32 * j, 32 * j + HD)
                        if n >= 2:
                            pe.wait_ge(mx_ready, 16 * (p.b + d) + n - 1)
                        for t in range(NT):
                            last = pe.matmul(pm[n % 2][:, t * SEQ:(t + 1) * SEQ], otb[p.ring(d)][rows, g, t * P:(t + 1) * P],
                                             kT[p.ring(d)][rows, 2 * g + j % 2, :], start=True, stop=True)
                        last.then_inc(mxs_done, 1)

                def finish_a(p):
                    pe.wait_ge(ot_copied, 4 * p.pend0[0] + 4)
                    if p.between:
                        pe.wait_ge(mx_ready, 16 * p.b)
                    for t in range(NT):
                        ot_transposes(ot1, ot1T_done, t)

                def state_transposes(p):
                    pe.wait_ge(aug_ready, p.b)
                    pe.wait_ge(s6_ready, p.b)
                    if p.first_step:
                        pe.wait_ge(exp_done, 8 * p.loop0 + NP - 1)
                    for t in range(NT):
                        transposes6(s6, s6T_done, t, px[0][:, t, :])

                def finish_b(p):
                    pe.wait_ge(s1_ready, NT * (p.b - 1))
                    for t in range(NT):
                        last = pe.transpose(pm[0][:, t * P:(t + 1) * P], s1[:, t, :, :].rearrange("p h d -> p (h d)"), ident[:])
                    last.then_inc(s1T_done, 1)

                def finish_c(p):
                    pe.wait_ge(s1T_ready, p.b - 1)
                    for t in range(NT):
                        last = pe.matmul(pm[1][:, t * P:(t + 1) * P], s1T[:, t * P:(t + 1) * P], wo[:], start=True, stop=True)
                    last.then_inc(wo_done, 1)

                def run(p):
                    def side0(at):
                        if p.prepare:
                            if at == 0:
                                pe.wait_ge(z_ready, p.b + 2)
                                for t in range(NT):
                                    last = pe.transpose(pm[0][:, t * P:(t + 1) * P], z[:, t, :], ident[:])
                                last.then_inc(zT_done, 1)
                            if at == 1:
                                pe.wait_ge(zT_ready, p.b + 2)
                                for t in range(NT):
                                    pe.matmul(pm[t][:, 0:3 * P], zT[:, t * P:(t + 1) * P], wqkv[:], start=True,
                                              stop=True).then_inc(qkv_done, 1)
                        if p.between:
                            if at == 2 and p.prepare:
                                pe.wait_ge(qkv_ready, NT * (p.b + 1) + 1)
                                maxima(p, -1, (8,))
                                pe.wait_ge(qkv_ready, NT * (p.b + 2))
                                maxima(p, -1, (9,))
                                return
                            if 2 <= at <= 5:
                                maxima(p, -1, range(4 + 2 * at, 6 + 2 * at))
                        if at == 6 and p.finish:
                            finish_a(p)
                        if at == 7:
                            if p.between:
                                state_transposes(p)
                            if p.finish:
                                finish_b(p)

                    def side1(at):
                        if at == 0 and p.finish:
                            finish_c(p)
                        if p.first_step:
                            if at == 2:
                                pe.wait_ge(ot_copied, 4 * p.loop0 + 4)
                                if p.finish:
                                    pe.wait_ge(y_ready, p.b - 1)
                                elif p.between:
                                    pe.wait_ge(mx_ready, 16 * p.b)
                                else:
                                    pe.wait_ge(qkv_ready, NT * (p.b + 2))
                                for t in range(NT):
                                    ot_transposes(ot0, otT_done, t)
                            if 3 <= at <= 6:
                                if at == 3:
                                    pe.wait_ge(s0_ready, NT * (p.b + 1))
                                    pe.wait_ge(otb_ready, NG * (p.b + 1))
                                maxima(p, 0, range(2 * at - 6, 2 * at - 4))
                        if at == 7 and p.prepare:
                            pe.wait_ge(q6_ready, p.b + 2)
                            pe.wait_ge(k6_ready, p.b + 2)
                            if p.first_step:
                                pe.wait_ge(exp_done, 8 * p.loop1 + NP - 1)
                                pe.wait_ge(mx_ready, 16 * p.b + 8)
                            for t in range(NT):
                                transposes6(q6, q6T_done, t, px[0][:, t, :])
                                transposes6(k6, k6T_done, t)
                            pe.wait_ge(qT_ready, NT * (p.b + 2))
                            pe.wait_ge(kT_ready, NT * (p.b + 2))

                    if p.n >= -1:
                        half(p.loop0, p.first_step, qT, kT[p.ring(0)], v1[p.ring(0)], p.pend0, side0)
                        if p.second_step:
                            pe.wait_ge(sT_ready, NT * p.b)
                        half(p.loop1, p.second_step, sT, kT[p.ring(-1)], v1[p.ring(-1)], p.pend1, side1)

                each_pass(pe, run)
                values(2 * NB - 1, 3, v1[(NB - 1) % RING])
                pe.wait_ge(ot_copied, 4 * 2 * NB)
                pe.wait_ge(y_ready, NB - 1)
                for t in range(NT):
                    ot_transposes(ot1, ot1T_done, t)
                finish_b(Pass((NB + 1) // RING, (NB + 1) % RING))
                finish_c(Pass((NB + 1) // RING, (NB + 1) % RING))

            @block.gpsimd
            def _(pool):
                zln, resc = (Chain(pool, s, pool_passed) for s in (zln_c, res_c))
                pool.wait_ge(consts, 16 * NCONST)
                pool.wait_ge(memsets, 2)

                def wide(t):
                    return t[:].unsqueeze(1).to_broadcast([P, NT, P])

                def norms(p):
                    pool.wait_ge(ss_ready, p.b + 2)
                    pool.tensor_tensor(rn[:], ss[:], mhalf[:].to_broadcast([P, NT * 2 * NH]), ALU.pow).then_inc(rn_ready, 1)

                def residual(p):
                    resc.start(p.b + 1)
                    u = p.ring(1)
                    pool.wait_ge(r_ready, p.b + 2)
                    if p.n + 1 >= RING:
                        pool.wait_ge(y_ready, p.b + 2 - RING)
                    resc.step(pool.tensor_tensor(xres[u][:], x[u][:], wide(bo), ALU.add))
                    pool.tensor_tensor(xres[u][:], xres[u][:], r[u][:], ALU.add).then_inc(xres_ready, 1)

                def first_roots(p):
                    pool.wait_ge(ve1_ready, p.b + 3)
                    pool.tensor_tensor(rs1[:], ve1[:], mhalf[:].to_broadcast([P, NT]), ALU.pow).then_inc(rs1_ready, 1)

                def second_ln(p):
                    zln.start(3 * (p.b + 2))
                    rb = r[p.ring(2)]
                    pool.wait_ge(ve2_ready, p.b + 3)
                    zln.step(pool.tensor_tensor(rs2[:], ve2[:], mhalf[:].to_broadcast([P, NT]), ALU.pow))
                    if p.n >= -1:
                        pool.wait_ge(zT_done, p.b + 2)
                    zln.own_wait()
                    for t in range(NT):
                        last = pool.tensor_scalar(z[:, t, :], rb[:, t, :], mv2[:, t, 0:1], rs2[:, t:t + 1], ALU.subtract, ALU.mult)
                    zln.step(last)
                    zln.step(pool.tensor_tensor(z[:], z[:], wide(lnw), ALU.mult))
                    pool.tensor_tensor(z[:], z[:], wide(lnb), ALU.add).then_inc(z_ready, 1)

                def run(p):
                    if p.ahead:
                        first_roots(p)
                    if p.prepare:
                        norms(p)
                    if p.ahead:
                        second_ln(p)
                    if p.prepare:
                        residual(p)

                each_pass(pool, run)



def program(nc, T, out):
    stages = [nc.dram_tensor(f"stage{n}", [TOK, P], F32, kind="Internal").ap() for n in range(3)]
    rows = [row_space(nc, layer) for layer in range(2)]
    recurrent_mixer(nc, T, T["L0_attn_x"].rearrange("b s d -> (b s) d"), stages[0], clear=rows[0] + rows[1])
    expert_mixture(nc, T, stages[0], stages[1], rows[0], 0)
    hopfield_mixer(nc, T, stages[1], stages[2])
    expert_mixture(nc, T, stages[2], out.rearrange("b s d -> (b s) d"), rows[1], 1)


def _tables():
    import numpy as np
    eye = np.eye(128, dtype=np.float32)
    headsel = np.zeros((128, 32), np.float32)
    headsel[:64, 0] = 1
    headsel[64:, 1] = 1
    sel3 = np.zeros((32, 4, 128), np.float32)
    for part in range(3):
        for c in range(4):
            for r in range(2):
                sel3[8 * part + 2 * c + r, c, 64 * r:64 * r + 64] = 1
    bits = lambda t: np.where(t != 0, 0x3F80, 0).astype(np.uint16)
    return {"ident": eye, "ident_bf": bits(eye), "headsel": headsel, "sel3": bits(sel3),
            "m_iota": np.arange(128, dtype=np.float32), "m_before": bits(np.triu(np.ones((128, 128)), 1))}


def _layout(inputs):
    import numpy as np
    arrays = {k: np.ascontiguousarray(v) for k, v in inputs.items()}
    by_channel = lambda v: np.asarray(v).reshape(4, 128).T
    arrays["a_cols"] = np.ascontiguousarray(np.stack(
        [by_channel(arrays[f"L0_attn_{n}"]) for n in ("bq", "bk", "bv", "alpha", "aug_param")], axis=1))
    arrays["c_bqkv"] = np.concatenate([arrays[f"L1_attn_b{n}"] for n in "qkv"])
    arrays["m_gate"] = np.ascontiguousarray(arrays["L0_ffn_gate_w"].T)
    arrays["m_b1"] = np.ascontiguousarray(arrays["L0_ffn_b1"].reshape(8, 4, 128).transpose(2, 0, 1))
    arrays["m_w2"] = np.ascontiguousarray(
        arrays["L0_ffn_W2"].reshape(8, 4, 128, 128).transpose(2, 0, 1, 3).reshape(128, 8, 512))
    arrays["m_sb1"] = np.ascontiguousarray(by_channel(arrays["L0_ffn_sb1"]))
    arrays["m_router"] = np.concatenate([arrays[f"L1_ffn_router_w{g}"] for g in range(2)], axis=1)
    group = lambda name: np.concatenate([arrays[f"L1_ffn_{name}{g}"] for g in range(2)], axis=0)
    down = np.zeros((64, 128, 128), np.float32)
    down[:, :64] = group("wd")
    arrays["m_w"] = np.ascontiguousarray(np.concatenate([group("wg"), group("wu"), down], axis=2).transpose(1, 0, 2))
    arrays.update(_tables())
    return arrays


def kernel(**inputs):
    import concourse.bacc as bacc
    from concourse.bass_utils import run_bass_kernel_spmd

    nc = bacc.Bacc("TRN2", target_bir_lowering=False, num_devices=1)
    arrays, T = {}, {}
    for name, a in _layout(inputs).items():
        arrays[f"in_{name}"] = a
        T[name] = nc.dram_tensor(f"in_{name}", a.shape, mybir.dt.from_np(a.dtype), kind="ExternalInput").ap()
    out = nc.dram_tensor("out", [16, SEQ, P], F32, kind="ExternalOutput").ap()
    program(nc, T, out)
    return run_bass_kernel_spmd(nc, [arrays], core_ids=[0]).results[0]["out"]
```
